# Optimizing a Trainium2 kernel written in Bass

```python
import numpy as np
import jax
import jax.numpy as jnp

def _softmax(x, axis=-1):
    return jax.nn.softmax(x, axis=axis)

def _gelu(x):
    return jax.nn.gelu(x, approximate=True)

def _silu(x):
    return jax.nn.silu(x)

def _sigmoid(x):
    return jax.nn.sigmoid(x)

def _layernorm(x, axis=-1, eps=1e-05):
    m = jnp.mean(x, axis=axis, keepdims=True)
    v = jnp.var(x, axis=axis, keepdims=True)
    return (x - m) / jnp.sqrt(v + eps)

def _scatter_add(tgt, idx, src, axis=0):
    return tgt.at[idx].add(src)

def _segment_sum(src, seg, n):
    return jax.ops.segment_sum(src, seg, n)
kernel_name = 'mk_decoder_postln_d2_seqx_r4_25b943'

def setup_inputs(seed: int=0):
    np.random.seed(seed)
    _w = jnp.asarray

    def _rec_inputs():
        import jax
        import jax.numpy as jnp
        _rk = jax.random.key(seed)
        x = -0.0002928 + 1 * jax.random.normal(jax.random.fold_in(_rk, 1), (16, 112, 256), jnp.float32)
        _lenS = 112 - jax.random.randint(jax.random.fold_in(_rk, 7), (16,), 0, max(1, 112 // 4) + 1, jnp.int32)
        _lenS2 = 375 - jax.random.randint(jax.random.fold_in(_rk, 8), (16,), 0, max(1, 375 // 4) + 1, jnp.int32)
        _ctx_1024P = jax.random.normal(jax.random.fold_in(_rk, 11), (16, 16, 256), jnp.float32)
        _ctx_1024c = jax.random.dirichlet(jax.random.fold_in(_rk, 511), 0.3 * jnp.ones((16,), jnp.float32), (16, 375))
        _ctx_1024t = jnp.einsum('bsk,bkd->bsd', _ctx_1024c, _ctx_1024P)
        _ctx_1024t = _ctx_1024t * jax.lax.rsqrt(jnp.mean(jnp.square(_ctx_1024t)) + 1e-12) * 0.953939
        ctx_1024 = -1.39393e-06 + 0.999914 * (_ctx_1024t + 0.3 * jax.random.normal(jax.random.fold_in(_rk, 611), (16, 375, 256), jnp.float32))
        _validS = jnp.arange(112)[None, :] < _lenS[:, None]
        _validS2 = jnp.arange(375)[None, :] < _lenS2[:, None]
        _causal = jnp.tril(jnp.ones((112, 112), dtype=bool))
        mask_BxS2_bk0 = jnp.logical_not(jnp.broadcast_to(_validS2[:, :], (16, 375)))
        return (x, ctx_1024, mask_BxS2_bk0)
    x, ctx_1024, mask_BxS2_bk0 = _rec_inputs()

    def _L0_attn_setup():
        import jax, jax.numpy as jnp
        import numpy as np
        D_MODEL = 256
        N_HEADS = 16
        D_HEAD = D_MODEL // N_HEADS
        ROPE_BASE = 10000.0

        def _rope_cos_sin(seq_len, dtype):
            inv_freq = 1.0 / ROPE_BASE ** (jnp.arange(0, D_HEAD, 2, dtype=jnp.float32) / D_HEAD)
            t = jnp.arange(seq_len, dtype=jnp.float32)
            freqs = jnp.einsum('t,d->td', t, inv_freq)
            freqs = jnp.concatenate([freqs, freqs], axis=-1)
            return (jnp.cos(freqs).astype(dtype), jnp.sin(freqs).astype(dtype))

        def _rotate_half(x):
            x1, x2 = jnp.split(x, 2, axis=-1)
            return jnp.concatenate([-x2, x1], axis=-1)
        key = jax.random.key(seed)
        k1, k2, k3, k4, k5 = jax.random.split(key, 5)
        std = 0.02 / np.sqrt(2 * 12)
        x = jax.random.normal(k1, (2, 512, D_MODEL), dtype=jnp.float32)
        qkv_w = jax.random.normal(k2, (3 * D_MODEL, D_MODEL), dtype=jnp.float32) * std
        qkv_b = jnp.zeros((3 * D_MODEL,), dtype=jnp.float32)
        proj_w = jax.random.normal(k3, (D_MODEL, D_MODEL), dtype=jnp.float32) * std
        proj_b = jnp.zeros((D_MODEL,), dtype=jnp.float32)
        return {'x': x, 'qkv_w': qkv_w, 'qkv_b': qkv_b, 'proj_w': proj_w, 'proj_b': proj_b}
    _L0_attn_all = _L0_attn_setup()
    _L0_attn_in = {k: v for k, v in _L0_attn_all.items() if k in ('qkv_w', 'qkv_b', 'proj_w', 'proj_b')}
    del _L0_attn_all

    def _L0_xattn_setup():
        import jax, jax.numpy as jnp
        import numpy as np
        EMBED_DIM = 256
        NUM_HEADS = 16
        HEAD_DIM = EMBED_DIM // NUM_HEADS
        key = jax.random.key(seed)
        ks = jax.random.split(key, 12)
        B, S, E = (2, 512, EMBED_DIM)
        scale = 1.0 / np.sqrt(E)
        inp = {'query': jax.random.normal(ks[0], (B, S, E), dtype=jnp.float32), 'key': jax.random.normal(ks[1], (B, S, E), dtype=jnp.float32), 'value': jax.random.normal(ks[2], (B, S, E), dtype=jnp.float32), 'key_padding_mask': jax.random.randint(ks[3], (B, S), 0, 2).astype(bool), 'Wq': jax.random.normal(ks[4], (E, E), dtype=jnp.float32) * scale, 'bq': jnp.zeros((E,), dtype=jnp.float32), 'Wk': jax.random.normal(ks[5], (E, E), dtype=jnp.float32) * scale, 'bk': jnp.zeros((E,), dtype=jnp.float32), 'Wv': jax.random.normal(ks[6], (E, E), dtype=jnp.float32) * scale, 'bv': jnp.zeros((E,), dtype=jnp.float32), 'Wo': jax.random.normal(ks[7], (E, E), dtype=jnp.float32) * scale, 'bo': jnp.zeros((E,), dtype=jnp.float32)}
        return inp
    _L0_xattn_all = _L0_xattn_setup()
    _L0_xattn_in = {k: v for k, v in _L0_xattn_all.items() if k in ('Wq', 'bq', 'Wk', 'bk', 'Wv', 'bv', 'Wo', 'bo')}
    del _L0_xattn_all

    def _L0_ffn_setup():
        import jax, jax.numpy as jnp
        import numpy as np
        B, L, M = (4, 512, 256)
        G, E = (8, 8)
        CAP_FACTOR = 2.0

        def _ffn_size(m, widening=8.0):
            f = int(widening * m) * 2 // 3
            return f + (8 - f) % 8
        H = _ffn_size(M)

        def _gating_top2(logits, C):
            Gd, Sd, Ed = logits.shape
            raw = jax.nn.softmax(logits, axis=-1)
            idx1 = jnp.argmax(raw, axis=-1)
            m1 = jax.nn.one_hot(idx1, Ed, dtype=logits.dtype)
            gate1 = jnp.sum(raw * m1, axis=-1)
            rest = raw * (1.0 - m1)
            idx2 = jnp.argmax(rest, axis=-1)
            m2 = jax.nn.one_hot(idx2, Ed, dtype=logits.dtype)
            gate2 = jnp.sum(rest * m2, axis=-1)
            p1 = jnp.cumsum(m1, axis=-2) - m1
            m1 = m1 * (p1 < C).astype(m1.dtype)
            p1 = jnp.sum(p1 * m1, axis=-1)
            m1_flat = jnp.sum(m1, axis=-1)
            m1_count = jnp.sum(m1, axis=-2)
            p2 = jnp.cumsum(m2, axis=-2) - m2 + m1_count[:, None, :]
            m2 = m2 * (p2 < C).astype(m2.dtype)
            p2 = jnp.sum(p2 * m2, axis=-1)
            m2_flat = jnp.sum(m2, axis=-1)
            gate1 = gate1 * m1_flat
            gate2 = gate2 * m2_flat
            c1 = (gate1[..., None] * jax.nn.one_hot(idx1, Ed, dtype=jnp.float32))[..., None] * jax.nn.one_hot(p1.astype(jnp.int32), C, dtype=jnp.float32)[:, :, None, :]
            c2 = (gate2[..., None] * jax.nn.one_hot(idx2, Ed, dtype=jnp.float32))[..., None] * jax.nn.one_hot(p2.astype(jnp.int32), C, dtype=jnp.float32)[:, :, None, :]
            combine = (c1 + c2).astype(logits.dtype)
            dispatch = (combine != 0).astype(logits.dtype)
            return (dispatch, combine)
        key = jax.random.key(seed)
        k0, k1, k2, k3, k4 = jax.random.split(key, 5)
        return {'inputs': jax.random.normal(k0, (B, L, M), jnp.float32), 'router_w': jax.random.normal(k1, (M, E), jnp.float32) * 0.02, 'w0_kernel': jax.random.normal(k2, (E, M, H), jnp.float32) * 0.02, 'w1_kernel': jax.random.normal(k3, (E, M, H), jnp.float32) * 0.02, 'wo_kernel': jax.random.normal(k4, (E, H, M), jnp.float32) * 0.02}
    _L0_ffn_all = _L0_ffn_setup()
    _L0_ffn_in = {k: v for k, v in _L0_ffn_all.items() if k in ('router_w', 'w0_kernel', 'w1_kernel', 'wo_kernel')}
    del _L0_ffn_all

    def _L1_attn_setup():
        import jax, jax.numpy as jnp
        import numpy as np
        DIM = 256
        D_IN = 512
        N = 16
        DT_RANK = 64
        K = 4
        B_, L_ = (2, 256)
        key = jax.random.key(seed)
        ks = jax.random.split(key, 9)
        s = lambda k, sh, sc: jax.random.normal(k, sh, dtype=jnp.float32) * sc
        x = s(ks[0], (B_, L_, DIM), 1.0)
        W_in = s(ks[1], (2 * D_IN, DIM), 0.02)
        conv_w = s(ks[2], (D_IN, 1, K), 0.1)
        conv_b = s(ks[3], (D_IN,), 0.02)
        W_x = s(ks[4], (DT_RANK + 2 * N, D_IN), 0.02)
        W_dt = s(ks[5], (D_IN, DT_RANK), 0.02)
        b_dt = s(ks[6], (D_IN,), 0.02)
        A_log = jnp.log(jnp.broadcast_to(jnp.arange(1, N + 1, dtype=jnp.float32), (D_IN, N)))
        Dp = jnp.ones((D_IN,), jnp.float32)
        W_out = s(ks[7], (DIM, D_IN), 0.02)
        return dict(x=x, W_in=W_in, conv_w=conv_w, conv_b=conv_b, W_x=W_x, W_dt=W_dt, b_dt=b_dt, A_log=A_log, Dp=Dp, W_out=W_out)
    _L1_attn_all = _L1_attn_setup()
    _L1_attn_in = {k: v for k, v in _L1_attn_all.items() if k in ('W_in', 'conv_w', 'conv_b', 'W_x', 'W_dt', 'b_dt', 'A_log', 'Dp', 'W_out')}
    del _L1_attn_all

    def _L1_xattn_setup():
        import jax, jax.numpy as jnp
        import numpy as np
        D = 256
        NUM_ITERS = 3
        EPS = 1e-06
        SCALE = D ** (-0.5)

        def rmsnorm(x, w, eps=EPS):
            return x * jax.lax.rsqrt(jnp.mean(x * x, axis=-1, keepdims=True) + eps) * w

        def gru_cell(x, h, wih, whh, bih, bhh):
            gx = x @ wih.T + bih
            gh = h @ whh.T + bhh
            xr, xz, xn = jnp.split(gx, 3, axis=-1)
            hr, hz, hn = jnp.split(gh, 3, axis=-1)
            r = jax.nn.sigmoid(xr + hr)
            z = jax.nn.sigmoid(xz + hz)
            n = jnp.tanh(xn + r * hn)
            return (1.0 - z) * n + z * h
        key = jax.random.key(seed)
        ks = jax.random.split(key, 8)
        B, K, M, d = (8, 64, 1024, D)
        w_std = d ** (-0.5)
        return {'slots': jax.random.normal(ks[0], (B, K, d), jnp.float32), 'P': jax.random.normal(ks[1], (B, M, d), jnp.float32), 'Wq': jax.random.normal(ks[2], (d, d), jnp.float32) * w_std, 'Wk': jax.random.normal(ks[3], (d, d), jnp.float32) * w_std, 'Wv': jax.random.normal(ks[4], (d, d), jnp.float32) * w_std, 'gru_wih': jax.random.normal(ks[5], (3 * d, d), jnp.float32) * w_std, 'gru_whh': jax.random.normal(ks[6], (3 * d, d), jnp.float32) * w_std, 'gru_bih': jnp.zeros((3 * d,), jnp.float32), 'gru_bhh': jnp.zeros((3 * d,), jnp.float32), 'slot_norm_w': jnp.ones((d,), jnp.float32), 'input_norm_w': jnp.ones((d,), jnp.float32)}
    _L1_xattn_all = _L1_xattn_setup()
    _L1_xattn_in = {k: v for k, v in _L1_xattn_all.items() if k in ('Wq', 'Wk', 'Wv', 'gru_wih', 'gru_whh', 'gru_bih', 'gru_bhh', 'slot_norm_w', 'input_norm_w')}
    del _L1_xattn_all

    def _L1_ffn_setup():
        import jax, jax.numpy as jnp
        import numpy as np
        HIDDEN = 256
        NUM_EXPERTS = 8
        TOP_K = 2
        B, S = (2, 512)
        key = jax.random.key(seed)
        k1, k2, k3, k4, k5 = jax.random.split(key, 5)
        d, dff, E = (HIDDEN, 4 * HIDDEN, NUM_EXPERTS)
        x = jax.random.normal(k1, (B, S, d), dtype=jnp.float32)
        W1 = jax.random.normal(k2, (E, d, dff), dtype=jnp.float32) * (1.0 / np.sqrt(d))
        b1 = jax.random.normal(k3, (E, dff), dtype=jnp.float32) * 0.01
        W2 = jax.random.normal(k4, (E, dff, d), dtype=jnp.float32) * (1.0 / np.sqrt(dff))
        b2 = jax.random.normal(k5, (E, d), dtype=jnp.float32) * 0.01
        return {'x': x, 'W1': W1, 'b1': b1, 'W2': W2, 'b2': b2}
    _L1_ffn_all = _L1_ffn_setup()
    _L1_ffn_in = {k: v for k, v in _L1_ffn_all.items() if k in ('W1', 'b1', 'W2', 'b2')}
    del _L1_ffn_all
    return {'x': x, 'ctx_1024': ctx_1024, 'mask_BxS2_bk0': mask_BxS2_bk0, 'L0_attn_qkv_w': _L0_attn_in['qkv_w'], 'L0_attn_qkv_b': _L0_attn_in['qkv_b'], 'L0_attn_proj_w': _L0_attn_in['proj_w'], 'L0_attn_proj_b': _L0_attn_in['proj_b'], 'L0_xattn_Wq': _L0_xattn_in['Wq'], 'L0_xattn_bq': _L0_xattn_in['bq'], 'L0_xattn_Wk': _L0_xattn_in['Wk'], 'L0_xattn_bk': _L0_xattn_in['bk'], 'L0_xattn_Wv': _L0_xattn_in['Wv'], 'L0_xattn_bv': _L0_xattn_in['bv'], 'L0_xattn_Wo': _L0_xattn_in['Wo'], 'L0_xattn_bo': _L0_xattn_in['bo'], 'L0_ffn_router_w': _L0_ffn_in['router_w'], 'L0_ffn_w0_kernel': _L0_ffn_in['w0_kernel'], 'L0_ffn_w1_kernel': _L0_ffn_in['w1_kernel'], 'L0_ffn_wo_kernel': _L0_ffn_in['wo_kernel'], 'L1_attn_W_in': _L1_attn_in['W_in'], 'L1_attn_conv_w': _L1_attn_in['conv_w'], 'L1_attn_conv_b': _L1_attn_in['conv_b'], 'L1_attn_W_x': _L1_attn_in['W_x'], 'L1_attn_W_dt': _L1_attn_in['W_dt'], 'L1_attn_b_dt': _L1_attn_in['b_dt'], 'L1_attn_A_log': _L1_attn_in['A_log'], 'L1_attn_Dp': _L1_attn_in['Dp'], 'L1_attn_W_out': _L1_attn_in['W_out'], 'L1_xattn_Wq': _L1_xattn_in['Wq'], 'L1_xattn_Wk': _L1_xattn_in['Wk'], 'L1_xattn_Wv': _L1_xattn_in['Wv'], 'L1_xattn_gru_wih': _L1_xattn_in['gru_wih'], 'L1_xattn_gru_whh': _L1_xattn_in['gru_whh'], 'L1_xattn_gru_bih': _L1_xattn_in['gru_bih'], 'L1_xattn_gru_bhh': _L1_xattn_in['gru_bhh'], 'L1_xattn_slot_norm_w': _L1_xattn_in['slot_norm_w'], 'L1_xattn_input_norm_w': _L1_xattn_in['input_norm_w'], 'L1_ffn_W1': _L1_ffn_in['W1'], 'L1_ffn_b1': _L1_ffn_in['b1'], 'L1_ffn_W2': _L1_ffn_in['W2'], 'L1_ffn_b2': _L1_ffn_in['b2']}

def reference(x, ctx_1024, mask_BxS2_bk0, L0_attn_qkv_w, L0_attn_qkv_b, L0_attn_proj_w, L0_attn_proj_b, L0_xattn_Wq, L0_xattn_bq, L0_xattn_Wk, L0_xattn_bk, L0_xattn_Wv, L0_xattn_bv, L0_xattn_Wo, L0_xattn_bo, L0_ffn_router_w, L0_ffn_w0_kernel, L0_ffn_w1_kernel, L0_ffn_wo_kernel, L1_attn_W_in, L1_attn_conv_w, L1_attn_conv_b, L1_attn_W_x, L1_attn_W_dt, L1_attn_b_dt, L1_attn_A_log, L1_attn_Dp, L1_attn_W_out, L1_xattn_Wq, L1_xattn_Wk, L1_xattn_Wv, L1_xattn_gru_wih, L1_xattn_gru_whh, L1_xattn_gru_bih, L1_xattn_gru_bhh, L1_xattn_slot_norm_w, L1_xattn_input_norm_w, L1_ffn_W1, L1_ffn_b1, L1_ffn_W2, L1_ffn_b2):
    import jax
    import jax.numpy as jnp

    def _L0_attn_ref(x, qkv_w, qkv_b, proj_w, proj_b):
        import jax, jax.numpy as jnp
        import numpy as np
        D_MODEL = 256
        N_HEADS = 16
        D_HEAD = D_MODEL // N_HEADS
        ROPE_BASE = 10000.0

        def _rope_cos_sin(seq_len, dtype):
            inv_freq = 1.0 / ROPE_BASE ** (jnp.arange(0, D_HEAD, 2, dtype=jnp.float32) / D_HEAD)
            t = jnp.arange(seq_len, dtype=jnp.float32)
            freqs = jnp.einsum('t,d->td', t, inv_freq)
            freqs = jnp.concatenate([freqs, freqs], axis=-1)
            return (jnp.cos(freqs).astype(dtype), jnp.sin(freqs).astype(dtype))

        def _rotate_half(x):
            x1, x2 = jnp.split(x, 2, axis=-1)
            return jnp.concatenate([-x2, x1], axis=-1)
        B, S, D = x.shape
        H, Dh = (N_HEADS, D_HEAD)
        scale = 1.0 / np.sqrt(Dh)
        qkv = x @ qkv_w.T + qkv_b
        qkv = qkv.reshape(B, S, 3, H, Dh)
        q = jnp.transpose(qkv[:, :, 0], (0, 2, 1, 3))
        k = jnp.transpose(qkv[:, :, 1], (0, 2, 1, 3))
        v = jnp.transpose(qkv[:, :, 2], (0, 2, 1, 3))
        cos, sin = _rope_cos_sin(S, x.dtype)
        q = q * cos + _rotate_half(q) * sin
        k = k * cos + _rotate_half(k) * sin
        scores = jnp.einsum('bhsd,bhtd->bhst', q, k) * scale
        causal = jnp.triu(jnp.ones((S, S), dtype=bool), k=1)
        neg = jnp.finfo(scores.dtype).min
        scores = jnp.where(causal[None, None], neg, scores)
        probs = jax.nn.softmax(scores, axis=-1)
        ctx = jnp.einsum('bhst,bhtd->bhsd', probs, v)
        out = jnp.transpose(ctx, (0, 2, 1, 3)).reshape(B, S, D)
        out = out @ proj_w.T + proj_b
        return out

    def _L0_xattn_ref(query, key, value, key_padding_mask, Wq, bq, Wk, bk, Wv, bv, Wo, bo):
        import jax, jax.numpy as jnp
        import numpy as np
        EMBED_DIM = 256
        NUM_HEADS = 16
        HEAD_DIM = EMBED_DIM // NUM_HEADS
        B, Sq, E = query.shape
        H, D = (NUM_HEADS, HEAD_DIM)

        def split_heads(x, W, b):
            y = x @ W.T + b
            return y.reshape(B, -1, H, D).transpose(0, 2, 1, 3)
        q = split_heads(query, Wq, bq)
        k = split_heads(key, Wk, bk)
        v = split_heads(value, Wv, bv)
        scores = jnp.einsum('bhqd,bhkd->bhqk', q, k) / jnp.sqrt(jnp.float32(D))
        scores = jnp.where(key_padding_mask[:, None, None, :], -jnp.inf, scores)
        probs = jax.nn.softmax(scores, axis=-1)
        attn = jnp.einsum('bhqk,bhkd->bhqd', probs, v)
        attn = attn.transpose(0, 2, 1, 3).reshape(B, Sq, E)
        return attn @ Wo.T + bo

    def _L0_ffn_ref(inputs, router_w, w0_kernel, w1_kernel, wo_kernel):
        import jax, jax.numpy as jnp
        import numpy as np
        B, L, M = (4, 512, 256)
        G, E = (8, 8)
        CAP_FACTOR = 2.0

        def _ffn_size(m, widening=8.0):
            f = int(widening * m) * 2 // 3
            return f + (8 - f) % 8
        H = _ffn_size(M)

        def _gating_top2(logits, C):
            Gd, Sd, Ed = logits.shape
            raw = jax.nn.softmax(logits, axis=-1)
            idx1 = jnp.argmax(raw, axis=-1)
            m1 = jax.nn.one_hot(idx1, Ed, dtype=logits.dtype)
            gate1 = jnp.sum(raw * m1, axis=-1)
            rest = raw * (1.0 - m1)
            idx2 = jnp.argmax(rest, axis=-1)
            m2 = jax.nn.one_hot(idx2, Ed, dtype=logits.dtype)
            gate2 = jnp.sum(rest * m2, axis=-1)
            p1 = jnp.cumsum(m1, axis=-2) - m1
            m1 = m1 * (p1 < C).astype(m1.dtype)
            p1 = jnp.sum(p1 * m1, axis=-1)
            m1_flat = jnp.sum(m1, axis=-1)
            m1_count = jnp.sum(m1, axis=-2)
            p2 = jnp.cumsum(m2, axis=-2) - m2 + m1_count[:, None, :]
            m2 = m2 * (p2 < C).astype(m2.dtype)
            p2 = jnp.sum(p2 * m2, axis=-1)
            m2_flat = jnp.sum(m2, axis=-1)
            gate1 = gate1 * m1_flat
            gate2 = gate2 * m2_flat
            c1 = (gate1[..., None] * jax.nn.one_hot(idx1, Ed, dtype=jnp.float32))[..., None] * jax.nn.one_hot(p1.astype(jnp.int32), C, dtype=jnp.float32)[:, :, None, :]
            c2 = (gate2[..., None] * jax.nn.one_hot(idx2, Ed, dtype=jnp.float32))[..., None] * jax.nn.one_hot(p2.astype(jnp.int32), C, dtype=jnp.float32)[:, :, None, :]
            combine = (c1 + c2).astype(logits.dtype)
            dispatch = (combine != 0).astype(logits.dtype)
            return (dispatch, combine)
        Bb, Ll, Mm = inputs.shape
        S = Bb * Ll // G
        x = inputs.reshape(G, S, Mm)
        logits = jnp.einsum('GSM,ME->GSE', x, router_w)
        cap = int(CAP_FACTOR * S / E)
        C = (cap + 3) // 4 * 4
        dispatch, combine = _gating_top2(logits, C)
        expert_inputs = jnp.einsum('GSEC,GSM->EGCM', dispatch, x)
        layer_w0 = jnp.einsum('EGCM,EMH->EGCH', expert_inputs, w0_kernel)
        layer_w1 = jnp.einsum('EGCM,EMH->EGCH', expert_inputs, w1_kernel)
        hidden = jax.nn.gelu(layer_w0, approximate=True) * layer_w1
        expert_outputs = jnp.einsum('EGCH,EHM->EGCM', hidden, wo_kernel)
        out = jnp.einsum('EGCM,GSEC->GSM', expert_outputs, combine)
        return out.reshape(Bb, Ll, Mm)

    def _L1_attn_ref(x, W_in, conv_w, conv_b, W_x, W_dt, b_dt, A_log, Dp, W_out):
        import jax, jax.numpy as jnp
        import numpy as np
        DIM = 256
        D_IN = 512
        N = 16
        DT_RANK = 64
        K = 4
        B_, L_ = (2, 256)
        b, l, d = x.shape
        xr = x @ W_in.T
        u, res = jnp.split(xr, 2, axis=-1)
        uc = jax.lax.conv_general_dilated(u.transpose(0, 2, 1), conv_w, window_strides=(1,), padding=[(K - 1, 0)], feature_group_count=D_IN, dimension_numbers=('NCH', 'OIH', 'NCH')) + conv_b[None, :, None]
        u = jax.nn.silu(uc.transpose(0, 2, 1))
        A = -jnp.exp(A_log)
        x_dbl = u @ W_x.T
        dlt, Bm, Cm = jnp.split(x_dbl, [DT_RANK, DT_RANK + N], axis=-1)
        delta = jax.nn.softplus(dlt @ W_dt.T + b_dt)
        deltaA = jnp.exp(delta[..., None] * A)
        deltaBu = (delta * u)[..., None] * Bm[:, :, None, :]

        def comb(e1, e2):
            a1, b1 = e1
            a2, b2 = e2
            return (a1 * a2, a2 * b1 + b2)
        hs = jax.lax.associative_scan(comb, (deltaA, deltaBu), axis=1)[1]
        y = jnp.einsum('bldn,bln->bld', hs, Cm) + u * Dp
        y = y * jax.nn.silu(res)
        return y @ W_out.T

    def _L1_xattn_ref(slots, P, Wq, Wk, Wv, gru_wih, gru_whh, gru_bih, gru_bhh, slot_norm_w, input_norm_w):
        import jax, jax.numpy as jnp
        import numpy as np
        D = 256
        NUM_ITERS = 3
        EPS = 1e-06
        SCALE = D ** (-0.5)

        def rmsnorm(x, w, eps=EPS):
            return x * jax.lax.rsqrt(jnp.mean(x * x, axis=-1, keepdims=True) + eps) * w

        def gru_cell(x, h, wih, whh, bih, bhh):
            gx = x @ wih.T + bih
            gh = h @ whh.T + bhh
            xr, xz, xn = jnp.split(gx, 3, axis=-1)
            hr, hz, hn = jnp.split(gh, 3, axis=-1)
            r = jax.nn.sigmoid(xr + hr)
            z = jax.nn.sigmoid(xz + hz)
            n = jnp.tanh(xn + r * hn)
            return (1.0 - z) * n + z * h
        Pn = rmsnorm(P, input_norm_w)
        k_proj = Pn @ Wk.T
        v_proj = Pn @ Wv.T
        for _ in range(NUM_ITERS):
            sn = rmsnorm(slots, slot_norm_w)
            q_proj = sn @ Wq.T
            scores = jnp.einsum('bkd,bmd->bkm', q_proj, k_proj) * SCALE
            attn = jax.nn.softmax(scores, axis=-2)
            attn = attn / (jnp.sum(attn, axis=-1, keepdims=True) + EPS)
            updates = jnp.einsum('bkm,bmd->bkd', attn, v_proj)
            slots = gru_cell(updates, slots, gru_wih, gru_whh, gru_bih, gru_bhh)
        return slots

    def _L1_ffn_ref(x, W1, b1, W2, b2):
        import jax, jax.numpy as jnp
        import numpy as np
        HIDDEN = 256
        NUM_EXPERTS = 8
        TOP_K = 2
        B, S = (2, 512)
        Bm, Sm, d = x.shape
        E = W1.shape[0]
        x_flat = x.reshape(-1, d)
        h = jnp.mod(x_flat[:, :TOP_K].sum(axis=1).astype(jnp.int32), E)
        sel = jnp.stack([h, jnp.mod(h + 1, E)], axis=1)

        def step(acc, params):
            e, W1e, b1e, W2e, b2e = params
            w = jnp.any(sel == e, axis=1).astype(x.dtype) / TOP_K
            y = jnp.maximum(x_flat @ W1e + b1e, 0.0) @ W2e + b2e
            return (acc + w[:, None] * y, None)
        init = jnp.zeros_like(x_flat)
        out_flat, _ = jax.lax.scan(step, init, (jnp.arange(E), W1, b1, W2, b2))
        return out_flat.reshape(Bm, Sm, d)
    x = _layernorm(x + _L0_attn_ref(x, L0_attn_qkv_w, L0_attn_qkv_b, L0_attn_proj_w, L0_attn_proj_b), axis=-1)
    x = _layernorm(x + _L0_xattn_ref(x, ctx_1024, ctx_1024, mask_BxS2_bk0, L0_xattn_Wq, L0_xattn_bq, L0_xattn_Wk, L0_xattn_bk, L0_xattn_Wv, L0_xattn_bv, L0_xattn_Wo, L0_xattn_bo), axis=-1)
    x = _layernorm(x + _L0_ffn_ref(x, L0_ffn_router_w, L0_ffn_w0_kernel, L0_ffn_w1_kernel, L0_ffn_wo_kernel), axis=-1)
    x = _layernorm(x + _L1_attn_ref(x, L1_attn_W_in, L1_attn_conv_w, L1_attn_conv_b, L1_attn_W_x, L1_attn_W_dt, L1_attn_b_dt, L1_attn_A_log, L1_attn_Dp, L1_attn_W_out), axis=-1)
    x = _layernorm(x + _L1_xattn_ref(x, ctx_1024, L1_xattn_Wq, L1_xattn_Wk, L1_xattn_Wv, L1_xattn_gru_wih, L1_xattn_gru_whh, L1_xattn_gru_bih, L1_xattn_gru_bhh, L1_xattn_slot_norm_w, L1_xattn_input_norm_w), axis=-1)
    x = _layernorm(x + _L1_ffn_ref(x, L1_ffn_W1, L1_ffn_b1, L1_ffn_W2, L1_ffn_b2), axis=-1)
    return x

_drawn_inputs = setup_inputs


def setup_inputs(seed=0):
    import zlib

    import numpy as np

    out = dict(_drawn_inputs(seed))
    spreads = {'L0_attn_qkv_b': (0.0, 0.1),
     'L0_attn_proj_b': (0.0, 0.1),
     'L0_xattn_bq': (0.0, 0.1),
     'L0_xattn_bk': (0.0, 0.8),
     'L0_xattn_bv': (0.0, 0.1),
     'L0_xattn_bo': (0.0, 0.1),
     'L1_attn_Dp': (1.0, 0.6),
     'L1_xattn_gru_bih': (0.0, 0.1),
     'L1_xattn_gru_bhh': (0.0, 0.1),
     'L1_xattn_slot_norm_w': (1.0, 0.2),
     'L1_xattn_input_norm_w': (1.0, 0.2)}
    factors = {'L0_attn_qkv_w': 5.691,
     'L1_attn_W_in': 2.691,
     'L1_attn_conv_w': 2.693,
     'L1_attn_conv_b': 4.286,
     'L1_attn_W_x': 8.0,
     'L1_attn_W_dt': 8.0,
     'L1_attn_b_dt': 8.0,
     'L1_attn_A_log': 8.0,
     'L1_attn_W_out': 3.381,
     'L1_ffn_b1': 8.0,
     'L1_ffn_b2': 8.0}
    for name, (base, spread) in spreads.items():
        noise = np.random.default_rng([zlib.crc32(name.encode()), seed]).standard_normal(out[name].shape)
        drawn = base * np.exp(spread * noise) if base else spread * noise
        out[name] = jnp.asarray(drawn.astype(out[name].dtype))
    for name, factor in factors.items():
        out[name] = (out[name] * factor).astype(out[name].dtype)
    return out
```

```python
import concourse.bass as bass
from concourse import mybir
from contextlib import ExitStack

F32 = mybir.dt.float32
BF16 = mybir.dt.bfloat16
U8 = mybir.dt.uint8
I32 = mybir.dt.int32
ALU = mybir.AluOpType
ACT = mybir.ActivationFunctionType
AX = mybir.AxisListType

B, T, D = 16, 112, 256
S2 = 375
KC = D // 128
HEADS, DH, PAD = 16, 16, 32
HG = HEADS * PAD // 128
KT, KP = 3, S2 // 3
G, GB = 8, 2
E = 8
CAP = 56
SL = E * CAP
ST = SL // T
HID = 1368
HT, HP = 12, HID // 12
NEG = -1.0e30
LN_EPS = 1e-5


class Steps:

    def __init__(self, sem, per, unit=1, early=False):
        self.sem, self.per, self.unit, self.start, self.seen = sem, per, unit, int(early), 0

    def at(self, i, k):
        assert k or self.start or isinstance(i, int), self.sem.name
        return i * (self.per * self.unit) + (k * self.unit + self.start)

    def chain(self, eng, i, instruction):
        self.seen += 1
        instruction.then_inc(self.sem, 1)
        eng.wait_ge(self.sem, self.at(i, self.seen))


def run_phase(nc, phase, d):
    used = []

    def own(name, early):
        used.append(nc.alloc_semaphore(name=name))
        if early:
            nc.sync.sem_inc(used[-1], 1)
        return used[-1]

    phase(nc, d, own)
    nc.clear_and_free_semaphores(used)
    nc.all_engine_barrier()


def inverse_root(dve, nc, links, i, value, root, tmp):
    V = nc.vector
    links.chain(dve, i, V.tensor_scalar(root.bitcast(I32), value.bitcast(I32), -0.5, float(0x5F3759DF), ALU.mult, ALU.add))
    k = 1.0
    for step in range(3):
        if value.shape[-1] == 1:
            links.chain(dve, i, V.scalar_tensor_tensor(tmp, root, value, root, ALU.mult, ALU.mult))
        else:
            links.chain(dve, i, V.tensor_tensor(tmp, root, root, ALU.mult))
            links.chain(dve, i, V.tensor_tensor(tmp, tmp, value, ALU.mult))
        if step < 2:
            links.chain(dve, i, V.scalar_tensor_tensor(root, tmp, 3 * k * k, root, ALU.subtract, ALU.mult))
            k = -2 * k ** 3
    links.chain(dve, i, V.tensor_scalar(tmp, tmp, -0.5 / k ** 3, 1.5 / k, ALU.mult, ALU.add))
    links.chain(dve, i, V.tensor_tensor(root, root, tmp, ALU.mult))


def layer_norms(dve, nc, links, i, rows, stats, outs, done):
    for n, t in enumerate(rows):
        last = nc.vector.bn_stats(stats[:, n, 0:6], t)
        if n < len(rows) - 1:
            last.then_inc(links.sem, 1)
    links.seen += len(rows) - 1
    links.chain(dve, i, last)
    nc.vector.memset(stats[:, 0, 9:10], 0.0)
    for n in range(len(rows)):
        last = nc.vector.bn_aggr(stats[:, n, 6:8], stats[:, n, 0:6])
        if n < len(rows) - 1:
            last.then_inc(links.sem, 1)
    links.seen += len(rows) - 1
    links.chain(dve, i, last)
    n = len(rows)
    links.chain(dve, i, nc.vector.tensor_scalar(stats[:, 0:n, 7], stats[:, 0:n, 7], LN_EPS, None, ALU.add))
    inverse_root(dve, nc, links, i, stats[:, 0:n, 7], stats[:, 0:n, 8], stats[:, 0:n, 9])
    for n, (t, out) in enumerate(zip(rows, outs)):
        nc.vector.tensor_scalar(out, t, stats[:, n, 6:7], stats[:, n, 8:9], ALU.subtract, ALU.mult).then_inc(done.sem, 1)


def attention_phase(nc, d, own):
    ctx = ExitStack()
    with ctx:
        def sb(name, shape, dt=F32):
            return ctx.enter_context(nc.sbuf_tensor("a_" + name, shape, dt))

        def sem(name, per, unit=1, early=False):
            return Steps(own("a_" + name, early), per, unit, early)

        wqkv = sb("wqkv", [128, KC, 3 * D])
        bqkv = sb("bqkv", [T, 3 * D])
        wproj = sb("wproj", [128, HG, D])
        bproj = sb("bproj", [T, D])
        wqx = sb("wqx", [128, KC, HG * 128])
        bqx = sb("bqx", [128, HG])
        wkx = sb("wkx", [128, KC, HG * 128])
        bkx = sb("bkx", [128, HG])
        wvx = sb("wvx", [128, KC, D])
        bvx = sb("bvx", [KP, D])
        wox = sb("wox", [128, HG, D])
        box = sb("box", [T, D])
        router = sb("router", [128, KC, E])
        cos = sb("cos", [T, DH])
        sin = sb("sin", [T, DH])
        ident = sb("ident", [128, 128])
        earlier = sb("earlier", [T, T])
        ones = sb("ones", [T, T])
        rev = sb("rev", [T, E])
        slot_no = sb("slot_no", [T, CAP])
        ident_f = sb("ident_f", [T, T])
        causal_f = sb("causal_f", [T, T])
        maskrow_f = sb("maskrow_f", [1, 128])
        identb = sb("identb", [T, T], BF16)
        causalb = sb("causalb", [T, 4, T], BF16)
        maskrowb = sb("maskrowb", [1, 128], BF16)

        xt = sb("xt", [128, GB, KC, T])
        x = sb("x", [T, GB, D])
        ctxt = sb("ctxt", [128, GB, KC, S2])
        mask8 = sb("mask8", [1, GB, S2], U8)
        maskb = sb("maskb", [1, GB, S2], BF16)

        qkb = sb("qkb", [T, 2 * D])
        rot1 = sb("rot1", [T, 2 * D])
        rot2 = sb("rot2", [T, 2 * D])
        qkp = sb("qkp", [T, 2 * HEADS, PAD])
        vp = sb("vp", [T, HEADS, PAD])
        qt = sb("qt", [128, HG, T])
        kt = sb("kt", [128, HG, T])
        rowmax = sb("rowmax", [T, HEADS])
        negmax = sb("negmax", [T, HEADS])
        rowsum = sb("rowsum", [T, HEADS])
        rowinv = sb("rowinv", [T, HEADS])
        inv_wide = sb("inv_wide", [T, HEADS, PAD])
        p = sb("p", [T, 2, 4, T])
        pt = sb("pt", [T, 2, 4, T])
        inv_t = sb("inv_t", [128, HG, T])
        ot = sb("ot", [128, HG, T])
        xb = sb("xb", [T, D])
        t = sb("t", [T, D])
        stats = sb("stats", [T, 1, 10])
        x1 = sb("x1", [T, D])
        x1t = sb("x1t", [128, KC, T])
        ktx = sb("ktx", [128, HG, S2])
        vx = sb("vx", [KP, KT, HEADS, PAD])
        px = sb("px", [T, 4, S2])
        ptx = sb("ptx", [KP, 2, KT, T])
        x2 = sb("x2", [T, GB, D])
        x2t = sb("x2t", [128, GB, KC, T])
        lg = sb("lg", [T, GB, E])
        raw = sb("raw", [T, GB, E])
        tmp = sb("tmp", [T, GB, E])
        cand = sb("cand", [T, GB, E])
        pick = sb("pick", [T, GB, 2, E])
        kept = sb("kept", [T, GB, 2, E])
        pos = sb("pos", [T, GB, 2, E])
        s1 = sb("s1", [T, 8, GB])
        gate = sb("gate", [T, GB, 2])
        place = sb("place", [T, GB, 2])
        onehot = sb("onehot", [T, GB, 2, CAP])
        comb = sb("comb", [T, GB, E, CAP])
        comb2 = sb("comb2", [T, GB, E, CAP])
        disp = sb("disp", [T, GB, SL])
        xe = sb("xe", [128, KC, SL])
        combt = sb("combt", [T, GB, ST, T])

        def ps(name, shape):
            return ctx.enter_context(nc.psum_tensor("a_" + name, shape, F32))

        score = [ps(f"score{n}", [128, 512]) for n in range(4)]
        trans = [ps(f"trans{n}", [128, 512]) for n in range(2)]
        outt = ps("outt", [128, 512])
        misc = ps("misc", [128, 512])

        weights = sem("weights", 1)
        ready = sem("ready", 1)
        in_x = [sem(f"in_x{j}", 2, 16) for j in range(GB)]
        in_ctx = [sem(f"in_ctx{j}", 2, 16) for j in range(GB)]
        x_done = sem("x_done", GB, early=True)
        mask_done = sem("mask_done", GB, early=True)
        qkv = sem("qkv", GB, early=True)
        roped = sem("roped", GB)
        qk_t = sem("qk_t", GB)
        qk_sb = sem("qk_sb", GB)
        s_done = sem("s_done", GB * HG)
        m_done = sem("m_done", GB * HG)
        p_done = sem("p_done", GB * HG)
        pt_done = sem("pt_done", GB * HG)
        pt_sb = sem("pt_sb", GB * HG)
        o_done = sem("o_done", GB * 2)
        inv_done = sem("inv_done", GB * 2)
        invt_done = sem("invt_done", GB * 2)
        invt_sb = sem("invt_sb", GB * 2)
        o_sb = sem("o_sb", GB * 2, early=True)
        proj = sem("proj", GB * 2)
        x1_done = sem("x1_done", GB)
        x1t_done = sem("x1t_done", GB)
        x1t_sb = sem("x1t_sb", GB)
        kx = sem("kx", GB * HG)
        kx_sb = sem("kx_sb", GB * HG)
        vxp = sem("vxp", GB * KT, early=True)
        vx_sb = sem("vx_sb", GB * KT, early=True)
        qx = sem("qx", GB)
        qx_sb = sem("qx_sb", GB)
        sx = sem("sx", GB * HEADS)
        mx = sem("mx", GB * HEADS // 2)
        pxd = sem("pxd", GB * HEADS, early=True)
        ptxd = sem("ptxd", GB * HEADS)
        ptx_sb = sem("ptx_sb", GB * HEADS)
        x2_done = sem("x2_done", GB)
        x2t_done = sem("x2t_done", 1)
        x2t_sb = sem("x2t_sb", 1)
        lg_done = sem("lg_done", 1)
        lg_sub = sem("lg_sub", 1)
        lg_exp = sem("lg_exp", 1)
        picked = sem("picked", 1)
        counted = sem("counted", 1)
        kept1 = sem("kept1", 1)
        total1 = sem("total1", 1)
        routed = sem("routed", 1)
        xe_done = sem("xe_done", 2)
        xe_sb = sem("xe_sb", 2)
        ct_done = sem("ct_done", GB)
        ct_sb = sem("ct_sb", GB)
        stored = sem("stored", 3, 16)
        saved = sem("saved", 1, early=True)
        vlink = sem("vlink", 111)
        block = ctx.enter_context(nc.Block())

        def column(h):
            return 4 * (h % 4) + h // 4

        loads = [
            (wqkv[:, :, :], d["wqkv"]), (bqkv[:, :], d["L0_attn_qkv_b"].partition_broadcast(T)),
            (wproj[:, :, :], d["wproj"]), (bproj[:, :], d["L0_attn_proj_b"].partition_broadcast(T)),
            (wqx[:, :, :], d["wqx"]), (bqx[:, :], d["bqx"]), (wkx[:, :, :], d["wkx"]), (bkx[:, :], d["bkx"]),
            (wvx[:, :, :], d["wvx"]), (bvx[:, :], d["L0_xattn_bv"].partition_broadcast(KP)),
            (wox[:, :, :], d["wox"]), (box[:, :], d["L0_xattn_bo"].partition_broadcast(T)),
            (router[:, :, :], d["router"]), (cos[:, :], d["cos"]), (sin[:, :], d["sin"]),
            (ident[:, :], d["ident"]), (earlier[:, :], d["earlier"]), (ones[:, :], d["ones"]),
            (rev[:, :], d["rev"]), (slot_no[:, :], d["slot_no"]), (ident_f[:, :], d["ident"][0:T, 0:T]),
            (causal_f[:, :], d["causal"]), (maskrow_f[:, :], d["maskrow"]),
        ]

        @block.sync
        def _(sp):
            for dst, src in loads:
                sp.dma_start(dst, src).then_inc(weights.sem, 16)
            with sp.Fori(0, G) as i:
                for j in range(GB):
                    sp.wait_ge(qkv.sem, qkv.at(i, 0))
                    sp.wait_ge(x_done.sem, x_done.at(i, 0))
                    sp.dma_start(xt[:, j, :, :], d["xt"][i * GB + j]).then_inc(in_x[j].sem, 16)
                    sp.dma_start(x[:, j, :], d["x"][i * GB + j]).then_inc(in_x[j].sem, 16)
                    sp.wait_ge(vxp.sem, vxp.at(i, 0))
                    sp.wait_ge(mask_done.sem, mask_done.at(i, 0))
                    sp.dma_start(ctxt[:, j, :, :], d["ctxt"][i * GB + j]).then_inc(in_ctx[j].sem, 16)
                    sp.dma_start(mask8[:, j, :], d["mask"][i * GB + j]).then_inc(in_ctx[j].sem, 16)

        @block.gpsimd
        def _(pool):
            with pool.Fori(0, G) as i:
                pool.wait_ge(x2_done.sem, x2_done.at(i, GB))
                pool.dma_start(d["s_x2"][i], x2[:, :, :]).then_inc(stored.sem, 16)
                pool.wait_ge(xe_sb.sem, xe_sb.at(i, 2))
                pool.dma_start(d["s_xe"][i], xe[:, :, :]).then_inc(stored.sem, 16)
                pool.wait_ge(ct_sb.sem, ct_sb.at(i, GB))
                pool.dma_start(d["s_ct"][i], combt[:, :, :, :]).then_inc(stored.sem, 16)
                pool.wait_ge(stored.sem, stored.at(i, 3))
                pool.sem_inc(saved.sem, 1)

        @block.tensor
        def _(pe):
            pe.wait_ge(weights.sem, 16 * len(loads))
            pe.wait_ge(ready.sem, 1)
            mm = nc.tensor.matmul
            with pe.Fori(0, G) as i:
                for j in range(GB):
                    pe.wait_ge(in_x[j].sem, in_x[j].at(i, 2))
                    pe.wait_ge(pxd.sem, pxd.at(i, j * HEADS))
                    for kc in range(KC):
                        mm(score[0][0:T, :], xt[:, j, kc, :], wqkv[:, kc, 0:2 * D], start=kc == 0, stop=kc == KC - 1)
                    for kc in range(KC):
                        last = mm(score[1][0:T, 0:D], xt[:, j, kc, :], wqkv[:, kc, 2 * D:3 * D], start=kc == 0, stop=kc == KC - 1)
                    last.then_inc(qkv.sem, 1)
                    pe.wait_ge(roped.sem, roped.at(i, j + 1))
                    for n in range(2):
                        for hg in range(HG):
                            last = nc.tensor.transpose(
                                score[2 + n][:, hg * T:(hg + 1) * T],
                                qkp[:, n * HEADS + 4 * hg:n * HEADS + 4 * hg + 4, :].rearrange("p h d -> p (h d)"), ident[0:T, 0:T])
                    last.then_inc(qk_t.sem, 1)

                    def scores(r):
                        if r == 0:
                            pe.wait_ge(qk_sb.sem, qk_sb.at(i, j + 1))
                        mm(score[r][0:T, 0:4 * T], identb[:, :], causalb[:, :, :].rearrange("p h k -> p (h k)"), start=True, stop=False)
                        q = 32 * r
                        for hg in range(HG):
                            last = mm(score[r][0:T, hg * T:(hg + 1) * T], qt[q:q + 32, hg, :], kt[q:q + 32, hg, :], start=False, stop=hg == HG - 1, tile_position=(q, 0))
                        last.then_inc(s_done.sem, 1)

                    def turn(r):
                        pe.wait_ge(p_done.sem, p_done.at(i, j * 4 + r + 1))
                        for hg in range(HG):
                            last = nc.tensor.transpose(trans[r % 2][0:T, hg * T:(hg + 1) * T], p[:, r % 2, hg, :], ident[0:T, 0:T])
                        last.then_inc(pt_done.sem, 1)

                    def values(r):
                        pe.wait_ge(pt_sb.sem, pt_sb.at(i, j * 4 + r + 1))
                        for hg in range(HG):
                            last = mm(outt[32 * r:32 * r + 32, hg * T:(hg + 1) * T], vp[:, 4 * hg + r, :], pt[:, r % 2, hg, :],
                                      start=True, stop=True, tile_position=(0, 32 * r))
                        if r == 3:
                            last.then_inc(o_done.sem, 1)

                    pe.wait_ge(o_sb.sem, o_sb.at(i, 2 * j))
                    scores(0)
                    scores(1)
                    for r in range(4):
                        turn(r)
                        if r + 2 < 4:
                            scores(r + 2)
                        values(r)

                    def finish(n, w):
                        pe.wait_ge(inv_done.sem, inv_done.at(i, 2 * j + n + 1))
                        for hg in range(HG):
                            last = nc.tensor.transpose(misc[:, hg * T:(hg + 1) * T],
                                                       inv_wide[:, 4 * hg:4 * hg + 4, :].rearrange("p h d -> p (h d)"), ident[0:T, 0:T])
                        last.then_inc(invt_done.sem, 1)
                        pe.wait_ge(o_sb.sem, o_sb.at(i, 2 * j + n + 1))
                        for hg in range(HG):
                            last = mm(misc[0:T, 0:D], ot[:, hg, :], w[:, hg, :], start=hg == 0, stop=hg == HG - 1)
                        last.then_inc(proj.sem, 1)

                    finish(0, wproj)

                    pe.wait_ge(in_ctx[j].sem, in_ctx[j].at(i, 2))
                    pe.wait_ge(mask_done.sem, mask_done.at(i, j + 1))
                    for hg in range(HG):
                        for kc in range(KC):
                            mm(score[hg][:, 0:S2], wkx[:, kc, hg * 128:(hg + 1) * 128], ctxt[:, j, kc, :], start=kc == 0, stop=False)
                        mm(score[hg][:, 0:S2], maskrowb[:, :], maskb[:, j, :], start=False, stop=True).then_inc(kx.sem, 1)
                    for k in range(KT):
                        pe.wait_ge(vx_sb.sem, vx_sb.at(i, max(j * KT + k - 1, 0)))
                        for kc in range(KC):
                            last = mm(trans[k % 2][0:KP, 0:D], ctxt[:, j, kc, k * KP:(k + 1) * KP], wvx[:, kc, :], start=kc == 0, stop=kc == KC - 1)
                        last.then_inc(vxp.sem, 1)

                    pe.wait_ge(x1_done.sem, x1_done.at(i, j + 1))
                    pe.wait_ge(vx_sb.sem, vx_sb.at(i, j * KT + KT))
                    for kc in range(KC):
                        last = nc.tensor.transpose(trans[0][:, kc * T:(kc + 1) * T], x1[:, kc * 128:(kc + 1) * 128], ident[0:T, 0:T])
                    last.then_inc(x1t_done.sem, 1)
                    pe.wait_ge(x1t_sb.sem, x1t_sb.at(i, j + 1))
                    for hg in range(HG):
                        for kc in range(KC):
                            last = mm(trans[1][:, hg * T:(hg + 1) * T], wqx[:, kc, hg * 128:(hg + 1) * 128], x1t[:, kc, :], start=kc == 0, stop=kc == KC - 1)
                    last.then_inc(qx.sem, 1)

                    def xscore(h):
                        if h == 0:
                            pe.wait_ge(qx_sb.sem, qx_sb.at(i, j + 1))
                            pe.wait_ge(kx_sb.sem, kx_sb.at(i, j * HG + HG))
                        if h >= 4:
                            pe.wait_ge(pxd.sem, pxd.at(i, j * HEADS + h - 3))
                        q = 32 * (h % 4)
                        mm(score[h % 4][0:T, 0:S2], qt[q:q + 32, h // 4, :], ktx[q:q + 32, h // 4, :], start=True, stop=True,
                           tile_position=(q, 0)).then_inc(sx.sem, 1)

                    def xturn(h):
                        pe.wait_ge(pxd.sem, pxd.at(i, j * HEADS + h + 1))
                        if h >= 2:
                            pe.wait_ge(ptx_sb.sem, ptx_sb.at(i, j * HEADS + h - 1))
                        for k in range(KT):
                            last = nc.tensor.transpose(trans[h % 2][0:KP, k * T:(k + 1) * T], px[:, h % 4, k * KP:(k + 1) * KP], ident[0:T, 0:T])
                        last.then_inc(ptxd.sem, 1)

                    def xvalues(h):
                        pe.wait_ge(ptx_sb.sem, ptx_sb.at(i, j * HEADS + h + 1))
                        for k in range(KT):
                            q = 32 * (h % 4)
                            last = mm(outt[q:q + 32, (h // 4) * T:(h // 4 + 1) * T], vx[:, k, h, :], ptx[:, h % 2, k, :],
                                      start=k == 0, stop=k == KT - 1, tile_position=(0, q))
                        if h == HEADS - 1:
                            last.then_inc(o_done.sem, 1)

                    for h in range(4):
                        xscore(h)
                    for h in range(0, HEADS, 2):
                        xturn(h)
                        xturn(h + 1)
                        if h + 4 < HEADS:
                            xscore(h + 4)
                            xscore(h + 5)
                        xvalues(h)
                        xvalues(h + 1)
                    finish(1, wox)

                pe.wait_ge(x2_done.sem, x2_done.at(i, GB))
                for j in range(GB):
                    for kc in range(KC):
                        last = nc.tensor.transpose(trans[0][:, (j * KC + kc) * T:(j * KC + kc + 1) * T], x2[:, j, kc * 128:(kc + 1) * 128], ident[0:T, 0:T])
                last.then_inc(x2t_done.sem, 1)
                pe.wait_ge(x2t_sb.sem, x2t_sb.at(i, 1))
                for j in range(GB):
                    for kc in range(KC):
                        last = mm(misc[0:T, j * E:(j + 1) * E], x2t[:, j, kc, :], router[:, kc, :], start=kc == 0, stop=kc == KC - 1)
                last.then_inc(lg_done.sem, 1)
                pe.wait_ge(picked.sem, picked.at(i, 1))
                mm(misc[0:T, 0:2 * E], earlier[:, :], pick[:, 0, :, :].rearrange("p c e -> p (c e)"), start=True, stop=True)
                mm(misc[0:T, 2 * E:4 * E], earlier[:, :], pick[:, 1, :, :].rearrange("p c e -> p (c e)"), start=True, stop=False)
                mm(misc[0:T, 2 * E:4 * E], ones[:, :], pick[:, 0, :, :].rearrange("p c e -> p (c e)"), start=False, stop=True).then_inc(counted.sem, 1)
                pe.wait_ge(kept1.sem, kept1.at(i, 1))
                for j in range(GB):
                    last = mm(misc[0:T, 4 * E:5 * E], ones[:, :], kept[:, j, 0, :], start=j == 0, stop=j == GB - 1)
                last.then_inc(total1.sem, 1)
                pe.wait_ge(routed.sem, routed.at(i, 1))
                for fc in range(KC):
                    for j in range(GB):
                        last = mm(score[fc][:, 0:SL], x2[:, j, fc * 128:(fc + 1) * 128], disp[:, j, :], start=j == 0, stop=j == GB - 1)
                    last.then_inc(xe_done.sem, 1)
                for j in range(GB):
                    for s in range(ST):
                        last = nc.tensor.transpose(score[2 + j][0:T, s * T:(s + 1) * T],
                                                   comb[:, j, 2 * s:2 * s + 2, :].rearrange("p e c -> p (e c)"), ident[0:T, 0:T])
                    last.then_inc(ct_done.sem, 1)
                pe.wait_ge(xe_sb.sem, xe_sb.at(i, 2))
                pe.wait_ge(ct_sb.sem, ct_sb.at(i, GB))

        @block.scalar
        def _(act):
            act.wait_ge(weights.sem, 16 * len(loads))
            fn = nc.scalar.activation
            with act.Fori(0, G) as i:
                for j in range(GB):
                    act.wait_ge(qk_t.sem, qk_t.at(i, j + 1))
                    fn(qt[:, :, :].rearrange("p h t -> p (h t)"), score[2][:, 0:HG * T], ACT.Copy)
                    fn(kt[:, :, :].rearrange("p h t -> p (h t)"), score[3][:, 0:HG * T], ACT.Copy).then_inc(qk_sb.sem, 1)
                    for r in range(4):
                        act.wait_ge(m_done.sem, m_done.at(i, j * 4 + r + 1))
                        for hg in range(HG):
                            c = column(4 * hg + r)
                            last = fn(p[:, r % 2, hg, :], score[r][0:T, hg * T:(hg + 1) * T], ACT.Exp, bias=negmax[:, c:c + 1],
                                      scale=0.25, accum_out=rowsum[:, c:c + 1])
                        last.then_inc(p_done.sem, 1)

                    def inverse_sums(n):
                        act.wait_ge(invt_done.sem, invt_done.at(i, 2 * j + n + 1))
                        fn(inv_t[:, :, :].rearrange("p h t -> p (h t)"), misc[:, 0:HG * T], ACT.Copy).then_inc(invt_sb.sem, 1)

                    inverse_sums(0)
                    for hg in range(HG):
                        act.wait_ge(kx.sem, kx.at(i, j * HG + hg + 1))
                        fn(ktx[:, hg, :], score[hg][:, 0:S2], ACT.Identity, bias=bkx[:, hg:hg + 1]).then_inc(kx_sb.sem, 1)
                    act.wait_ge(x1t_done.sem, x1t_done.at(i, j + 1))
                    fn(x1t[:, :, :].rearrange("p c t -> p (c t)"), trans[0][:, 0:KC * T], ACT.Copy).then_inc(x1t_sb.sem, 1)
                    act.wait_ge(qx.sem, qx.at(i, j + 1))
                    for hg in range(HG):
                        last = fn(qt[:, hg, :], trans[1][:, hg * T:(hg + 1) * T], ACT.Identity, bias=bqx[:, hg:hg + 1])
                    last.then_inc(qx_sb.sem, 1)
                    for h in range(HEADS):
                        if h % 2 == 0:
                            act.wait_ge(mx.sem, mx.at(i, (j * HEADS + h) // 2 + 1))
                        if h >= 4:
                            act.wait_ge(ptxd.sem, ptxd.at(i, j * HEADS + h - 3))
                        fn(px[:, h % 4, :], score[h % 4][0:T, 0:S2], ACT.Exp, bias=negmax[:, column(h):column(h) + 1], scale=0.25,
                           accum_out=rowsum[:, column(h):column(h) + 1]).then_inc(pxd.sem, 1)
                    inverse_sums(1)
                act.wait_ge(x2t_done.sem, x2t_done.at(i, 1))
                fn(x2t[:, :, :, :].rearrange("p j c t -> p (j c t)"), trans[0][:, 0:GB * KC * T], ACT.Copy).then_inc(x2t_sb.sem, 1)
                act.wait_ge(lg_sub.sem, lg_sub.at(i, 1))
                fn(raw[:, :, :], lg[:, :, :], ACT.Exp).then_inc(lg_exp.sem, 1)
                act.wait_ge(saved.sem, saved.at(i, 0))
                for fc in range(KC):
                    act.wait_ge(xe_done.sem, xe_done.at(i, fc + 1))
                    fn(xe[:, fc, :], score[fc][:, 0:SL], ACT.Copy).then_inc(xe_sb.sem, 1)
                for j in range(GB):
                    act.wait_ge(ct_done.sem, ct_done.at(i, j + 1))
                    fn(combt[:, j, :, :].rearrange("p s t -> p (s t)"), score[2 + j][0:T, 0:ST * T], ACT.Copy).then_inc(ct_sb.sem, 1)

        @block.vector
        def _(dve):
            V = nc.vector
            dve.wait_ge(weights.sem, 16 * len(loads))
            V.memset(qkp[:, :, :].rearrange("p h d -> p (h d)"), 0.0)
            V.memset(vp[:, :, :].rearrange("p h d -> p (h d)"), 0.0)
            V.memset(vx[:, :, :, :].rearrange("p k h d -> p (k h d)"), 0.0)
            V.tensor_copy(identb[:, :], ident_f[:, :])
            V.tensor_copy(maskrowb[:, :], maskrow_f[:, :])
            V.tensor_copy(causalb[:, :, :], causal_f[:, :].unsqueeze(1).broadcast_to([T, 4, T])).then_inc(ready.sem, 1)
            dve.wait_ge(ready.sem, 1)
            with dve.Fori(0, G) as i:
                link = lambda ins: vlink.chain(dve, i, ins)
                for j in range(GB):
                    dve.wait_ge(in_x[j].sem, in_x[j].at(i, 2))
                    V.tensor_tensor(xb[:, :], x[:, j, :], bproj[:, :], ALU.add).then_inc(x_done.sem, 1)
                    dve.wait_ge(in_ctx[j].sem, in_ctx[j].at(i, 2))
                    V.tensor_scalar(maskb[:, j, :], mask8[:, j, :], NEG, None, ALU.mult).then_inc(mask_done.sem, 1)
                    dve.wait_ge(qkv.sem, qkv.at(i, j + 1))
                    link(V.tensor_tensor(qkb[:, :], score[0][0:T, :], bqkv[:, 0:2 * D], ALU.add))
                    q3 = qkb[:, :].rearrange("p (h d) -> p h d", d=DH)
                    r2 = rot2[:, :].rearrange("p (h d) -> p h d", d=DH)
                    V.tensor_tensor(rot1[:, :].rearrange("p (h d) -> p h d", d=DH), q3, cos[:, :].unsqueeze(1).broadcast_to([T, 2 * HEADS, DH]), ALU.mult)
                    V.tensor_tensor(r2[:, :, 0:8], q3[:, :, 8:16], sin[:, 0:8].unsqueeze(1).broadcast_to([T, 2 * HEADS, 8]), ALU.mult)
                    link(V.tensor_tensor(r2[:, :, 8:16], q3[:, :, 0:8], sin[:, 8:16].unsqueeze(1).broadcast_to([T, 2 * HEADS, 8]), ALU.mult))
                    V.tensor_tensor(qkp[:, :, 0:DH], rot1[:, :].rearrange("p (h d) -> p h d", d=DH), r2, ALU.add)
                    V.tensor_tensor(vp[:, :, 0:DH], score[1][0:T, 0:D].rearrange("p (h d) -> p h d", d=DH),
                                    bqkv[:, 2 * D:3 * D].rearrange("p (h d) -> p h d", d=DH), ALU.add).then_inc(roped.sem, 1)

                    def maxima(hg):
                        dve.wait_ge(s_done.sem, s_done.at(i, j * 4 + hg + 1))
                        link(V.tensor_reduce(rowmax[:, 4 * hg:4 * hg + 4], score[hg][0:T, 0:4 * T].rearrange("p (h k) -> p h k", h=4), AX.X, ALU.max))
                        V.tensor_scalar(negmax[:, 4 * hg:4 * hg + 4], rowmax[:, 4 * hg:4 * hg + 4], -0.25, None, ALU.mult).then_inc(m_done.sem, 1)

                    maxima(0)
                    maxima(1)
                    for hg in range(HG):
                        dve.wait_ge(pt_done.sem, pt_done.at(i, j * HG + hg + 1))
                        V.tensor_copy(pt[:, hg % 2, :, :].rearrange("p h k -> p (h k)"), trans[hg % 2][0:T, 0:4 * T]).then_inc(pt_sb.sem, 1)
                        if hg + 2 < HG:
                            maxima(hg + 2)

                    def normalise(n, last_p, bias_x, out, done):
                        dve.wait_ge(last_p.sem, last_p.at(i, (j + 1) * (last_p.per // GB)))
                        link(V.reciprocal(rowinv[:, :], rowsum[:, :]))
                        V.tensor_copy(inv_wide[:, :, :].rearrange("p (g r) d -> p g r d", r=4), rowinv[:, :].rearrange("p (r g) -> p g r", r=4).unsqueeze(3).broadcast_to([T, HG, 4, PAD])).then_inc(inv_done.sem, 1)
                        dve.wait_ge(o_done.sem, o_done.at(i, 2 * j + n + 1))
                        dve.wait_ge(invt_sb.sem, invt_sb.at(i, 2 * j + n + 1))
                        V.tensor_tensor(ot[:, :, :].rearrange("p h t -> p (h t)"), outt[:, 0:HG * T],
                                        inv_t[:, :, :].rearrange("p h t -> p (h t)"), ALU.mult).then_inc(o_sb.sem, 1)
                        dve.wait_ge(proj.sem, proj.at(i, 2 * j + n + 1))
                        link(V.tensor_tensor(t[:, :], misc[0:T, 0:D], bias_x, ALU.add))
                        layer_norms(dve, nc, vlink, i, [t[:, :]], stats, [out], done)

                    normalise(0, p_done, xb[:, :], x1[:, :], x1_done)
                    dve.wait_ge(x1_done.sem, x1_done.at(i, j + 1))
                    V.tensor_tensor(xb[:, :], x1[:, :], box[:, :], ALU.add)
                    for k in range(KT):
                        dve.wait_ge(vxp.sem, vxp.at(i, j * KT + k + 1))
                        V.tensor_tensor(vx[:, k, :, 0:DH], trans[k % 2][0:KP, 0:D].rearrange("p (h d) -> p h d", d=DH),
                                        bvx[:, :].rearrange("p (h d) -> p h d", d=DH), ALU.add).then_inc(vx_sb.sem, 1)

                    def xmax(h):
                        dve.wait_ge(sx.sem, sx.at(i, j * HEADS + h + 2))
                        for n in range(2):
                            last = V.tensor_reduce(rowmax[:, column(h + n):column(h + n) + 1], score[(h + n) % 4][0:T, 0:S2], AX.X, ALU.max)
                        link(last)
                        V.tensor_scalar(negmax[:, column(h):column(h) + 5:4], rowmax[:, column(h):column(h) + 5:4], -0.25, None, ALU.mult).then_inc(mx.sem, 1)

                    xmax(0)
                    xmax(2)
                    for h in range(0, HEADS, 2):
                        for n in range(2):
                            dve.wait_ge(ptxd.sem, ptxd.at(i, j * HEADS + h + n + 1))
                            V.tensor_copy(ptx[:, n, :, :].rearrange("p k t -> p (k t)"), trans[n][0:KP, 0:KT * T]).then_inc(ptx_sb.sem, 1)
                        if h + 4 < HEADS:
                            xmax(h + 4)
                    if j == 0:
                        dve.wait_ge(saved.sem, saved.at(i, 0))
                    normalise(1, pxd, xb[:, :], x2[:, j, :], x2_done)

                dve.wait_ge(lg_done.sem, lg_done.at(i, 1))
                wide = lambda a: a.unsqueeze(2).broadcast_to([T, GB, E])
                link(V.tensor_copy(lg[:, :, :], misc[0:T, 0:GB * E].rearrange("p (j e) -> p j e", j=GB)))
                link(V.tensor_reduce(s1[:, 0, :], lg[:, :, :], AX.X, ALU.max))
                V.tensor_tensor(lg[:, :, :], lg[:, :, :], wide(s1[:, 0, :]), ALU.subtract).then_inc(lg_sub.sem, 1)
                dve.wait_ge(lg_exp.sem, lg_exp.at(i, 1))
                link(V.tensor_reduce(s1[:, 1, :], raw[:, :, :], AX.X, ALU.add))
                link(V.reciprocal(s1[:, 2, :], s1[:, 1, :]))
                link(V.tensor_tensor(raw[:, :, :], raw[:, :, :], wide(s1[:, 2, :]), ALU.mult))
                for c in range(2):
                    link(V.tensor_reduce(s1[:, 3 + c, :], raw[:, :, :], AX.X, ALU.max))
                    link(V.tensor_tensor(tmp[:, :, :], raw[:, :, :], wide(s1[:, 3 + c, :]), ALU.is_equal))
                    link(V.tensor_tensor(cand[:, :, :], tmp[:, :, :], rev[:, :].unsqueeze(1).broadcast_to([T, GB, E]), ALU.mult))
                    link(V.tensor_reduce(s1[:, 5, :], cand[:, :, :], AX.X, ALU.max))
                    last = V.tensor_tensor(pick[:, :, c, :], cand[:, :, :], wide(s1[:, 5, :]), ALU.is_equal)
                    if c == 0:
                        link(last)
                        link(V.tensor_scalar(tmp[:, :, :], pick[:, :, 0, :], -1.0, 1.0, ALU.mult, ALU.add))
                        link(V.tensor_tensor(raw[:, :, :], raw[:, :, :], tmp[:, :, :], ALU.mult))
                last.then_inc(picked.sem, 1)
                dve.wait_ge(counted.sem, counted.at(i, 1))
                link(V.tensor_copy(pos[:, :, :, :].rearrange("p j c e -> p (j c e)"), misc[0:T, 0:4 * E]))
                link(V.tensor_scalar(tmp[:, :, :], pos[:, :, 0, :], float(CAP), None, ALU.is_lt))
                V.tensor_tensor(kept[:, :, 0, :], pick[:, :, 0, :], tmp[:, :, :], ALU.mult).then_inc(kept1.sem, 1)
                dve.wait_ge(total1.sem, total1.at(i, 1))
                link(V.tensor_copy(cand[:, 0, :], misc[0:T, 4 * E:5 * E]))
                link(V.tensor_tensor(pos[:, :, 1, :], pos[:, :, 1, :], cand[:, 0, :].unsqueeze(1).broadcast_to([T, GB, E]), ALU.add))
                link(V.tensor_scalar(tmp[:, :, :], pos[:, :, 1, :], float(CAP), None, ALU.is_lt))
                link(V.tensor_tensor(kept[:, :, 1, :], pick[:, :, 1, :], tmp[:, :, :], ALU.mult))
                link(V.tensor_reduce(gate[:, :, :], kept[:, :, :, :], AX.X, ALU.add))
                link(V.tensor_tensor(gate[:, :, :], gate[:, :, :], s1[:, 3:5, :].rearrange("p c j -> p j c"), ALU.mult))
                link(V.tensor_tensor(pos[:, :, :, :], pos[:, :, :, :], kept[:, :, :, :], ALU.mult))
                link(V.tensor_reduce(place[:, :, :], pos[:, :, :, :], AX.X, ALU.add))
                for j in range(GB):
                    for c in range(2):
                        last = V.tensor_scalar(onehot[:, j, c, :], slot_no[:, :], place[:, j, c:c + 1], gate[:, j, c:c + 1], ALU.is_equal, ALU.mult)
                link(last)
                for j in range(GB):
                    spread = lambda a, n: a.unsqueeze(2).broadcast_to([T, E, CAP]) if n else a.unsqueeze(1).broadcast_to([T, E, CAP])
                    V.tensor_tensor(comb[:, j, :, :], spread(kept[:, j, 0, :], 1), spread(onehot[:, j, 0, :], 0), ALU.mult)
                    link(V.tensor_tensor(comb2[:, j, :, :], spread(kept[:, j, 1, :], 1), spread(onehot[:, j, 1, :], 0), ALU.mult))
                    link(V.tensor_tensor(comb[:, j, :, :], comb[:, j, :, :], comb2[:, j, :, :], ALU.add))
                    last = V.tensor_scalar(disp[:, j, :], comb[:, j, :, :].rearrange("p e c -> p (e c)"), 0.0, None, ALU.not_equal)
                last.then_inc(routed.sem, 1)
            assert vlink.seen == vlink.per, vlink.seen



def expert_phase(nc, d, own):
    NP = 2
    ctx = ExitStack()
    with ctx:
        def sb(name, shape, dt=F32):
            return ctx.enter_context(nc.sbuf_tensor("b_" + name, shape, dt))

        def sem(name, per, unit=1, early=False):
            return Steps(own("b_" + name, early), per, unit, early)

        w0 = [sb(f"w0_{n}", [128, KC, HID]) for n in range(NP)]
        w1 = [sb(f"w1_{n}", [128, KC, HID]) for n in range(NP)]
        wo = [sb(f"wo_{n}", [HP, HT, D]) for n in range(NP)]
        xe = [sb(f"xe_{n}", [128, KC, G, CAP]) for n in range(NP)]
        act_out = sb("act_out", [HP, 2, SL])
        hid = sb("hid", [HP, HT, SL])
        eo = [sb(f"eo_{n}", [T, ST, D]) for n in range(NP)]
        up = [ctx.enter_context(nc.psum_tensor(f"b_up{n}", [128, 512], F32)) for n in range(4)]
        down = [ctx.enter_context(nc.psum_tensor(f"b_down{n}", [128, 512], F32)) for n in range(4)]

        loaded = [sem(f"loaded{n}", 5, 16) for n in range(NP)]
        up_done = sem("up_done", NP * HT)
        gelu = sem("gelu", NP * HT)
        hid_done = sem("hid_done", NP * HT, early=True)
        down_done = sem("down_done", NP * ST)
        eo_sb = sem("eo_sb", NP * ST, early=True)
        stored = [sem(f"stored{n}", 2, 16) for n in range(NP)]
        saved = sem("saved", NP, early=True)
        block = ctx.enter_context(nc.Block())

        @block.sync
        def _(sp):
            def load(e, n):
                for dst, src in ((w0[n][:, :, :], d["w0"][e]), (w1[n][:, :, :], d["w1"][e]), (wo[n][:, :, :], d["wo"][e])):
                    sp.dma_start(dst, src).then_inc(loaded[n].sem, 16)
                for kc in range(KC):
                    sp.dma_start(xe[n][:, kc, :, :], d["s_xe_by_expert"][e][kc]).then_inc(loaded[n].sem, 16)

            for n in range(NP):
                load(n, n)
            with sp.Fori(0, E // NP - 1) as i:
                for n in range(NP):
                    sp.wait_ge(down_done.sem, down_done.at(i, (n + 1) * ST))
                    load(i * NP + (NP + n), n)

        @block.gpsimd
        def _(pool):
            with pool.Fori(0, E // NP) as i:
                for n in range(NP):
                    pool.wait_ge(eo_sb.sem, eo_sb.at(i, (n + 1) * ST))
                    for g in range(2):
                        pool.dma_start(d["s_eo_by_expert"][i * NP + n][g], eo[n][g * CAP:(g + 1) * CAP, :, :]).then_inc(stored[n].sem, 16)
                    pool.wait_ge(stored[n].sem, stored[n].at(i, 2))
                    pool.sem_inc(saved.sem, 1)

        @block.tensor
        def _(pe):
            mm = nc.tensor.matmul
            with pe.Fori(0, E // NP) as i:
                for n in range(NP):
                    pe.wait_ge(loaded[n].sem, loaded[n].at(i, 5))
                    for h in range(HT):
                        pe.wait_ge(hid_done.sem, hid_done.at(i, max(n * HT + h - 1, 0)))
                        for m, w in enumerate((w0[n], w1[n])):
                            for kc in range(KC):
                                last = mm(up[2 * (h % 2) + m][0:HP, 0:SL], w[:, kc, h * HP:(h + 1) * HP],
                                          xe[n][:, kc, :, :].rearrange("p g c -> p (g c)"), start=kc == 0, stop=kc == KC - 1)
                        last.then_inc(up_done.sem, 1)
                    for s in range(ST):
                        pe.wait_ge(eo_sb.sem, eo_sb.at(i, max(n * ST + s - 3, 0)))
                        for h in range(HT):
                            if s == 0:
                                pe.wait_ge(hid_done.sem, hid_done.at(i, n * HT + h + 1))
                            last = mm(down[s][0:T, 0:D], hid[:, h, s * T:(s + 1) * T], wo[n][:, h, :], start=h == 0, stop=h == HT - 1)
                        last.then_inc(down_done.sem, 1)

        @block.scalar
        def _(act):
            with act.Fori(0, E // NP) as i:
                for n in range(NP):
                    for h in range(HT):
                        act.wait_ge(up_done.sem, up_done.at(i, n * HT + h + 1))
                        nc.scalar.activation(act_out[:, h % 2, :], up[2 * (h % 2)][0:HP, 0:SL], ACT.Gelu_apprx_tanh).then_inc(gelu.sem, 1)

        @block.vector
        def _(dve):
            with dve.Fori(0, E // NP) as i:
                for n in range(NP):
                    for h in range(HT):
                        dve.wait_ge(gelu.sem, gelu.at(i, n * HT + h + 1))
                        nc.vector.tensor_tensor(hid[:, h, :], up[2 * (h % 2) + 1][0:HP, 0:SL], act_out[:, h % 2, :], ALU.mult).then_inc(hid_done.sem, 1)
                    dve.wait_ge(saved.sem, saved.at(i, 0))
                    for s in range(ST):
                        dve.wait_ge(down_done.sem, down_done.at(i, n * ST + s + 1))
                        nc.vector.tensor_copy(eo[n][:, s, :], down[s][0:T, 0:D]).then_inc(eo_sb.sem, 1)

DIN, NST, RANK, TAPS = 512, 16, 64, 4
DT = DIN // 128
QB = 4
QT = QB * T
XD = RANK + 2 * NST
SPREAD = 6


def mixer_phase(nc, d, own):
    ctx = ExitStack()
    with ctx:
        def sb(name, shape, dt=F32):
            return ctx.enter_context(nc.sbuf_tensor("c_" + name, shape, dt))

        def sem(name, per, unit=1, early=False):
            return Steps(own("c_" + name, early), per, unit, early)

        win = sb("win", [128, KC, 2 * DIN])
        convw = sb("convw", [128, DT, TAPS])
        convb = sb("convb", [128, DT])
        wx = sb("wx", [128, DT, XD])
        wdt = sb("wdt", [RANK, DIN])
        bdt = sb("bdt", [128, DT])
        alog = sb("alog", [128, DT, NST])
        aneg = sb("aneg", [128, DT, NST])
        dp = sb("dp", [128, DT])
        wout = sb("wout", [128, DT, D])
        ident = sb("ident", [128, 128])
        row_of = sb("row_of", [XD, 2 * NST, 128])

        x2 = sb("x2", [T, QB // GB, GB, D])
        eo = sb("eo", [T, QB // GB, ST, D])
        ct = sb("ct", [T, QB // GB, GB, ST, T])
        t = sb("t", [T, QB, D])
        stats = sb("stats", [T, QB, 10])
        x3 = sb("x3", [T, QB, D])
        x3t = sb("x3t", [128, KC, QT])
        u = sb("u", [128, DT, QB, TAPS - 1 + T])
        conv = sb("conv", [128, DT, QT])
        us = sb("us", [128, DT, QT])
        rs = sb("rs", [128, DT, QT])
        xd = sb("xd", [XD, QT])
        z = sb("z", [128, DT, QT])
        soft = sb("soft", [128, DT, QT])
        delta = sb("delta", [128, DT, QT])
        du = sb("du", [128, DT, QT])
        bc = sb("bc", [128, 2 * NST, QT])
        decay = sb("decay", [128, 2, QT])
        bu = sb("bu", [128, 3, QT])
        state = sb("state", [128, 2, QT])
        out_c = sb("out_c", [128, 2, QT])
        x4 = sb("x4", [T, QB, D])
        bank = [ctx.enter_context(nc.psum_tensor(f"c_bank{n}", [128, 512], F32)) for n in range(8)]

        weights = sem("weights", 1)
        ready = sem("ready", 1)
        loaded = sem("loaded", 3 * (QB // GB), 16)
        gathered = sem("gathered", QB)
        g_read = sem("g_read", QB, early=True)
        x3_done = sem("x3_done", QB)
        x3t_done = sem("x3t_done", 1)
        x3t_sb = sem("x3t_sb", 1)
        xr = sem("xr", 2 * DT)
        xr_sb = sem("xr_sb", 2 * DT, early=True)
        conv_done = sem("conv_done", DT)
        us_done = sem("us_done", DT)
        xd_done = sem("xd_done", 1)
        xd_sb = sem("xd_sb", 1)
        dz = sem("dz", DT)
        z_done = sem("z_done", DT, early=True)
        alink = sem("alink", 2 * DT)
        sp_done = sem("sp_done", DT)
        du_done = sem("du_done", DT, early=True)
        bc_done = sem("bc_done", 2 * NST)
        bc_sb = sem("bc_sb", 2 * NST, early=True)
        decayed = sem("decayed", DT * NST)
        bu_done = sem("bu_done", DT * NST)
        scanned = sem("scanned", DT * NST, early=True)
        weighted = sem("weighted", DT * NST, early=True)
        summed = sem("summed", DT * NST, early=True)
        y_done = sem("y_done", DT, early=True)
        out_done = sem("out_done", QB)
        x4_done = sem("x4_done", QB, early=True)
        stored = sem("stored", 1, 16)
        saved = sem("saved", 1, early=True)
        vlink = sem("vlink", 61)
        gather_bank = [0, 1, 6, 7]
        block = ctx.enter_context(nc.Block())
        flat = lambda a: a.rearrange("p a b -> p (a b)")

        loads = [(win[:, :, :], d["win"]), (convw[:, :, :], d["convw"]), (convb[:, :], d["convb"]), (wx[:, :, :], d["wx"]),
                 (wdt[:, :], d["wdt"]), (bdt[:, :], d["bdt"]), (alog[:, :, :], d["alog"]), (dp[:, :], d["dp"]),
                 (wout[:, :, :], d["wout"]), (ident[:, :], d["ident"]), (row_of[:, :, :], d["row_of"])]

        @block.sync
        def _(sp):
            for dst, src in loads:
                sp.dma_start(dst, src).then_inc(weights.sem, 16)
            with sp.Fori(0, B // QB) as i:
                sp.wait_ge(g_read.sem, g_read.at(i, 0))
                for g in range(QB // GB):
                    sp.dma_start(x2[:, g, :, :], d["s_x2"][i * (QB // GB) + g]).then_inc(loaded.sem, 16)
                    sp.dma_start(eo[:, g, :, :], d["s_eo_by_group"][i * (QB // GB) + g]).then_inc(loaded.sem, 16)
                    sp.dma_start(ct[:, g, :, :, :], d["s_ct"][i * (QB // GB) + g]).then_inc(loaded.sem, 16)

        @block.gpsimd
        def _(pool):
            nc.gpsimd.memset(u[:, :, :, :].rearrange("p a b c -> p (a b c)"), 0.0)
            nc.gpsimd.memset(flat(decay[:, :, :]), 0.0).then_inc(ready.sem, 1)
            with pool.Fori(0, B // QB) as i:
                for k in range(DT * NST):
                    pool.wait_ge(scanned.sem, scanned.at(i, k + 1))
                    pool.wait_ge(summed.sem, summed.at(i, max(k - 1, 0)))
                    nc.gpsimd.tensor_tensor(out_c[:, k % 2, :], state[:, k % 2, :], bc[:, NST + k % NST, :], ALU.mult).then_inc(weighted.sem, 1)
                pool.wait_ge(x4_done.sem, x4_done.at(i, QB))
                pool.dma_start(d["s_x4_by_four"][i], x4[:, :, :]).then_inc(stored.sem, 16)
                pool.wait_ge(stored.sem, stored.at(i, 1))
                pool.sem_inc(saved.sem, 1)

        @block.tensor
        def _(pe):
            mm = nc.tensor.matmul
            pe.wait_ge(weights.sem, 16 * len(loads))
            with pe.Fori(0, B // QB) as i:
                pe.wait_ge(loaded.sem, loaded.at(i, 6))
                pe.wait_ge(x4_done.sem, x4_done.at(i, 0))
                for b in range(QB):
                    for s in range(ST):
                        last = mm(bank[gather_bank[b]][0:T, 0:D], ct[:, b // GB, b % GB, s, :], eo[:, b // GB, s, :], start=s == 0, stop=s == ST - 1)
                    last.then_inc(gathered.sem, 1)
                for b in range(QB):
                    pe.wait_ge(x3_done.sem, x3_done.at(i, b + 1))
                    for kc in range(KC):
                        last = nc.tensor.transpose(bank[2 + kc][:, b * T:(b + 1) * T], x3[:, b, kc * 128:(kc + 1) * 128], ident[0:T, 0:T])
                last.then_inc(x3t_done.sem, 1)
                pe.wait_ge(x3t_sb.sem, x3t_sb.at(i, 1))
                for k in range(2 * DT):
                    pe.wait_ge(xr_sb.sem, xr_sb.at(i, max(k - 1, 0)))
                    for kc in range(KC):
                        last = mm(bank[4 + k % 2][:, 0:QT], win[:, kc, k * 128:(k + 1) * 128], x3t[:, kc, :], start=kc == 0, stop=kc == KC - 1)
                    last.then_inc(xr.sem, 1)
                for k in range(DT):
                    pe.wait_ge(us_done.sem, us_done.at(i, k + 1))
                    last = mm(bank[6][0:XD, 0:QT], wx[:, k, :], us[:, k, :], start=k == 0, stop=k == DT - 1)
                last.then_inc(xd_done.sem, 1)
                pe.wait_ge(xd_sb.sem, xd_sb.at(i, 1))
                pe.wait_ge(xr_sb.sem, xr_sb.at(i, 2 * DT))

                def spread(k):
                    pe.wait_ge(bc_sb.sem, bc_sb.at(i, max(k + 1 - SPREAD, 0)))
                    mm(bank[k % SPREAD][:, 0:QT], row_of[RANK:XD, (k % 2) * NST + k // 2, :], xd[RANK:XD, :], start=True, stop=True,
                       tile_position=(RANK, 0)).then_inc(bc_done.sem, 1)

                for k in range(4):
                    spread(k)
                for k in range(DT):
                    pe.wait_ge(z_done.sem, z_done.at(i, max(k - 1, 0)))
                    mm(bank[4 + k % 2][:, 0:QT], wdt[:, k * 128:(k + 1) * 128], xd[0:RANK, :], start=True, stop=True).then_inc(dz.sem, 1)

                pe.wait_ge(z_done.sem, z_done.at(i, DT))
                for k in range(4, SPREAD):
                    spread(k)
                for k in range(DT * NST):
                    for n in range(SPREAD + 2 * k, SPREAD + 2 * k + 2):
                        if n < 2 * NST:
                            spread(n)
                    n, dt = k % NST, k // NST
                    if n == 0:
                        pe.wait_ge(y_done.sem, y_done.at(i, max(dt - 1, 0)))
                    pe.wait_ge(weighted.sem, weighted.at(i, k + 1))
                    mm(bank[6 + dt % 2][:, 0:QT], ident[:, :], out_c[:, k % 2, :], start=n == 0, stop=n == NST - 1).then_inc(summed.sem, 1)
                pe.wait_ge(y_done.sem, y_done.at(i, DT))
                for b in range(QB):
                    for k in range(DT):
                        last = mm(bank[b][0:T, 0:D], rs[:, k, b * T:(b + 1) * T], wout[:, k, :], start=k == 0, stop=k == DT - 1)
                    last.then_inc(out_done.sem, 1)

        @block.scalar
        def _(act):
            fn = nc.scalar.activation
            act.wait_ge(weights.sem, 16 * len(loads))
            fn(flat(aneg[:, :, :]), flat(alog[:, :, :]), ACT.Exp).then_inc(ready.sem, 1)
            act.wait_ge(ready.sem, 3)
            with act.Fori(0, B // QB) as i:
                act.wait_ge(x3t_done.sem, x3t_done.at(i, 1))
                fn(x3t[:, 0, :], bank[2][:, 0:QT], ACT.Copy)
                fn(x3t[:, 1, :], bank[3][:, 0:QT], ACT.Copy).then_inc(x3t_sb.sem, 1)
                for k in range(2 * DT):
                    act.wait_ge(xr.sem, xr.at(i, k + 1))
                    src = bank[4 + k % 2][:, 0:QT]
                    if k < DT:
                        fn(u[:, k, :, TAPS - 1:], src.rearrange("p (b t) -> p b t", b=QB), ACT.Copy).then_inc(xr_sb.sem, 1)
                    else:
                        fn(rs[:, k - DT, :], src, ACT.Silu).then_inc(xr_sb.sem, 1)
                for k in range(DT):
                    act.wait_ge(conv_done.sem, conv_done.at(i, k + 1))
                    fn(us[:, k, :], conv[:, k, :], ACT.Silu, bias=convb[:, k:k + 1]).then_inc(us_done.sem, 1)
                act.wait_ge(xd_done.sem, xd_done.at(i, 1))
                fn(xd[:, :], bank[6][0:XD, 0:QT], ACT.Copy).then_inc(xd_sb.sem, 1)

                def take_rows(k):
                    for n in range(2):
                        act.wait_ge(bc_done.sem, bc_done.at(i, 2 * k + n + 1))
                        fn(bc[:, n * NST + k, :], bank[(2 * k + n) % SPREAD][:, 0:QT], ACT.Copy).then_inc(bc_sb.sem, 1)

                take_rows(0)
                take_rows(1)
                for k in range(DT):
                    act.wait_ge(z_done.sem, z_done.at(i, k + 1))
                    fn(soft[:, k, :], z[:, k, :], ACT.Abs).then_inc(alink.sem, 1)
                for k in range(DT):
                    act.wait_ge(alink.sem, alink.at(i, k + 1))
                    fn(soft[:, k, :], soft[:, k, :], ACT.Exp, scale=-1.0).then_inc(alink.sem, 1)
                for k in range(DT):
                    act.wait_ge(alink.sem, alink.at(i, DT + k + 1))
                    fn(soft[:, k, :], soft[:, k, :], ACT.Ln, bias=1.0).then_inc(sp_done.sem, 1)
                for k in range(DT * NST):
                    if 2 <= k < NST:
                        take_rows(k)
                    if k % NST == 0:
                        act.wait_ge(du_done.sem, du_done.at(i, k // NST + 1))
                    act.wait_ge(scanned.sem, scanned.at(i, max(k - 1, 0)))
                    by_seq = lambda a: a.rearrange("p (b t) -> p b t", b=QB)[:, :, 1:]
                    fn(by_seq(decay[:, k % 2, :]), by_seq(delta[:, k // NST, :]), ACT.Exp,
                       scale=aneg[:, k // NST, k % NST:k % NST + 1]).then_inc(decayed.sem, 1)

        @block.vector
        def _(dve):
            V = nc.vector
            dve.wait_ge(weights.sem, 16 * len(loads))
            dve.wait_ge(ready.sem, 2)
            V.tensor_scalar(flat(aneg[:, :, :]), flat(aneg[:, :, :]), -1.0, None, ALU.mult).then_inc(ready.sem, 1)
            with dve.Fori(0, B // QB) as i:
                link = lambda ins: vlink.chain(dve, i, ins)
                dve.wait_ge(loaded.sem, loaded.at(i, 6))
                for b in range(QB):
                    dve.wait_ge(gathered.sem, gathered.at(i, b + 1))
                    V.tensor_tensor(t[:, b, :], bank[gather_bank[b]][0:T, 0:D], x2[:, b // GB, b % GB, :], ALU.add).then_inc(g_read.sem, 1)
                dve.wait_ge(g_read.sem, g_read.at(i, QB))
                layer_norms(dve, nc, vlink, i, [t[:, b, :] for b in range(QB)], stats, [x3[:, b, :] for b in range(QB)], x3_done)
                for k in range(DT):
                    dve.wait_ge(xr_sb.sem, xr_sb.at(i, k + 1))
                    c3 = conv[:, k, :].rearrange("p (b t) -> p b t", b=QB)
                    link(V.tensor_scalar(c3, u[:, k, :, 0:T], convw[:, k, 0:1], None, ALU.mult))
                    for tap in range(1, TAPS):
                        last = V.scalar_tensor_tensor(c3, u[:, k, :, tap:tap + T], convw[:, k, tap:tap + 1], c3, ALU.mult, ALU.add)
                        if tap < TAPS - 1:
                            link(last)
                    last.then_inc(conv_done.sem, 1)
                for k in range(DT):
                    dve.wait_ge(dz.sem, dz.at(i, k + 1))
                    V.tensor_scalar(z[:, k, :], bank[4 + k % 2][:, 0:QT], bdt[:, k:k + 1], None, ALU.add).then_inc(z_done.sem, 1)
                for k in range(DT):
                    dve.wait_ge(sp_done.sem, sp_done.at(i, k + 1))
                    link(V.scalar_tensor_tensor(delta[:, k, :], z[:, k, :], 0.0, soft[:, k, :], ALU.max, ALU.add))
                    V.tensor_tensor(du[:, k, :], delta[:, k, :], us[:, k, :], ALU.mult).then_inc(du_done.sem, 1)
                dve.wait_ge(du_done.sem, du_done.at(i, DT))

                def times_b(k):
                    if k < NST:
                        dve.wait_ge(bc_sb.sem, bc_sb.at(i, 2 * k + 1))
                    dve.wait_ge(scanned.sem, scanned.at(i, max(k - 2, 0)))
                    V.tensor_tensor(bu[:, k % 3, :], du[:, k // NST, :], bc[:, k % NST, :], ALU.mult).then_inc(bu_done.sem, 1)

                def gate(dt):
                    dve.wait_ge(summed.sem, summed.at(i, (dt + 1) * NST))
                    link(V.scalar_tensor_tensor(conv[:, dt, :], us[:, dt, :], dp[:, dt:dt + 1], bank[6 + dt % 2][:, 0:QT], ALU.mult, ALU.add))
                    V.tensor_tensor(rs[:, dt, :], conv[:, dt, :], rs[:, dt, :], ALU.mult).then_inc(y_done.sem, 1)

                times_b(0)
                for k in range(DT * NST):
                    if k + 1 < DT * NST:
                        times_b(k + 1)
                    dve.wait_ge(bu_done.sem, bu_done.at(i, k + 1))
                    dve.wait_ge(decayed.sem, decayed.at(i, k + 1))
                    dve.wait_ge(weighted.sem, weighted.at(i, max(k - 1, 0)))
                    V.tensor_tensor_scan(state[:, k % 2, :], decay[:, k % 2, :], bu[:, k % 3, :], 0.0, ALU.mult, ALU.add).then_inc(scanned.sem, 1)
                    if k % NST == 4 and k > NST:
                        gate(k // NST - 1)
                gate(DT - 1)
                dve.wait_ge(saved.sem, saved.at(i, 0))
                for b in range(QB):
                    dve.wait_ge(out_done.sem, out_done.at(i, b + 1))
                    last = V.tensor_tensor(t[:, b, :], bank[b][0:T, 0:D], x3[:, b, :], ALU.add)
                link(last)
                layer_norms(dve, nc, vlink, i, [t[:, b, :] for b in range(QB)], stats, [x4[:, b, :] for b in range(QB)], x4_done)
            assert vlink.seen == vlink.per, vlink.seen

ROUNDS = 3
RMS_EPS = 1e-6
SLOT_INPUTS = ["ctxt", "ctx_rows", "wk", "wv", "wq", "wih", "whh", "L1_xattn_gru_bih", "L1_xattn_gru_bhh", "snorm", "inorm", "ident"]


def slot_phase(nc, d, own):
    ctx = ExitStack()
    with ctx:
        def sb(name, shape, dt=F32):
            return ctx.enter_context(nc.sbuf_tensor("d_" + name, shape, dt))

        def sem(name, per, unit=1, early=False):
            return Steps(own("d_" + name, early), per, unit, early)

        wk = sb("wk", [128, KC, D])
        wv = sb("wv", [128, KC, D])
        wq = sb("wq", [128, KC, D])
        wih = sb("wih", [128, KC, 3 * D])
        whh = sb("whh", [128, KC, 3 * D])
        bih = sb("bih", [T, 3 * D])
        bhh = sb("bhh", [T, 3 * D])
        snorm = sb("snorm", [128, KC])
        inorm = sb("inorm", [128, KC])
        ident = sb("ident", [128, 128])

        ctxt = sb("ctxt", [128, GB, KC, S2])
        rows = sb("rows", [KP, GB, KT, D])
        x4 = sb("x4", [T, GB, D])
        csq = sb("csq", [KP, GB, KT, D])
        ssq = sb("ssq", [T, GB, D])
        csum = sb("csum", [KP, GB, KT])
        cinv = sb("cinv", [KP, GB, KT])
        ctmp = sb("ctmp", [KP, GB, KT])
        cscale = sb("cscale", [KP, GB, KT])
        kt = sb("kt", [128, GB, KC, S2])
        v = sb("v", [KP, GB, KT, D + 1])
        ssum = sb("ssum", [T, GB])
        sinv = sb("sinv", [T, GB])
        stmp = sb("stmp", [T, GB])
        s = sb("s", [T, GB, D])
        sn = sb("sn", [T, GB, D])
        stn = sb("stn", [128, GB, 2 * KC, T])
        qt = sb("qt", [128, GB, KC, T])
        smax = sb("smax", [KP, GB, KT])
        nmax = sb("nmax", [KP, GB, KT])
        esum = sb("esum", [KP, GB, KT])
        einv = sb("einv", [KP, GB, KT])
        e = sb("e", [KP, GB, KT, T])
        den = sb("den", [T, GB])
        upd = sb("upd", [T, GB, D])
        ut = sb("ut", [128, GB, KC, T])
        rz = sb("rz", [T, GB, 2 * D])
        hn = sb("hn", [T, GB, D])
        xn = sb("xn", [T, GB, D])
        cand = sb("cand", [T, GB, D])
        t = sb("t", [T, GB, D])
        stats = sb("stats", [T, GB, 10])
        x5 = sb("x5", [T, GB, D])
        small = [ctx.enter_context(nc.psum_tensor(f"d_small{j}", [128, 512], F32)) for j in range(GB)]
        wide = [ctx.enter_context(nc.psum_tensor(f"d_wide{j}", [128, 512], F32)) for j in range(GB)]
        gates = [ctx.enter_context(nc.psum_tensor(f"d_gates{j}", [128, 512], F32)) for j in range(GB)]
        news = [ctx.enter_context(nc.psum_tensor(f"d_news{j}", [128, 512], F32)) for j in range(GB)]

        N = ROUNDS * GB
        weights = sem("weights", 1)
        ready = sem("ready", 1)
        in_ctx = [sem(f"in_ctx{j}", 2, 16) for j in range(GB)]
        in_x = [sem(f"in_x{j}", 1, 16) for j in range(GB)]
        squares = sem("squares", GB)
        kproj = sem("kproj", GB)
        k_sb = sem("k_sb", GB)
        vproj = sem("vproj", GB * KT)
        v_sb = sem("v_sb", GB * KT, early=True)
        s_sq = sem("s_sq", N)
        sn_done = sem("sn_done", N)
        stn_done = sem("stn_done", N)
        stn_sb = sem("stn_sb", N)
        q_done = sem("q_done", N)
        q_sb = sem("q_sb", N)
        score = sem("score", N)
        max_done = sem("max_done", N)
        exp_done = sem("exp_done", N)
        attn = sem("attn", N)
        u_done = sem("u_done", N)
        upd_done = sem("upd_done", N)
        ut_done = sem("ut_done", N)
        ut_sb = sem("ut_sb", N)
        gru = sem("gru", N)
        rz_sb = sem("rz_sb", N)
        rz_tanh = sem("rz_tanh", N)
        pre_n = sem("pre_n", N)
        n_tanh = sem("n_tanh", N)
        s_done = sem("s_done", N, early=True)
        x5_done = sem("x5_done", GB, early=True)
        stored = sem("stored", 1, 16)
        saved = sem("saved", 1, early=True)
        vlink = sem("vlink", 151)
        block = ctx.enter_context(nc.Block())
        loads = [(wk[:, :, :], d["wk"]), (wv[:, :, :], d["wv"]), (wq[:, :, :], d["wq"]), (wih[:, :, :], d["wih"]), (whh[:, :, :], d["whh"]),
                 (bih[:, :], d["L1_xattn_gru_bih"].partition_broadcast(T)), (bhh[:, :], d["L1_xattn_gru_bhh"].partition_broadcast(T)),
                 (snorm[:, :], d["snorm"]), (inorm[:, :], d["inorm"]), (ident[:, :], d["ident"])]

        def slots(r, j):
            return x4[:, j, :] if r == 0 else s[:, j, :]

        @block.sync
        def _(sp):
            for dst, src in loads:
                sp.dma_start(dst, src).then_inc(weights.sem, 16)
            with sp.Fori(0, B // GB) as i:
                sp.wait_ge(v_sb.sem, v_sb.at(i, 0))
                for j in range(GB):
                    sp.dma_start(ctxt[:, j, :, :], d["ctxt"][i * GB + j]).then_inc(in_ctx[j].sem, 16)
                    sp.dma_start(rows[:, j, :, :], d["ctx_rows"][i * GB + j]).then_inc(in_ctx[j].sem, 16)
                sp.wait_ge(x5_done.sem, x5_done.at(i, 0))
                for j in range(GB):
                    sp.dma_start(x4[:, j, :], d["s_x4"][i * GB + j]).then_inc(in_x[j].sem, 16)

        @block.gpsimd
        def _(pool):
            with pool.Fori(0, B // GB) as i:
                pool.wait_ge(x5_done.sem, x5_done.at(i, GB))
                pool.dma_start(d["s_x5_by_two"][i], x5[:, :, :]).then_inc(stored.sem, 16)
                pool.wait_ge(stored.sem, stored.at(i, 1))
                pool.sem_inc(saved.sem, 1)

        @block.tensor
        def _(pe):
            mm = nc.tensor.matmul
            pe.wait_ge(ready.sem, 1)
            with pe.Fori(0, B // GB) as i:
                for j in range(GB):
                    pe.wait_ge(in_ctx[j].sem, in_ctx[j].at(i, 2))
                    pe.wait_ge(s_done.sem, s_done.at(i, 0))
                    for oc, bank in enumerate((gates[j], news[j])):
                        for kc in range(KC):
                            last = mm(bank[:, 0:S2], wk[:, kc, oc * 128:(oc + 1) * 128], ctxt[:, j, kc, :], start=kc == 0, stop=kc == KC - 1)
                    last.then_inc(kproj.sem, 1)
                    for k, bank in enumerate((small[j], wide[j], gates[j])):
                        if k == 2:
                            pe.wait_ge(k_sb.sem, k_sb.at(i, j + 1))
                        for kc in range(KC):
                            last = mm(bank[0:KP, 0:D], ctxt[:, j, kc, k * KP:(k + 1) * KP], wv[:, kc, :], start=kc == 0, stop=kc == KC - 1)
                        last.then_inc(vproj.sem, 1)
                for r in range(ROUNDS):
                    for j in range(GB):
                        n = r * GB + j
                        pe.wait_ge(sn_done.sem, sn_done.at(i, n + 1))
                        if r == 0:
                            pe.wait_ge(v_sb.sem, v_sb.at(i, (j + 1) * KT))
                        for m, src in enumerate((slots(r, j), sn[:, j, :])):
                            for kc in range(KC):
                                c = m * KC + kc
                                last = nc.tensor.transpose(small[j][:, c * T:(c + 1) * T], src[:, kc * 128:(kc + 1) * 128], ident[0:T, 0:T])
                        last.then_inc(stn_done.sem, 1)
                    for j in range(GB):
                        n = r * GB + j
                        pe.wait_ge(stn_sb.sem, stn_sb.at(i, n + 1))
                        for oc in range(KC):
                            for kc in range(KC):
                                last = mm(small[j][:, oc * T:(oc + 1) * T], wq[:, kc, oc * 128:(oc + 1) * 128], stn[:, j, KC + kc, :],
                                          start=kc == 0, stop=kc == KC - 1)
                        last.then_inc(q_done.sem, 1)
                    for j in range(GB):
                        for kc in range(KC):
                            mm(gates[j][0:T, :], stn[:, j, kc, :], whh[:, kc, 0:2 * D], start=kc == 0, stop=False)
                        for kc in range(KC):
                            mm(news[j][0:T, D:2 * D], stn[:, j, kc, :], whh[:, kc, 2 * D:3 * D], start=kc == 0, stop=kc == KC - 1)
                    for j in range(GB):
                        n = r * GB + j
                        pe.wait_ge(q_sb.sem, q_sb.at(i, n + 1))
                        for k in range(KT):
                            for kc in range(KC):
                                last = mm(wide[j][0:KP, k * T:(k + 1) * T], kt[:, j, kc, k * KP:(k + 1) * KP], qt[:, j, kc, :],
                                          start=kc == 0, stop=kc == KC - 1)
                        last.then_inc(score.sem, 1)
                    for j in range(GB):
                        n = r * GB + j
                        pe.wait_ge(attn.sem, attn.at(i, n + 1))
                        for k in range(KT):
                            last = mm(small[j][0:T, 0:D + 1], e[:, j, k, :], v[:, j, k, :], start=k == 0, stop=k == KT - 1)
                        last.then_inc(u_done.sem, 1)
                    for j in range(GB):
                        n = r * GB + j
                        pe.wait_ge(upd_done.sem, upd_done.at(i, n + 1))
                        for kc in range(KC):
                            last = nc.tensor.transpose(wide[j][:, kc * T:(kc + 1) * T], upd[:, j, kc * 128:(kc + 1) * 128], ident[0:T, 0:T])
                        last.then_inc(ut_done.sem, 1)
                    for j in range(GB):
                        n = r * GB + j
                        pe.wait_ge(ut_sb.sem, ut_sb.at(i, n + 1))
                        for kc in range(KC):
                            mm(gates[j][0:T, :], ut[:, j, kc, :], wih[:, kc, 0:2 * D], start=False, stop=kc == KC - 1)
                        for kc in range(KC):
                            last = mm(news[j][0:T, 0:D], ut[:, j, kc, :], wih[:, kc, 2 * D:3 * D], start=kc == 0, stop=kc == KC - 1)
                        last.then_inc(gru.sem, 1)

        @block.scalar
        def _(act):
            fn = nc.scalar.activation
            act.wait_ge(ready.sem, 1)
            with act.Fori(0, B // GB) as i:
                for j in range(GB):
                    act.wait_ge(in_ctx[j].sem, in_ctx[j].at(i, 2))
                    for k in range(KT):
                        last = fn(csq[:, j, k, :], rows[:, j, k, :], ACT.Square, accum_out=csum[:, j, k:k + 1])
                    last.then_inc(squares.sem, 1)
                for j in range(GB):
                    act.wait_ge(kproj.sem, kproj.at(i, j + 1))
                    fn(kt[:, j, 0, :], gates[j][:, 0:S2], ACT.Copy)
                    fn(kt[:, j, 1, :], news[j][:, 0:S2], ACT.Copy).then_inc(k_sb.sem, 1)
                for r in range(ROUNDS):
                    for j in range(GB):
                        n = r * GB + j
                        if r == 0:
                            act.wait_ge(in_x[j].sem, in_x[j].at(i, 1))
                        else:
                            act.wait_ge(s_done.sem, s_done.at(i, n - GB + 1))
                        fn(ssq[:, j, :], slots(r, j), ACT.Square, accum_out=ssum[:, j:j + 1]).then_inc(s_sq.sem, 1)
                    for j in range(GB):
                        n = r * GB + j
                        act.wait_ge(stn_done.sem, stn_done.at(i, n + 1))
                        fn(stn[:, j, :, :].rearrange("p c t -> p (c t)"), small[j][:, 0:2 * KC * T], ACT.Copy).then_inc(stn_sb.sem, 1)
                    for j in range(GB):
                        n = r * GB + j
                        act.wait_ge(q_done.sem, q_done.at(i, n + 1))
                        fn(qt[:, j, :, :].rearrange("p c t -> p (c t)"), small[j][:, 0:KC * T], ACT.Copy).then_inc(q_sb.sem, 1)
                    for j in range(GB):
                        n = r * GB + j
                        act.wait_ge(max_done.sem, max_done.at(i, n + 1))
                        for k in range(KT):
                            last = fn(e[:, j, k, :], wide[j][0:KP, k * T:(k + 1) * T], ACT.Exp, bias=nmax[:, j, k:k + 1],
                                      scale=cscale[:, j, k:k + 1], accum_out=esum[:, j, k:k + 1])
                        last.then_inc(exp_done.sem, 1)
                    for j in range(GB):
                        n = r * GB + j
                        act.wait_ge(ut_done.sem, ut_done.at(i, n + 1))
                        fn(ut[:, j, :, :].rearrange("p c t -> p (c t)"), wide[j][:, 0:KC * T], ACT.Copy).then_inc(ut_sb.sem, 1)
                    for j in range(GB):
                        n = r * GB + j
                        act.wait_ge(rz_sb.sem, rz_sb.at(i, n + 1))
                        fn(rz[:, j, :], rz[:, j, :], ACT.Tanh, scale=0.5).then_inc(rz_tanh.sem, 1)
                    for j in range(GB):
                        n = r * GB + j
                        act.wait_ge(pre_n.sem, pre_n.at(i, n + 1))
                        fn(cand[:, j, :], xn[:, j, :], ACT.Tanh).then_inc(n_tanh.sem, 1)

        @block.vector
        def _(dve):
            V = nc.vector
            dve.wait_ge(weights.sem, 16 * len(loads))
            V.memset(v[:, :, :, :].rearrange("p a b c -> p (a b c)"), 1.0)
            for kc in range(KC):
                V.tensor_scalar(wk[:, kc, :], wk[:, kc, :], inorm[:, kc:kc + 1], None, ALU.mult)
                V.tensor_scalar(wv[:, kc, :], wv[:, kc, :], inorm[:, kc:kc + 1], None, ALU.mult)
                V.tensor_scalar(wq[:, kc, :], wq[:, kc, :], snorm[:, kc:kc + 1], None, ALU.mult)
            V.tensor_tensor(bih[:, 0:2 * D], bih[:, 0:2 * D], bhh[:, 0:2 * D], ALU.add).then_inc(ready.sem, 1)
            dve.wait_ge(ready.sem, 1)
            with dve.Fori(0, B // GB) as i:
                link = lambda ins: vlink.chain(dve, i, ins)
                for j in range(GB):
                    dve.wait_ge(squares.sem, squares.at(i, j + 1))
                    link(V.tensor_scalar(csum[:, j, :], csum[:, j, :], 1.0 / D, RMS_EPS, ALU.mult, ALU.add))
                    inverse_root(dve, nc, vlink, i, csum[:, j, :], cinv[:, j, :], ctmp[:, j, :])
                for j in range(GB):
                    link(V.tensor_scalar(cscale[:, j, :], cinv[:, j, :], D ** -0.5, None, ALU.mult))
                    for k, bank in enumerate((small[j], wide[j], gates[j])):
                        dve.wait_ge(vproj.sem, vproj.at(i, j * KT + k + 1))
                        V.tensor_scalar(v[:, j, k, 0:D], bank[0:KP, 0:D], cinv[:, j, k:k + 1], None, ALU.mult).then_inc(v_sb.sem, 1)
                for r in range(ROUNDS):
                    for j in range(GB):
                        n = r * GB + j
                        dve.wait_ge(s_sq.sem, s_sq.at(i, n + 1))
                        link(V.tensor_scalar(ssum[:, j:j + 1], ssum[:, j:j + 1], 1.0 / D, RMS_EPS, ALU.mult, ALU.add))
                        inverse_root(dve, nc, vlink, i, ssum[:, j:j + 1], sinv[:, j:j + 1], stmp[:, j:j + 1])
                        V.tensor_scalar(sn[:, j, :], slots(r, j), sinv[:, j:j + 1], None, ALU.mult).then_inc(sn_done.sem, 1)
                    for j in range(GB):
                        n = r * GB + j
                        dve.wait_ge(score.sem, score.at(i, n + 1))
                        link(V.tensor_reduce(smax[:, j, :], wide[j][0:KP, 0:KT * T].rearrange("p (k t) -> p k t", k=KT), AX.X, ALU.max))
                        V.scalar_tensor_tensor(nmax[:, j, :], smax[:, j, :], -1.0, cscale[:, j, :], ALU.mult, ALU.mult).then_inc(max_done.sem, 1)
                    for j in range(GB):
                        n = r * GB + j
                        dve.wait_ge(exp_done.sem, exp_done.at(i, n + 1))
                        link(V.reciprocal(einv[:, j, :], esum[:, j, :]))
                        V.tensor_tensor(e[:, j, :, :], e[:, j, :, :], einv[:, j, :].unsqueeze(2).broadcast_to([KP, KT, T]), ALU.mult).then_inc(attn.sem, 1)
                    for j in range(GB):
                        n = r * GB + j
                        dve.wait_ge(u_done.sem, u_done.at(i, n + 1))
                        link(V.tensor_scalar(den[:, j:j + 1], small[j][0:T, D:D + 1], RMS_EPS, None, ALU.add))
                        link(V.reciprocal(den[:, j:j + 1], den[:, j:j + 1]))
                        V.tensor_scalar(upd[:, j, :], small[j][0:T, 0:D], den[:, j:j + 1], None, ALU.mult).then_inc(upd_done.sem, 1)
                    for j in range(GB):
                        n = r * GB + j
                        dve.wait_ge(gru.sem, gru.at(i, n + 1))
                        V.tensor_tensor(rz[:, j, :], gates[j][0:T, :], bih[:, 0:2 * D], ALU.add).then_inc(rz_sb.sem, 1)
                        V.tensor_tensor(hn[:, j, :], news[j][0:T, D:2 * D], bhh[:, 2 * D:3 * D], ALU.add)
                        link(V.tensor_tensor(xn[:, j, :], news[j][0:T, 0:D], bih[:, 2 * D:3 * D], ALU.add))
                    for j in range(GB):
                        n = r * GB + j
                        dve.wait_ge(rz_tanh.sem, rz_tanh.at(i, n + 1))
                        link(V.tensor_scalar(rz[:, j, :], rz[:, j, :], 0.5, 0.5, ALU.mult, ALU.add))
                        link(V.tensor_tensor(hn[:, j, :], rz[:, j, 0:D], hn[:, j, :], ALU.mult))
                        V.tensor_tensor(xn[:, j, :], xn[:, j, :], hn[:, j, :], ALU.add).then_inc(pre_n.sem, 1)
                    for j in range(GB):
                        n = r * GB + j
                        dve.wait_ge(n_tanh.sem, n_tanh.at(i, n + 1))
                        link(V.tensor_tensor(t[:, j, :], slots(r, j), cand[:, j, :], ALU.subtract))
                        link(V.tensor_tensor(t[:, j, :], t[:, j, :], rz[:, j, D:2 * D], ALU.mult))
                        V.tensor_tensor(s[:, j, :], t[:, j, :], cand[:, j, :], ALU.add).then_inc(s_done.sem, 1)
                dve.wait_ge(saved.sem, saved.at(i, 0))
                dve.wait_ge(s_done.sem, s_done.at(i, N))
                link(V.tensor_tensor(t[:, :, :], x4[:, :, :], s[:, :, :], ALU.add))
                layer_norms(dve, nc, vlink, i, [t[:, j, :] for j in range(GB)], stats, [x5[:, j, :] for j in range(GB)], x5_done)
            assert vlink.seen == vlink.per, vlink.seen

DFF = 1024
FT = DFF // 128
NT = B * T // 128
CHUNKS = [(0, 4), (4, 4), (8, 4), (12, 2)]
TOP = 24
HASH_INPUTS = ["ident", "W1", "b1", "W2", "L1_ffn_b2", "count_to", "eights", "expert_no", "expert_before"]


def hashed_phase(nc, d, own):
    NP = 2
    ctx = ExitStack()
    with ctx:
        def sb(name, shape, dt=F32):
            return ctx.enter_context(nc.sbuf_tensor("e_" + name, shape, dt))

        def sem(name, per, unit=1, early=False):
            return Steps(own("e_" + name, early), per, unit, early)

        ident = sb("ident", [128, 128])
        count_to = sb("count_to", [128, TOP])
        eights = sb("eights", [128, TOP // 4])
        expert_no = sb("expert_no", [128, E])
        expert_before = sb("expert_before", [128, E])
        b2 = sb("b2", [E, D])
        x = sb("x", [128, NT, D])
        xt = sb("xt", [128, KC, NT, 128])
        acc = sb("acc", [128, NT, D])
        h1 = sb("h1", [128, NT])
        h2 = sb("h2", [128, NT])
        h3 = sb("h3", [128, NT])
        cmp = sb("cmp", [128, NT, TOP])
        eq1 = sb("eq1", [128, NT, E])
        share = sb("share", [128, NT, E])
        share_t = sb("share_t", [E, NT, 128])
        w1 = [sb(f"w1_{n}", [128, KC, DFF]) for n in range(NP)]
        w2 = [sb(f"w2_{n}", [128, FT, D]) for n in range(NP)]
        b1 = [sb(f"b1_{n}", [128, FT]) for n in range(NP)]
        hid = [sb(f"hid{n}", [128, FT, 512]) for n in range(2)]
        stats = sb("stats", [128, NT, 10])
        up = [ctx.enter_context(nc.psum_tensor(f"e_up{n}", [128, 512], F32)) for n in range(4)]
        down = [ctx.enter_context(nc.psum_tensor(f"e_down{n}", [128, 512], F32)) for n in range(4)]

        NC = len(CHUNKS)
        first = sem("first", 1)
        loaded = [sem(f"loaded{n}", 3, 16) for n in range(NP)]
        turned = sem("turned", 1)
        xt_sb = sem("xt_sb", 1)
        shares = sem("shares", 1)
        share_turned = sem("share_turned", 1)
        share_sb = sem("share_sb", 1)
        bias_done = sem("bias_done", 1)
        acc0 = sem("acc0", 1)
        up_done = sem("up_done", NP * NC * FT)
        relu_done = sem("relu_done", NP * NC * FT, early=True)
        down_done = sem("down_done", NP * NT, early=True)
        added = sem("added", NP * NT, early=True)
        normed = sem("normed", NT)
        stored = sem("stored", 1, 16)
        vlink = sem("vlink", 1)
        block = ctx.enter_context(nc.Block())
        loads = [(x[:, :, :], d["s_x5_by_tile"]), (ident[:, :], d["ident"]), (count_to[:, :], d["count_to"]), (eights[:, :], d["eights"]),
                 (expert_no[:, :], d["expert_no"]), (expert_before[:, :], d["expert_before"]), (b2[:, :], d["L1_ffn_b2"])]

        @block.sync
        def _(sp):
            for dst, src in loads:
                sp.dma_start(dst, src).then_inc(first.sem, 16)

            def load(e, n):
                for dst, src in ((w1[n][:, :, :], d["W1"][e]), (w2[n][:, :, :], d["W2"][e]), (b1[n][:, :], d["b1"][e])):
                    sp.dma_start(dst, src).then_inc(loaded[n].sem, 16)

            for n in range(NP):
                load(n, n)
            with sp.Fori(0, E // NP - 1) as i:
                for n in range(NP):
                    sp.wait_ge(down_done.sem, down_done.at(i, (n + 1) * NT))
                    load(i * NP + (NP + n), n)
            for t in range(NT):
                sp.wait_ge(normed.sem, t + 1)
                sp.dma_start(d["out_by_tile"][:, t, :], x[:, t, :]).then_inc(stored.sem, 16)
            sp.wait_ge(stored.sem, 16 * NT)

        @block.tensor
        def _(pe):
            mm = nc.tensor.matmul
            pe.wait_ge(first.sem, 16 * len(loads))
            for t in range(NT):
                for kc in range(KC):
                    k = t * KC + kc
                    if k % 4 == 0 and k >= 16:
                        pe.wait_ge(xt_sb.sem, k // 4 - 3)
                    last = nc.tensor.transpose(up[k // 4 % 4][:, (k % 4) * 128:(k % 4 + 1) * 128], x[:, t, kc * 128:(kc + 1) * 128], ident[:, :])
                    if k % 4 == 3:
                        last.then_inc(turned.sem, 1)
            pe.wait_ge(shares.sem, 1)
            for t in range(NT):
                if t % 4 == 0:
                    last = None
                last = nc.tensor.transpose(down[t // 4][0:E, (t % 4) * 128:(t % 4 + 1) * 128], share[:, t, :], ident[:, :])
            last.then_inc(share_turned.sem, 1)
            pe.wait_ge(share_sb.sem, 1)
            pe.wait_ge(xt_sb.sem, NT * KC // 4)
            for t in range(NT):
                if t >= 4:
                    pe.wait_ge(acc0.sem, t - 3)
                mm(down[t % 4][:, 0:D], share_t[:, t, :], b2[:, :], start=True, stop=True).then_inc(bias_done.sem, 1)
            pe.wait_ge(acc0.sem, NT)

            with pe.Fori(0, E // NP) as i:
                for n in range(NP):
                    pe.wait_ge(loaded[n].sem, loaded[n].at(i, 3))

                    def rise(c):
                        t0, tiles = CHUNKS[c]
                        for f in range(FT):
                            k = (n * NC + c) * FT + f
                            pe.wait_ge(relu_done.sem, relu_done.at(i, max(k - 3, 0)))
                            for kc in range(KC):
                                last = mm(up[k % 4][:, 0:tiles * 128], w1[n][:, kc, f * 128:(f + 1) * 128],
                                          xt[:, kc, t0:t0 + tiles, :].rearrange("p t c -> p (t c)"), start=kc == 0, stop=kc == KC - 1)
                            last.then_inc(up_done.sem, 1)

                    def fall(c):
                        t0, tiles = CHUNKS[c]
                        pe.wait_ge(relu_done.sem, relu_done.at(i, (n * NC + c + 1) * FT))
                        for t in range(tiles):
                            k = n * NT + t0 + t
                            pe.wait_ge(added.sem, added.at(i, max(k - 3, 0)))
                            for f in range(FT):
                                last = mm(down[k % 4][:, 0:D], hid[c % 2][:, f, t * 128:(t + 1) * 128], w2[n][:, f, :], start=f == 0, stop=f == FT - 1)
                            last.then_inc(down_done.sem, 1)

                    rise(0)
                    for c in range(1, NC):
                        rise(c)
                        fall(c - 1)
                    fall(NC - 1)

        @block.scalar
        def _(act):
            fn = nc.scalar.activation
            for k in range(NT * KC // 4):
                act.wait_ge(turned.sem, k + 1)
                fn(xt[:, :, 2 * k:2 * k + 2, :], up[k % 4][:, :].rearrange("p (t k c) -> p k t c", t=2, k=KC), ACT.Copy).then_inc(xt_sb.sem, 1)
            act.wait_ge(share_turned.sem, 1)
            for k in range((NT + 3) // 4):
                m = min(4, NT - 4 * k)
                last = fn(share_t[:, 4 * k:4 * k + m, :].rearrange("p t c -> p (t c)"), down[k][0:E, 0:m * 128], ACT.Copy)
            last.then_inc(share_sb.sem, 1)
            with act.Fori(0, E // NP) as i:
                for n in range(NP):
                    for c, (t0, tiles) in enumerate(CHUNKS):
                        before = n * NT + sum(CHUNKS[c - 2]) if c >= 2 else (n - 1) * NT + sum(CHUNKS[c - 2])
                        act.wait_ge(down_done.sem, down_done.at(i, max(before, 0)))
                        for f in range(FT):
                            k = (n * NC + c) * FT + f
                            act.wait_ge(up_done.sem, up_done.at(i, k + 1))
                            fn(hid[c % 2][:, f, 0:tiles * 128], up[k % 4][:, 0:tiles * 128], ACT.Relu, bias=b1[n][:, f:f + 1]).then_inc(relu_done.sem, 1)

        @block.vector
        def _(dve):
            V = nc.vector
            link = lambda ins: vlink.chain(dve, 0, ins)
            dve.wait_ge(first.sem, 16 * len(loads))
            link(V.tensor_tensor(h1[:, :], x[:, :, 0], x[:, :, 1], ALU.add))
            link(V.tensor_scalar(h2[:, :], h1[:, :], -1.0, None, ALU.mult))
            link(V.tensor_tensor(h2[:, :], h1[:, :], h2[:, :], ALU.max))
            link(V.tensor_tensor(cmp[:, :, :], h2[:, :].unsqueeze(2).broadcast_to([128, NT, TOP]), count_to[:, :].unsqueeze(1).broadcast_to([128, NT, TOP]), ALU.is_ge))
            link(V.tensor_reduce(h3[:, :], cmp[:, :, :], AX.X, ALU.add))
            link(V.tensor_scalar(h1[:, :], h1[:, :], 0.0, None, ALU.is_lt))
            link(V.tensor_scalar(h1[:, :], h1[:, :], -2.0, 1.0, ALU.mult, ALU.add))
            link(V.tensor_tensor(h1[:, :], h1[:, :], h3[:, :], ALU.mult))
            link(V.tensor_scalar(h1[:, :], h1[:, :], float(TOP), None, ALU.add))
            link(V.tensor_tensor(cmp[:, :, 0:TOP // 4], h1[:, :].unsqueeze(2).broadcast_to([128, NT, TOP // 4]), eights[:, :].unsqueeze(1).broadcast_to([128, NT, TOP // 4]), ALU.is_ge))
            link(V.tensor_reduce(h3[:, :], cmp[:, :, 0:TOP // 4], AX.X, ALU.add))
            link(V.scalar_tensor_tensor(h1[:, :], h3[:, :], -8.0, h1[:, :], ALU.mult, ALU.add))
            of_h = h1[:, :].unsqueeze(2).broadcast_to([128, NT, E])
            V.tensor_tensor(eq1[:, :, :], of_h, expert_no[:, :].unsqueeze(1).broadcast_to([128, NT, E]), ALU.is_equal)
            link(V.tensor_tensor(share[:, :, :], of_h, expert_before[:, :].unsqueeze(1).broadcast_to([128, NT, E]), ALU.is_equal))
            link(V.tensor_tensor(share[:, :, :], share[:, :, :], eq1[:, :, :], ALU.add))
            V.tensor_scalar(share[:, :, :], share[:, :, :], 0.5, None, ALU.mult).then_inc(shares.sem, 1)
            for t in range(NT):
                dve.wait_ge(bias_done.sem, t + 1)
                V.tensor_tensor(acc[:, t, :], down[t % 4][:, 0:D], x[:, t, :], ALU.add).then_inc(acc0.sem, 1)
            dve.wait_ge(acc0.sem, NT)
            with dve.Fori(0, E // NP) as i:
                for n in range(NP):
                    for t in range(NT):
                        k = n * NT + t
                        dve.wait_ge(down_done.sem, down_done.at(i, k + 1))
                        dve.wait_ge(added.sem, added.at(i, max(k - NT + 1, 0)))
                        V.scalar_tensor_tensor(acc[:, t, :], down[k % 4][:, 0:D], share[:, t, bass.ds(i * NP + n, 1)], acc[:, t, :],
                                               ALU.mult, ALU.add).then_inc(added.sem, 1)
            dve.wait_ge(added.sem, added.at(E // NP, 0))
            layer_norms(dve, nc, vlink, 0, [acc[:, t, :] for t in range(NT)], stats, [x[:, t, :] for t in range(NT)], normed)


def _constants():
    import numpy as np

    inv = (1.0 / 10000.0 ** (np.arange(0, DH, 2, dtype=np.float32) / DH)).astype(np.float32)
    ang = np.arange(T, dtype=np.float32)[:, None] * inv[None, :]
    s = np.sin(ang)
    c = {
        "cos": np.concatenate([np.cos(ang)] * 2, axis=1), "sin": np.concatenate([-s, s], axis=1),
        "ident": np.eye(128), "earlier": np.triu(np.ones((T, T)), 1), "ones": np.ones((T, T)),
        "count_to": np.tile(np.arange(1, TOP + 1), (128, 1)), "eights": np.tile(np.arange(8, 2 * TOP + 1, 8), (128, 1)),
        "expert_no": np.tile(np.arange(E), (128, 1)), "expert_before": np.tile((np.arange(E) - 1) % E, (128, 1)),
        "rev": np.tile(np.arange(E, 0, -1), (T, 1)), "slot_no": np.tile(np.arange(CAP), (T, 1)),
        "causal": np.triu(np.full((T, T), NEG), 1), "row_of": np.arange(XD)[:, None, None] - RANK == np.arange(2 * NST)[None, :, None] + np.zeros((1, 1, 128)),
        "maskrow": (np.arange(128) % PAD == DH)[None, :],
    }
    return {k: np.ascontiguousarray(v, dtype=np.float32) for k, v in c.items()}


def _layouts(a):
    import numpy as np

    def chunks(w):
        return w.reshape(-1, 128, w.shape[1]).transpose(1, 0, 2)

    def pad_heads(w):
        out = np.zeros(w.shape[:-1] + (HEADS, PAD), w.dtype)
        out[..., :DH] = w.reshape(w.shape[:-1] + (HEADS, DH))
        return out

    def pad_rows(w):
        out = np.zeros((HEADS, PAD, w.shape[1]), w.dtype)
        out[:, :DH] = w.reshape(HEADS, DH, -1)
        return out.reshape(HG, 128, -1).transpose(1, 0, 2)

    def columns(v):
        return v.reshape(-1, 128).T

    rows = lambda v: v.reshape(DT, 128, -1).transpose(1, 0, 2)
    bq = pad_heads(a["L0_xattn_bq"])
    bq[:, DH] = 1.0
    out = dict(a)
    out.update(
        xt=a["x"].reshape(B, T, KC, 128).transpose(0, 3, 2, 1), ctxt=a["ctx_1024"].reshape(B, S2, KC, 128).transpose(0, 3, 2, 1),
        mask=np.ascontiguousarray(a["mask_BxS2_bk0"]).reshape(-1).view(np.int32),
        wqkv=chunks(a["L0_attn_qkv_w"].T), wproj=pad_rows(a["L0_attn_proj_w"].T),
        wqx=chunks(pad_heads(a["L0_xattn_Wq"].T).reshape(D, -1)), bqx=columns(bq.reshape(-1)),
        wkx=chunks(pad_heads(a["L0_xattn_Wk"].T).reshape(D, -1)), bkx=columns(pad_heads(a["L0_xattn_bk"]).reshape(-1)),
        wvx=chunks(a["L0_xattn_Wv"].T), wox=pad_rows(a["L0_xattn_Wo"].T), router=chunks(a["L0_ffn_router_w"]),
        w0=a["L0_ffn_w0_kernel"].reshape(E, KC, 128, HID).transpose(0, 2, 1, 3), w1=a["L0_ffn_w1_kernel"].reshape(E, KC, 128, HID).transpose(0, 2, 1, 3),
        wo=a["L0_ffn_wo_kernel"].reshape(E, HT, HP, D).transpose(0, 2, 1, 3),
        win=chunks(a["L1_attn_W_in"].T), convw=rows(a["L1_attn_conv_w"].reshape(DIN, TAPS)), convb=columns(a["L1_attn_conv_b"]),
        wx=chunks(a["L1_attn_W_x"].T), wdt=a["L1_attn_W_dt"].T, bdt=columns(a["L1_attn_b_dt"]), alog=rows(a["L1_attn_A_log"]),
        ctx_rows=a["ctx_1024"].reshape(B, KT, KP, D).transpose(0, 2, 1, 3), wk=chunks(a["L1_xattn_Wk"].T), wv=chunks(a["L1_xattn_Wv"].T),
        wq=chunks(a["L1_xattn_Wq"].T), wih=chunks(a["L1_xattn_gru_wih"].T), whh=chunks(a["L1_xattn_gru_whh"].T),
        snorm=columns(a["L1_xattn_slot_norm_w"]), inorm=columns(a["L1_xattn_input_norm_w"]),
        W1=a["L1_ffn_W1"].reshape(E, KC, 128, DFF).transpose(0, 2, 1, 3), W2=a["L1_ffn_W2"].reshape(E, FT, 128, D).transpose(0, 2, 1, 3),
        b1=a["L1_ffn_b1"].reshape(E, FT, 128).transpose(0, 2, 1),
        dp=columns(a["L1_attn_Dp"]), wout=chunks(a["L1_attn_W_out"].T),
    )
    out.update(_constants())
    return out


def _views(d):
    if "mask" in d:
        d["mask"] = d["mask"].bitcast(U8).rearrange("(b o s) -> b o s", o=1, s=S2)
    if "s_xe" in d:
        d["s_xe_by_expert"] = d["s_xe"].rearrange("g p k (e c) -> e k p g c", e=E)
    if "s_eo" in d:
        d["s_eo_by_expert"] = d["s_eo"].rearrange("(s g) (e c) d -> e g c s d", g=2, e=E)
        d["s_eo_by_group"] = d["s_eo"].rearrange("g (s p) d -> g p s d", p=T)
    if "s_x4" in d:
        d["s_x4_by_four"] = d["s_x4"].rearrange("(i b) t d -> i t b d", b=QB)
    if "s_x5" in d:
        d["s_x5_by_two"] = d["s_x5"].rearrange("(i b) t d -> i t b d", b=GB)
        d["s_x5_by_tile"] = d["s_x5"].rearrange("b t d -> (b t) d").rearrange("(n p) d -> p n d", p=128)
    if "out" in d:
        d["out_by_tile"] = d["out"].rearrange("b t d -> (b t) d").rearrange("(n p) d -> p n d", p=128)


_A = ["xt", "x", "ctxt", "mask", "wqkv", "L0_attn_qkv_b", "wproj", "L0_attn_proj_b", "wqx", "bqx", "wkx", "bkx", "wvx", "L0_xattn_bv",
      "wox", "L0_xattn_bo", "router", "cos", "sin", "ident", "earlier", "ones", "rev", "slot_no", "causal", "maskrow"]
_B = ["w0", "w1", "wo"]
_C = ["win", "convw", "convb", "wx", "wdt", "bdt", "alog", "dp", "wout", "row_of"]
_INS = list(dict.fromkeys(_A + _B + _C + SLOT_INPUTS + HASH_INPUTS))
_SCRATCH = {"s_x2": (G, T, GB, D), "s_xe": (G, 128, KC, SL), "s_ct": (G, T, GB, ST, T), "s_eo": (G, SL, D), "s_x4": (B, T, D), "s_x5": (B, T, D)}


def kernel(**inputs):
    import numpy as np
    import concourse.bacc as bacc
    from concourse.bass_utils import run_bass_kernel_spmd

    nc = bacc.Bacc("TRN2", target_bir_lowering=False, num_devices=1)
    laid = _layouts({k: np.asarray(v) for k, v in inputs.items()})
    arrays = {f"in_{n}": np.ascontiguousarray(laid[n]) for n in _INS}
    d = {n: nc.dram_tensor(f"in_{n}", arrays[f"in_{n}"].shape, mybir.dt.from_np(arrays[f"in_{n}"].dtype), kind="ExternalInput").ap() for n in _INS}
    for n, shape in _SCRATCH.items():
        d[n] = nc.dram_tensor(n, shape, F32, kind="Internal").ap()
    d["out"] = nc.dram_tensor("out", (B, T, D), F32, kind="ExternalOutput").ap()
    _views(d)
    for phase in (attention_phase, expert_phase, mixer_phase, slot_phase, hashed_phase):
        run_phase(nc, phase, d)
    return run_bass_kernel_spmd(nc, [arrays], core_ids=[0]).results[0]["out"]
```

```python
import concourse.bass as bass
from concourse import mybir
from contextlib import ExitStack

F32 = mybir.dt.float32
BF16 = mybir.dt.bfloat16
U8 = mybir.dt.uint8
I32 = mybir.dt.int32
ALU = mybir.AluOpType
ACT = mybir.ActivationFunctionType
AX = mybir.AxisListType

B, T, D = 16, 112, 256
S2 = 375
KC = D // 128
HEADS, DH, PAD = 16, 16, 32
HG = HEADS * PAD // 128
KT, KP = 3, S2 // 3
G, GB = 8, 2
E = 8
CAP = 56
SL = E * CAP
ST = SL // T
HID = 1368
HT, HP = 12, HID // 12
NEG = -1.0e30
LN_EPS = 1e-5


class Steps:

    def __init__(self, sem, per, unit=1, early=False):
        self.sem, self.per, self.unit, self.start, self.seen = sem, per, unit, int(early), 0

    def at(self, i, k):
        assert k * self.unit + self.start > 0 or isinstance(i, int), self.sem.name
        return i * (self.per * self.unit) + (k * self.unit + self.start)

    def chain(self, eng, i, instruction):
        self.seen += 1
        instruction.then_inc(self.sem, 1)
        eng.wait_ge(self.sem, self.at(i, self.seen))


def run_phase(nc, phase, d):
    used = []

    def own(name, early):
        used.append(nc.alloc_semaphore(name=name))
        if early:
            nc.sync.sem_inc(used[-1], int(early))
        return used[-1]

    phase(nc, d, own)
    nc.clear_and_free_semaphores(used)
    nc.all_engine_barrier()


def inverse_root(dve, nc, links, i, value, root, tmp):
    V = nc.vector
    links.chain(dve, i, V.tensor_scalar(root.bitcast(I32), value.bitcast(I32), -0.5, float(0x5F3759DF), ALU.mult, ALU.add))
    k = 1.0
    for step in range(3):
        if value.shape[-1] == 1:
            links.chain(dve, i, V.scalar_tensor_tensor(tmp, root, value, root, ALU.mult, ALU.mult))
        else:
            links.chain(dve, i, V.tensor_tensor(tmp, root, root, ALU.mult))
            links.chain(dve, i, V.tensor_tensor(tmp, tmp, value, ALU.mult))
        if step < 2:
            links.chain(dve, i, V.scalar_tensor_tensor(root, tmp, 3 * k * k, root, ALU.subtract, ALU.mult))
            k = -2 * k ** 3
    links.chain(dve, i, V.tensor_scalar(tmp, tmp, -0.5 / k ** 3, 1.5 / k, ALU.mult, ALU.add))
    links.chain(dve, i, V.tensor_tensor(root, root, tmp, ALU.mult))


def layer_norms(dve, nc, links, i, rows, stats, outs, done):
    for n, t in enumerate(rows):
        last = nc.vector.bn_stats(stats[:, n, 0:6], t)
        if n < len(rows) - 1:
            last.then_inc(links.sem, 1)
    links.seen += len(rows) - 1
    links.chain(dve, i, last)
    nc.vector.memset(stats[:, 0, 9:10], 0.0)
    for n in range(len(rows)):
        last = nc.vector.bn_aggr(stats[:, n, 6:8], stats[:, n, 0:6])
        if n < len(rows) - 1:
            last.then_inc(links.sem, 1)
    links.seen += len(rows) - 1
    links.chain(dve, i, last)
    n = len(rows)
    links.chain(dve, i, nc.vector.tensor_scalar(stats[:, 0:n, 7], stats[:, 0:n, 7], LN_EPS, None, ALU.add))
    inverse_root(dve, nc, links, i, stats[:, 0:n, 7], stats[:, 0:n, 8], stats[:, 0:n, 9])
    for n, (t, out) in enumerate(zip(rows, outs)):
        nc.vector.tensor_scalar(out, t, stats[:, n, 6:7], stats[:, n, 8:9], ALU.subtract, ALU.mult).then_inc(done.sem, 1)


def attention_phase(nc, d, own):
    ctx = ExitStack()
    with ctx:
        def sb(name, shape, dt=F32):
            return ctx.enter_context(nc.sbuf_tensor("a_" + name, shape, dt))

        def sem(name, per, unit=1, early=False):
            return Steps(own("a_" + name, early), per, unit, early)

        wqkv = sb("wqkv", [128, KC, 3 * D])
        bqkv = sb("bqkv", [T, 3 * D])
        wproj = sb("wproj", [128, HG, D])
        bproj = sb("bproj", [T, D])
        wqx = sb("wqx", [128, KC, HG * 128])
        bqx = sb("bqx", [128, HG])
        wkx = sb("wkx", [128, KC, HG * 128])
        bkx = sb("bkx", [128, HG])
        wvx = sb("wvx", [128, KC, D])
        bvx = sb("bvx", [KP, D])
        wox = sb("wox", [128, HG, D])
        box = sb("box", [T, D])
        router = sb("router", [128, KC, E])
        cos = sb("cos", [T, DH])
        sin = sb("sin", [T, DH])
        ident = sb("ident", [128, 128])
        earlier = sb("earlier", [T, T])
        ones = sb("ones", [T, T])
        rev = sb("rev", [T, E])
        slot_no = sb("slot_no", [T, CAP])
        ident_f = sb("ident_f", [T, T])
        causal_f = sb("causal_f", [T, T])
        maskrow_f = sb("maskrow_f", [1, 128])
        identb = sb("identb", [T, T], BF16)
        causalb = sb("causalb", [T, 4, T], BF16)
        maskrowb = sb("maskrowb", [1, 128], BF16)

        xt = sb("xt", [128, GB, KC, T])
        x = sb("x", [T, GB, D])
        ctxt = sb("ctxt", [128, GB, KC, S2])
        mask8 = sb("mask8", [1, GB, S2], U8)
        maskb = sb("maskb", [1, GB, S2], BF16)

        qkb = sb("qkb", [T, 2 * D])
        rot1 = sb("rot1", [T, 2 * D])
        rot2 = sb("rot2", [T, 2 * D])
        qkp = sb("qkp", [T, 2 * HEADS, PAD])
        vp = sb("vp", [T, HEADS, PAD])
        qt = sb("qt", [128, HG, T])
        kt = sb("kt", [128, HG, T])
        rowmax = sb("rowmax", [T, HEADS])
        negmax = sb("negmax", [T, HEADS])
        rowsum = sb("rowsum", [T, HEADS])
        rowinv = sb("rowinv", [T, HEADS])
        inv_wide = sb("inv_wide", [T, HEADS, PAD])
        p = sb("p", [T, 2, 4, T])
        pt = sb("pt", [T, 2, 4, T])
        inv_t = sb("inv_t", [128, HG, T])
        ot = sb("ot", [128, HG, T])
        xb = sb("xb", [T, D])
        t = sb("t", [T, D])
        stats = sb("stats", [T, 1, 10])
        x1 = sb("x1", [T, D])
        x1t = sb("x1t", [128, KC, T])
        ktx = sb("ktx", [128, HG, S2])
        vx = sb("vx", [KP, KT, HEADS, PAD])
        px = sb("px", [T, 4, S2])
        ptx = sb("ptx", [KP, 2, KT, T])
        x2 = sb("x2", [T, GB, D])
        x2t = sb("x2t", [128, GB, KC, T])
        lg = sb("lg", [T, GB, E])
        raw = sb("raw", [T, GB, E])
        tmp = sb("tmp", [T, GB, E])
        cand = sb("cand", [T, GB, E])
        pick = sb("pick", [T, GB, 2, E])
        kept = sb("kept", [T, GB, 2, E])
        pos = sb("pos", [T, GB, 2, E])
        s1 = sb("s1", [T, 8, GB])
        gate = sb("gate", [T, GB, 2])
        place = sb("place", [T, GB, 2])
        onehot = sb("onehot", [T, GB, 2, CAP])
        comb = sb("comb", [T, GB, E, CAP])
        comb2 = sb("comb2", [T, GB, E, CAP])
        disp = sb("disp", [T, GB, SL])
        xe = sb("xe", [128, KC, SL])
        combt = sb("combt", [T, GB, ST, T])

        def ps(name, shape):
            return ctx.enter_context(nc.psum_tensor("a_" + name, shape, F32))

        score = [ps(f"score{n}", [128, 512]) for n in range(4)]
        trans = [ps(f"trans{n}", [128, 512]) for n in range(2)]
        outt = ps("outt", [128, 512])
        misc = ps("misc", [128, 512])

        weights = sem("weights", 1)
        ready = sem("ready", 1)
        in_x = [sem(f"in_x{j}", 2, 16) for j in range(GB)]
        in_ctx = [sem(f"in_ctx{j}", 2, 16) for j in range(GB)]
        x_done = sem("x_done", GB, early=True)
        mask_done = sem("mask_done", GB, early=True)
        qkv = sem("qkv", GB, early=True)
        roped = sem("roped", GB)
        qk_t = sem("qk_t", GB)
        qk_sb = sem("qk_sb", GB)
        s_done = sem("s_done", GB * HG)
        m_done = sem("m_done", GB * HG)
        p_done = sem("p_done", GB * HG)
        pt_done = sem("pt_done", GB * HG)
        pt_sb = sem("pt_sb", GB * HG)
        o_done = sem("o_done", GB * 2)
        inv_done = sem("inv_done", GB * 2)
        invt_done = sem("invt_done", GB * 2)
        invt_sb = sem("invt_sb", GB * 2)
        o_sb = sem("o_sb", GB * 2, early=True)
        proj = sem("proj", GB * 2)
        x1_done = sem("x1_done", GB)
        x1t_done = sem("x1t_done", GB)
        x1t_sb = sem("x1t_sb", GB)
        kx = sem("kx", GB * HG)
        kx_sb = sem("kx_sb", GB * HG)
        vxp = sem("vxp", GB * KT, early=True)
        vx_sb = sem("vx_sb", GB * KT, early=True)
        qx = sem("qx", GB)
        qx_sb = sem("qx_sb", GB)
        sx = sem("sx", GB * HEADS)
        mx = sem("mx", GB * HEADS // 2)
        pxd = sem("pxd", GB * HEADS, early=True)
        ptxd = sem("ptxd", GB * HEADS)
        ptx_sb = sem("ptx_sb", GB * HEADS)
        x2_done = sem("x2_done", GB)
        x2t_done = sem("x2t_done", 1)
        x2t_sb = sem("x2t_sb", 1)
        lg_done = sem("lg_done", 1)
        lg_sub = sem("lg_sub", 1)
        lg_exp = sem("lg_exp", 1)
        picked = sem("picked", 1)
        counted = sem("counted", 1)
        kept1 = sem("kept1", 1)
        total1 = sem("total1", 1)
        routed = sem("routed", 1)
        xe_done = sem("xe_done", 2)
        xe_sb = sem("xe_sb", 2)
        ct_done = sem("ct_done", GB)
        ct_sb = sem("ct_sb", GB)
        stored = sem("stored", 3, 16)
        saved = sem("saved", 1, early=True)
        vlink = sem("vlink", 111)
        block = ctx.enter_context(nc.Block())

        def column(h):
            return 4 * (h % 4) + h // 4

        loads = [
            (wqkv[:, :, :], d["wqkv"]), (bqkv[:, :], d["L0_attn_qkv_b"].partition_broadcast(T)),
            (wproj[:, :, :], d["wproj"]), (bproj[:, :], d["L0_attn_proj_b"].partition_broadcast(T)),
            (wqx[:, :, :], d["wqx"]), (bqx[:, :], d["bqx"]), (wkx[:, :, :], d["wkx"]), (bkx[:, :], d["bkx"]),
            (wvx[:, :, :], d["wvx"]), (bvx[:, :], d["L0_xattn_bv"].partition_broadcast(KP)),
            (wox[:, :, :], d["wox"]), (box[:, :], d["L0_xattn_bo"].partition_broadcast(T)),
            (router[:, :, :], d["router"]), (cos[:, :], d["cos"]), (sin[:, :], d["sin"]),
            (ident[:, :], d["ident"]), (earlier[:, :], d["earlier"]), (ones[:, :], d["ones"]),
            (rev[:, :], d["rev"]), (slot_no[:, :], d["slot_no"]), (ident_f[:, :], d["ident"][0:T, 0:T]),
            (causal_f[:, :], d["causal"]), (maskrow_f[:, :], d["maskrow"]),
        ]

        @block.sync
        def _(sp):
            for dst, src in loads:
                sp.dma_start(dst, src).then_inc(weights.sem, 16)
            with sp.Fori(0, G) as i:
                for j in range(GB):
                    sp.wait_ge(qkv.sem, qkv.at(i, 0))
                    sp.wait_ge(x_done.sem, x_done.at(i, 0))
                    sp.dma_start(xt[:, j, :, :], d["xt"][i * GB + j]).then_inc(in_x[j].sem, 16)
                    sp.dma_start(x[:, j, :], d["x"][i * GB + j]).then_inc(in_x[j].sem, 16)
                    sp.wait_ge(vxp.sem, vxp.at(i, 0))
                    sp.wait_ge(mask_done.sem, mask_done.at(i, 0))
                    sp.dma_start(ctxt[:, j, :, :], d["ctxt"][i * GB + j]).then_inc(in_ctx[j].sem, 16)
                    sp.dma_start(mask8[:, j, :], d["mask"][i * GB + j]).then_inc(in_ctx[j].sem, 16)

        @block.gpsimd
        def _(pool):
            with pool.Fori(0, G) as i:
                pool.wait_ge(x2_done.sem, x2_done.at(i, GB))
                pool.dma_start(d["s_x2"][i], x2[:, :, :]).then_inc(stored.sem, 16)
                pool.wait_ge(xe_sb.sem, xe_sb.at(i, 2))
                pool.dma_start(d["s_xe"][i], xe[:, :, :]).then_inc(stored.sem, 16)
                pool.wait_ge(ct_sb.sem, ct_sb.at(i, GB))
                pool.dma_start(d["s_ct"][i], combt[:, :, :, :]).then_inc(stored.sem, 16)
                pool.wait_ge(stored.sem, stored.at(i, 3))
                pool.sem_inc(saved.sem, 1)

        @block.tensor
        def _(pe):
            pe.wait_ge(weights.sem, 16 * len(loads))
            pe.wait_ge(ready.sem, 1)
            mm = nc.tensor.matmul
            with pe.Fori(0, G) as i:
                for j in range(GB):
                    pe.wait_ge(in_x[j].sem, in_x[j].at(i, 2))
                    pe.wait_ge(pxd.sem, pxd.at(i, j * HEADS))
                    for kc in range(KC):
                        mm(score[0][0:T, :], xt[:, j, kc, :], wqkv[:, kc, 0:2 * D], start=kc == 0, stop=kc == KC - 1)
                    for kc in range(KC):
                        last = mm(score[1][0:T, 0:D], xt[:, j, kc, :], wqkv[:, kc, 2 * D:3 * D], start=kc == 0, stop=kc == KC - 1)
                    last.then_inc(qkv.sem, 1)
                    pe.wait_ge(roped.sem, roped.at(i, j + 1))
                    for n in range(2):
                        for hg in range(HG):
                            last = nc.tensor.transpose(
                                score[2 + n][:, hg * T:(hg + 1) * T],
                                qkp[:, n * HEADS + 4 * hg:n * HEADS + 4 * hg + 4, :].rearrange("p h d -> p (h d)"), ident[0:T, 0:T])
                    last.then_inc(qk_t.sem, 1)

                    def scores(r):
                        if r == 0:
                            pe.wait_ge(qk_sb.sem, qk_sb.at(i, j + 1))
                        mm(score[r][0:T, 0:4 * T], identb[:, :], causalb[:, :, :].rearrange("p h k -> p (h k)"), start=True, stop=False)
                        q = 32 * r
                        for hg in range(HG):
                            last = mm(score[r][0:T, hg * T:(hg + 1) * T], qt[q:q + 32, hg, :], kt[q:q + 32, hg, :], start=False, stop=hg == HG - 1, tile_position=(q, 0))
                        last.then_inc(s_done.sem, 1)

                    def turn(r):
                        pe.wait_ge(p_done.sem, p_done.at(i, j * 4 + r + 1))
                        for hg in range(HG):
                            last = nc.tensor.transpose(trans[r % 2][0:T, hg * T:(hg + 1) * T], p[:, r % 2, hg, :], ident[0:T, 0:T])
                        last.then_inc(pt_done.sem, 1)

                    def values(r):
                        pe.wait_ge(pt_sb.sem, pt_sb.at(i, j * 4 + r + 1))
                        for hg in range(HG):
                            last = mm(outt[32 * r:32 * r + 32, hg * T:(hg + 1) * T], vp[:, 4 * hg + r, :], pt[:, r % 2, hg, :],
                                      start=True, stop=True, tile_position=(0, 32 * r))
                        if r == 3:
                            last.then_inc(o_done.sem, 1)

                    pe.wait_ge(o_sb.sem, o_sb.at(i, 2 * j))
                    scores(0)
                    scores(1)
                    for r in range(4):
                        turn(r)
                        if r + 2 < 4:
                            scores(r + 2)
                        values(r)

                    def finish(n, w):
                        pe.wait_ge(inv_done.sem, inv_done.at(i, 2 * j + n + 1))
                        for hg in range(HG):
                            last = nc.tensor.transpose(misc[:, hg * T:(hg + 1) * T],
                                                       inv_wide[:, 4 * hg:4 * hg + 4, :].rearrange("p h d -> p (h d)"), ident[0:T, 0:T])
                        last.then_inc(invt_done.sem, 1)
                        pe.wait_ge(o_sb.sem, o_sb.at(i, 2 * j + n + 1))
                        for hg in range(HG):
                            last = mm(misc[0:T, 0:D], ot[:, hg, :], w[:, hg, :], start=hg == 0, stop=hg == HG - 1)
                        last.then_inc(proj.sem, 1)

                    finish(0, wproj)

                    pe.wait_ge(in_ctx[j].sem, in_ctx[j].at(i, 2))
                    pe.wait_ge(mask_done.sem, mask_done.at(i, j + 1))
                    for hg in range(HG):
                        for kc in range(KC):
                            mm(score[hg][:, 0:S2], wkx[:, kc, hg * 128:(hg + 1) * 128], ctxt[:, j, kc, :], start=kc == 0, stop=False)
                        mm(score[hg][:, 0:S2], maskrowb[:, :], maskb[:, j, :], start=False, stop=True).then_inc(kx.sem, 1)
                    for k in range(KT):
                        pe.wait_ge(vx_sb.sem, vx_sb.at(i, max(j * KT + k - 1, 0)))
                        for kc in range(KC):
                            last = mm(trans[k % 2][0:KP, 0:D], ctxt[:, j, kc, k * KP:(k + 1) * KP], wvx[:, kc, :], start=kc == 0, stop=kc == KC - 1)
                        last.then_inc(vxp.sem, 1)

                    pe.wait_ge(x1_done.sem, x1_done.at(i, j + 1))
                    pe.wait_ge(vx_sb.sem, vx_sb.at(i, j * KT + KT))
                    for kc in range(KC):
                        last = nc.tensor.transpose(trans[0][:, kc * T:(kc + 1) * T], x1[:, kc * 128:(kc + 1) * 128], ident[0:T, 0:T])
                    last.then_inc(x1t_done.sem, 1)
                    pe.wait_ge(x1t_sb.sem, x1t_sb.at(i, j + 1))
                    for hg in range(HG):
                        for kc in range(KC):
                            last = mm(trans[1][:, hg * T:(hg + 1) * T], wqx[:, kc, hg * 128:(hg + 1) * 128], x1t[:, kc, :], start=kc == 0, stop=kc == KC - 1)
                    last.then_inc(qx.sem, 1)

                    def xscore(h):
                        if h == 0:
                            pe.wait_ge(qx_sb.sem, qx_sb.at(i, j + 1))
                            pe.wait_ge(kx_sb.sem, kx_sb.at(i, j * HG + HG))
                        if h >= 4:
                            pe.wait_ge(pxd.sem, pxd.at(i, j * HEADS + h - 3))
                        q = 32 * (h % 4)
                        mm(score[h % 4][0:T, 0:S2], qt[q:q + 32, h // 4, :], ktx[q:q + 32, h // 4, :], start=True, stop=True,
                           tile_position=(q, 0)).then_inc(sx.sem, 1)

                    def xturn(h):
                        pe.wait_ge(pxd.sem, pxd.at(i, j * HEADS + h + 1))
                        if h >= 2:
                            pe.wait_ge(ptx_sb.sem, ptx_sb.at(i, j * HEADS + h - 1))
                        for k in range(KT):
                            last = nc.tensor.transpose(trans[h % 2][0:KP, k * T:(k + 1) * T], px[:, h % 4, k * KP:(k + 1) * KP], ident[0:T, 0:T])
                        last.then_inc(ptxd.sem, 1)

                    def xvalues(h):
                        pe.wait_ge(ptx_sb.sem, ptx_sb.at(i, j * HEADS + h + 1))
                        for k in range(KT):
                            q = 32 * (h % 4)
                            last = mm(outt[q:q + 32, (h // 4) * T:(h // 4 + 1) * T], vx[:, k, h, :], ptx[:, h % 2, k, :],
                                      start=k == 0, stop=k == KT - 1, tile_position=(0, q))
                        if h == HEADS - 1:
                            last.then_inc(o_done.sem, 1)

                    for h in range(4):
                        xscore(h)
                    for h in range(0, HEADS, 2):
                        xturn(h)
                        xturn(h + 1)
                        if h + 4 < HEADS:
                            xscore(h + 4)
                            xscore(h + 5)
                        xvalues(h)
                        xvalues(h + 1)
                    finish(1, wox)

                pe.wait_ge(x2_done.sem, x2_done.at(i, GB))
                for j in range(GB):
                    for kc in range(KC):
                        last = nc.tensor.transpose(trans[0][:, (j * KC + kc) * T:(j * KC + kc + 1) * T], x2[:, j, kc * 128:(kc + 1) * 128], ident[0:T, 0:T])
                last.then_inc(x2t_done.sem, 1)
                pe.wait_ge(x2t_sb.sem, x2t_sb.at(i, 1))
                for j in range(GB):
                    for kc in range(KC):
                        last = mm(misc[0:T, j * E:(j + 1) * E], x2t[:, j, kc, :], router[:, kc, :], start=kc == 0, stop=kc == KC - 1)
                last.then_inc(lg_done.sem, 1)
                pe.wait_ge(picked.sem, picked.at(i, 1))
                mm(misc[0:T, 0:2 * E], earlier[:, :], pick[:, 0, :, :].rearrange("p c e -> p (c e)"), start=True, stop=True)
                mm(misc[0:T, 2 * E:4 * E], earlier[:, :], pick[:, 1, :, :].rearrange("p c e -> p (c e)"), start=True, stop=False)
                mm(misc[0:T, 2 * E:4 * E], ones[:, :], pick[:, 0, :, :].rearrange("p c e -> p (c e)"), start=False, stop=True).then_inc(counted.sem, 1)
                pe.wait_ge(kept1.sem, kept1.at(i, 1))
                for j in range(GB):
                    last = mm(misc[0:T, 4 * E:5 * E], ones[:, :], kept[:, j, 0, :], start=j == 0, stop=j == GB - 1)
                last.then_inc(total1.sem, 1)
                pe.wait_ge(routed.sem, routed.at(i, 1))
                for fc in range(KC):
                    for j in range(GB):
                        last = mm(score[fc][:, 0:SL], x2[:, j, fc * 128:(fc + 1) * 128], disp[:, j, :], start=j == 0, stop=j == GB - 1)
                    last.then_inc(xe_done.sem, 1)
                for j in range(GB):
                    for s in range(ST):
                        last = nc.tensor.transpose(score[2 + j][0:T, s * T:(s + 1) * T],
                                                   comb[:, j, 2 * s:2 * s + 2, :].rearrange("p e c -> p (e c)"), ident[0:T, 0:T])
                    last.then_inc(ct_done.sem, 1)
                pe.wait_ge(xe_sb.sem, xe_sb.at(i, 2))
                pe.wait_ge(ct_sb.sem, ct_sb.at(i, GB))

        @block.scalar
        def _(act):
            act.wait_ge(weights.sem, 16 * len(loads))
            fn = nc.scalar.activation
            with act.Fori(0, G) as i:
                for j in range(GB):
                    act.wait_ge(qk_t.sem, qk_t.at(i, j + 1))
                    fn(qt[:, :, :].rearrange("p h t -> p (h t)"), score[2][:, 0:HG * T], ACT.Copy)
                    fn(kt[:, :, :].rearrange("p h t -> p (h t)"), score[3][:, 0:HG * T], ACT.Copy).then_inc(qk_sb.sem, 1)
                    for r in range(4):
                        act.wait_ge(m_done.sem, m_done.at(i, j * 4 + r + 1))
                        for hg in range(HG):
                            c = column(4 * hg + r)
                            last = fn(p[:, r % 2, hg, :], score[r][0:T, hg * T:(hg + 1) * T], ACT.Exp, bias=negmax[:, c:c + 1],
                                      scale=0.25, accum_out=rowsum[:, c:c + 1])
                        last.then_inc(p_done.sem, 1)

                    def inverse_sums(n):
                        act.wait_ge(invt_done.sem, invt_done.at(i, 2 * j + n + 1))
                        fn(inv_t[:, :, :].rearrange("p h t -> p (h t)"), misc[:, 0:HG * T], ACT.Copy).then_inc(invt_sb.sem, 1)

                    inverse_sums(0)
                    for hg in range(HG):
                        act.wait_ge(kx.sem, kx.at(i, j * HG + hg + 1))
                        fn(ktx[:, hg, :], score[hg][:, 0:S2], ACT.Identity, bias=bkx[:, hg:hg + 1]).then_inc(kx_sb.sem, 1)
                    act.wait_ge(x1t_done.sem, x1t_done.at(i, j + 1))
                    fn(x1t[:, :, :].rearrange("p c t -> p (c t)"), trans[0][:, 0:KC * T], ACT.Copy).then_inc(x1t_sb.sem, 1)
                    act.wait_ge(qx.sem, qx.at(i, j + 1))
                    for hg in range(HG):
                        last = fn(qt[:, hg, :], trans[1][:, hg * T:(hg + 1) * T], ACT.Identity, bias=bqx[:, hg:hg + 1])
                    last.then_inc(qx_sb.sem, 1)
                    for h in range(HEADS):
                        if h % 2 == 0:
                            act.wait_ge(mx.sem, mx.at(i, (j * HEADS + h) // 2 + 1))
                        if h >= 4:
                            act.wait_ge(ptxd.sem, ptxd.at(i, j * HEADS + h - 3))
                        fn(px[:, h % 4, :], score[h % 4][0:T, 0:S2], ACT.Exp, bias=negmax[:, column(h):column(h) + 1], scale=0.25,
                           accum_out=rowsum[:, column(h):column(h) + 1]).then_inc(pxd.sem, 1)
                    inverse_sums(1)
                act.wait_ge(x2t_done.sem, x2t_done.at(i, 1))
                fn(x2t[:, :, :, :].rearrange("p j c t -> p (j c t)"), trans[0][:, 0:GB * KC * T], ACT.Copy).then_inc(x2t_sb.sem, 1)
                act.wait_ge(lg_sub.sem, lg_sub.at(i, 1))
                fn(raw[:, :, :], lg[:, :, :], ACT.Exp).then_inc(lg_exp.sem, 1)
                act.wait_ge(saved.sem, saved.at(i, 0))
                for fc in range(KC):
                    act.wait_ge(xe_done.sem, xe_done.at(i, fc + 1))
                    fn(xe[:, fc, :], score[fc][:, 0:SL], ACT.Copy).then_inc(xe_sb.sem, 1)
                for j in range(GB):
                    act.wait_ge(ct_done.sem, ct_done.at(i, j + 1))
                    fn(combt[:, j, :, :].rearrange("p s t -> p (s t)"), score[2 + j][0:T, 0:ST * T], ACT.Copy).then_inc(ct_sb.sem, 1)

        @block.vector
        def _(dve):
            V = nc.vector
            dve.wait_ge(weights.sem, 16 * len(loads))
            V.memset(qkp[:, :, :].rearrange("p h d -> p (h d)"), 0.0)
            V.memset(vp[:, :, :].rearrange("p h d -> p (h d)"), 0.0)
            V.memset(vx[:, :, :, :].rearrange("p k h d -> p (k h d)"), 0.0)
            V.tensor_copy(identb[:, :], ident_f[:, :])
            V.tensor_copy(maskrowb[:, :], maskrow_f[:, :])
            V.tensor_copy(causalb[:, :, :], causal_f[:, :].unsqueeze(1).broadcast_to([T, 4, T])).then_inc(ready.sem, 1)
            dve.wait_ge(ready.sem, 1)
            with dve.Fori(0, G) as i:
                link = lambda ins: vlink.chain(dve, i, ins)
                for j in range(GB):
                    dve.wait_ge(in_x[j].sem, in_x[j].at(i, 2))
                    V.tensor_tensor(xb[:, :], x[:, j, :], bproj[:, :], ALU.add).then_inc(x_done.sem, 1)
                    dve.wait_ge(in_ctx[j].sem, in_ctx[j].at(i, 2))
                    V.tensor_scalar(maskb[:, j, :], mask8[:, j, :], NEG, None, ALU.mult).then_inc(mask_done.sem, 1)
                    dve.wait_ge(qkv.sem, qkv.at(i, j + 1))
                    link(V.tensor_tensor(qkb[:, :], score[0][0:T, :], bqkv[:, 0:2 * D], ALU.add))
                    q3 = qkb[:, :].rearrange("p (h d) -> p h d", d=DH)
                    r2 = rot2[:, :].rearrange("p (h d) -> p h d", d=DH)
                    V.tensor_tensor(rot1[:, :].rearrange("p (h d) -> p h d", d=DH), q3, cos[:, :].unsqueeze(1).broadcast_to([T, 2 * HEADS, DH]), ALU.mult)
                    V.tensor_tensor(r2[:, :, 0:8], q3[:, :, 8:16], sin[:, 0:8].unsqueeze(1).broadcast_to([T, 2 * HEADS, 8]), ALU.mult)
                    link(V.tensor_tensor(r2[:, :, 8:16], q3[:, :, 0:8], sin[:, 8:16].unsqueeze(1).broadcast_to([T, 2 * HEADS, 8]), ALU.mult))
                    V.tensor_tensor(qkp[:, :, 0:DH], rot1[:, :].rearrange("p (h d) -> p h d", d=DH), r2, ALU.add)
                    V.tensor_tensor(vp[:, :, 0:DH], score[1][0:T, 0:D].rearrange("p (h d) -> p h d", d=DH),
                                    bqkv[:, 2 * D:3 * D].rearrange("p (h d) -> p h d", d=DH), ALU.add).then_inc(roped.sem, 1)

                    def maxima(hg):
                        dve.wait_ge(s_done.sem, s_done.at(i, j * 4 + hg + 1))
                        link(V.tensor_reduce(rowmax[:, 4 * hg:4 * hg + 4], score[hg][0:T, 0:4 * T].rearrange("p (h k) -> p h k", h=4), AX.X, ALU.max))
                        V.tensor_scalar(negmax[:, 4 * hg:4 * hg + 4], rowmax[:, 4 * hg:4 * hg + 4], -0.25, None, ALU.mult).then_inc(m_done.sem, 1)

                    maxima(0)
                    maxima(1)
                    for hg in range(HG):
                        dve.wait_ge(pt_done.sem, pt_done.at(i, j * HG + hg + 1))
                        V.tensor_copy(pt[:, hg % 2, :, :].rearrange("p h k -> p (h k)"), trans[hg % 2][0:T, 0:4 * T]).then_inc(pt_sb.sem, 1)
                        if hg + 2 < HG:
                            maxima(hg + 2)

                    def normalise(n, last_p, bias_x, out, done):
                        dve.wait_ge(last_p.sem, last_p.at(i, (j + 1) * (last_p.per // GB)))
                        link(V.reciprocal(rowinv[:, :], rowsum[:, :]))
                        V.tensor_copy(inv_wide[:, :, :].rearrange("p (g r) d -> p g r d", r=4), rowinv[:, :].rearrange("p (r g) -> p g r", r=4).unsqueeze(3).broadcast_to([T, HG, 4, PAD])).then_inc(inv_done.sem, 1)
                        dve.wait_ge(o_done.sem, o_done.at(i, 2 * j + n + 1))
                        dve.wait_ge(invt_sb.sem, invt_sb.at(i, 2 * j + n + 1))
                        V.tensor_tensor(ot[:, :, :].rearrange("p h t -> p (h t)"), outt[:, 0:HG * T],
                                        inv_t[:, :, :].rearrange("p h t -> p (h t)"), ALU.mult).then_inc(o_sb.sem, 1)
                        dve.wait_ge(proj.sem, proj.at(i, 2 * j + n + 1))
                        link(V.tensor_tensor(t[:, :], misc[0:T, 0:D], bias_x, ALU.add))
                        layer_norms(dve, nc, vlink, i, [t[:, :]], stats, [out], done)

                    normalise(0, p_done, xb[:, :], x1[:, :], x1_done)
                    dve.wait_ge(x1_done.sem, x1_done.at(i, j + 1))
                    V.tensor_tensor(xb[:, :], x1[:, :], box[:, :], ALU.add)
                    for k in range(KT):
                        dve.wait_ge(vxp.sem, vxp.at(i, j * KT + k + 1))
                        V.tensor_tensor(vx[:, k, :, 0:DH], trans[k % 2][0:KP, 0:D].rearrange("p (h d) -> p h d", d=DH),
                                        bvx[:, :].rearrange("p (h d) -> p h d", d=DH), ALU.add).then_inc(vx_sb.sem, 1)

                    def xmax(h):
                        dve.wait_ge(sx.sem, sx.at(i, j * HEADS + h + 2))
                        for n in range(2):
                            last = V.tensor_reduce(rowmax[:, column(h + n):column(h + n) + 1], score[(h + n) % 4][0:T, 0:S2], AX.X, ALU.max)
                        link(last)
                        V.tensor_scalar(negmax[:, column(h):column(h) + 5:4], rowmax[:, column(h):column(h) + 5:4], -0.25, None, ALU.mult).then_inc(mx.sem, 1)

                    xmax(0)
                    xmax(2)
                    for h in range(0, HEADS, 2):
                        for n in range(2):
                            dve.wait_ge(ptxd.sem, ptxd.at(i, j * HEADS + h + n + 1))
                            V.tensor_copy(ptx[:, n, :, :].rearrange("p k t -> p (k t)"), trans[n][0:KP, 0:KT * T]).then_inc(ptx_sb.sem, 1)
                        if h + 4 < HEADS:
                            xmax(h + 4)
                    if j == 0:
                        dve.wait_ge(saved.sem, saved.at(i, 0))
                    normalise(1, pxd, xb[:, :], x2[:, j, :], x2_done)

                dve.wait_ge(lg_done.sem, lg_done.at(i, 1))
                wide = lambda a: a.unsqueeze(2).broadcast_to([T, GB, E])
                link(V.tensor_copy(lg[:, :, :], misc[0:T, 0:GB * E].rearrange("p (j e) -> p j e", j=GB)))
                link(V.tensor_reduce(s1[:, 0, :], lg[:, :, :], AX.X, ALU.max))
                V.tensor_tensor(lg[:, :, :], lg[:, :, :], wide(s1[:, 0, :]), ALU.subtract).then_inc(lg_sub.sem, 1)
                dve.wait_ge(lg_exp.sem, lg_exp.at(i, 1))
                link(V.tensor_reduce(s1[:, 1, :], raw[:, :, :], AX.X, ALU.add))
                link(V.reciprocal(s1[:, 2, :], s1[:, 1, :]))
                link(V.tensor_tensor(raw[:, :, :], raw[:, :, :], wide(s1[:, 2, :]), ALU.mult))
                for c in range(2):
                    link(V.tensor_reduce(s1[:, 3 + c, :], raw[:, :, :], AX.X, ALU.max))
                    link(V.tensor_tensor(tmp[:, :, :], raw[:, :, :], wide(s1[:, 3 + c, :]), ALU.is_equal))
                    link(V.tensor_tensor(cand[:, :, :], tmp[:, :, :], rev[:, :].unsqueeze(1).broadcast_to([T, GB, E]), ALU.mult))
                    link(V.tensor_reduce(s1[:, 5, :], cand[:, :, :], AX.X, ALU.max))
                    last = V.tensor_tensor(pick[:, :, c, :], cand[:, :, :], wide(s1[:, 5, :]), ALU.is_equal)
                    if c == 0:
                        link(last)
                        link(V.tensor_scalar(tmp[:, :, :], pick[:, :, 0, :], -1.0, 1.0, ALU.mult, ALU.add))
                        link(V.tensor_tensor(raw[:, :, :], raw[:, :, :], tmp[:, :, :], ALU.mult))
                last.then_inc(picked.sem, 1)
                dve.wait_ge(counted.sem, counted.at(i, 1))
                link(V.tensor_copy(pos[:, :, :, :].rearrange("p j c e -> p (j c e)"), misc[0:T, 0:4 * E]))
                link(V.tensor_scalar(tmp[:, :, :], pos[:, :, 0, :], float(CAP), None, ALU.is_lt))
                V.tensor_tensor(kept[:, :, 0, :], pick[:, :, 0, :], tmp[:, :, :], ALU.mult).then_inc(kept1.sem, 1)
                dve.wait_ge(total1.sem, total1.at(i, 1))
                link(V.tensor_copy(cand[:, 0, :], misc[0:T, 4 * E:5 * E]))
                link(V.tensor_tensor(pos[:, :, 1, :], pos[:, :, 1, :], cand[:, 0, :].unsqueeze(1).broadcast_to([T, GB, E]), ALU.add))
                link(V.tensor_scalar(tmp[:, :, :], pos[:, :, 1, :], float(CAP), None, ALU.is_lt))
                link(V.tensor_tensor(kept[:, :, 1, :], pick[:, :, 1, :], tmp[:, :, :], ALU.mult))
                link(V.tensor_reduce(gate[:, :, :], kept[:, :, :, :], AX.X, ALU.add))
                link(V.tensor_tensor(gate[:, :, :], gate[:, :, :], s1[:, 3:5, :].rearrange("p c j -> p j c"), ALU.mult))
                link(V.tensor_tensor(pos[:, :, :, :], pos[:, :, :, :], kept[:, :, :, :], ALU.mult))
                link(V.tensor_reduce(place[:, :, :], pos[:, :, :, :], AX.X, ALU.add))
                for j in range(GB):
                    for c in range(2):
                        last = V.tensor_scalar(onehot[:, j, c, :], slot_no[:, :], place[:, j, c:c + 1], gate[:, j, c:c + 1], ALU.is_equal, ALU.mult)
                link(last)
                for j in range(GB):
                    spread = lambda a, n: a.unsqueeze(2).broadcast_to([T, E, CAP]) if n else a.unsqueeze(1).broadcast_to([T, E, CAP])
                    V.tensor_tensor(comb[:, j, :, :], spread(kept[:, j, 0, :], 1), spread(onehot[:, j, 0, :], 0), ALU.mult)
                    link(V.tensor_tensor(comb2[:, j, :, :], spread(kept[:, j, 1, :], 1), spread(onehot[:, j, 1, :], 0), ALU.mult))
                    link(V.tensor_tensor(comb[:, j, :, :], comb[:, j, :, :], comb2[:, j, :, :], ALU.add))
                    last = V.tensor_scalar(disp[:, j, :], comb[:, j, :, :].rearrange("p e c -> p (e c)"), 0.0, None, ALU.not_equal)
                last.then_inc(routed.sem, 1)
            assert vlink.seen == vlink.per, vlink.seen



def expert_phase(nc, d, own):
    NP = 2
    ctx = ExitStack()
    with ctx:
        def sb(name, shape, dt=F32):
            return ctx.enter_context(nc.sbuf_tensor("b_" + name, shape, dt))

        def sem(name, per, unit=1, early=False):
            return Steps(own("b_" + name, early), per, unit, early)

        w0 = [sb(f"w0_{n}", [128, KC, HID]) for n in range(NP)]
        w1 = [sb(f"w1_{n}", [128, KC, HID]) for n in range(NP)]
        wo = [sb(f"wo_{n}", [HP, HT, D]) for n in range(NP)]
        xe = [sb(f"xe_{n}", [128, KC, G, CAP]) for n in range(NP)]
        act_out = sb("act_out", [HP, 2, SL])
        hid = sb("hid", [HP, HT, SL])
        eo = [sb(f"eo_{n}", [T, ST, D]) for n in range(NP)]
        up = [ctx.enter_context(nc.psum_tensor(f"b_up{n}", [128, 512], F32)) for n in range(4)]
        down = [ctx.enter_context(nc.psum_tensor(f"b_down{n}", [128, 512], F32)) for n in range(4)]

        loaded = [sem(f"loaded{n}", 5, 16) for n in range(NP)]
        up_done = sem("up_done", NP * HT)
        gelu = sem("gelu", NP * HT)
        hid_done = sem("hid_done", NP * HT, early=True)
        down_done = sem("down_done", NP * ST)
        eo_sb = sem("eo_sb", NP * ST, early=True)
        stored = [sem(f"stored{n}", 2, 16) for n in range(NP)]
        saved = sem("saved", NP, early=True)
        block = ctx.enter_context(nc.Block())

        @block.sync
        def _(sp):
            def load(e, n):
                for dst, src in ((w0[n][:, :, :], d["w0"][e]), (w1[n][:, :, :], d["w1"][e]), (wo[n][:, :, :], d["wo"][e])):
                    sp.dma_start(dst, src).then_inc(loaded[n].sem, 16)
                for kc in range(KC):
                    sp.dma_start(xe[n][:, kc, :, :], d["s_xe_by_expert"][e][kc]).then_inc(loaded[n].sem, 16)

            for n in range(NP):
                load(n, n)
            with sp.Fori(0, E // NP - 1) as i:
                for n in range(NP):
                    sp.wait_ge(down_done.sem, down_done.at(i, (n + 1) * ST))
                    load(i * NP + (NP + n), n)

        @block.gpsimd
        def _(pool):
            with pool.Fori(0, E // NP) as i:
                for n in range(NP):
                    pool.wait_ge(eo_sb.sem, eo_sb.at(i, (n + 1) * ST))
                    for g in range(2):
                        pool.dma_start(d["s_eo_by_expert"][i * NP + n][g], eo[n][g * CAP:(g + 1) * CAP, :, :]).then_inc(stored[n].sem, 16)
                    pool.wait_ge(stored[n].sem, stored[n].at(i, 2))
                    pool.sem_inc(saved.sem, 1)

        @block.tensor
        def _(pe):
            mm = nc.tensor.matmul
            with pe.Fori(0, E // NP) as i:
                for n in range(NP):
                    pe.wait_ge(loaded[n].sem, loaded[n].at(i, 5))
                    for h in range(HT):
                        pe.wait_ge(hid_done.sem, hid_done.at(i, max(n * HT + h - 1, 0)))
                        for m, w in enumerate((w0[n], w1[n])):
                            for kc in range(KC):
                                last = mm(up[2 * (h % 2) + m][0:HP, 0:SL], w[:, kc, h * HP:(h + 1) * HP],
                                          xe[n][:, kc, :, :].rearrange("p g c -> p (g c)"), start=kc == 0, stop=kc == KC - 1)
                        last.then_inc(up_done.sem, 1)
                    for s in range(ST):
                        pe.wait_ge(eo_sb.sem, eo_sb.at(i, max(n * ST + s - 3, 0)))
                        for h in range(HT):
                            if s == 0:
                                pe.wait_ge(hid_done.sem, hid_done.at(i, n * HT + h + 1))
                            last = mm(down[s][0:T, 0:D], hid[:, h, s * T:(s + 1) * T], wo[n][:, h, :], start=h == 0, stop=h == HT - 1)
                        last.then_inc(down_done.sem, 1)

        @block.scalar
        def _(act):
            with act.Fori(0, E // NP) as i:
                for n in range(NP):
                    for h in range(HT):
                        act.wait_ge(up_done.sem, up_done.at(i, n * HT + h + 1))
                        nc.scalar.activation(act_out[:, h % 2, :], up[2 * (h % 2)][0:HP, 0:SL], ACT.Gelu_apprx_tanh).then_inc(gelu.sem, 1)

        @block.vector
        def _(dve):
            with dve.Fori(0, E // NP) as i:
                for n in range(NP):
                    for h in range(HT):
                        dve.wait_ge(gelu.sem, gelu.at(i, n * HT + h + 1))
                        nc.vector.tensor_tensor(hid[:, h, :], up[2 * (h % 2) + 1][0:HP, 0:SL], act_out[:, h % 2, :], ALU.mult).then_inc(hid_done.sem, 1)
                    dve.wait_ge(saved.sem, saved.at(i, 0))
                    for s in range(ST):
                        dve.wait_ge(down_done.sem, down_done.at(i, n * ST + s + 1))
                        nc.vector.tensor_copy(eo[n][:, s, :], down[s][0:T, 0:D]).then_inc(eo_sb.sem, 1)

DIN, NST, RANK, TAPS = 512, 16, 64, 4
DT = DIN // 128
QB = 4
QT = QB * T
XD = RANK + 2 * NST
SPREAD = 6


def mixer_phase(nc, d, own):
    ctx = ExitStack()
    with ctx:
        def sb(name, shape, dt=F32):
            return ctx.enter_context(nc.sbuf_tensor("c_" + name, shape, dt))

        def sem(name, per, unit=1, early=False):
            return Steps(own("c_" + name, early), per, unit, early)

        win = sb("win", [128, KC, 2 * DIN])
        convw = sb("convw", [128, DT, TAPS])
        convb = sb("convb", [128, DT])
        wx = sb("wx", [128, DT, XD])
        wdt = sb("wdt", [RANK, DIN])
        bdt = sb("bdt", [128, DT])
        alog = sb("alog", [128, DT, NST])
        aneg = sb("aneg", [128, DT, NST])
        dp = sb("dp", [128, DT])
        wout = sb("wout", [128, DT, D])
        ident = sb("ident", [128, 128])
        row_of = sb("row_of", [XD, 2 * NST, 128])

        x2 = sb("x2", [T, QB // GB, GB, D])
        eo = sb("eo", [T, QB // GB, ST, D])
        ct = sb("ct", [T, QB // GB, GB, ST, T])
        t = sb("t", [T, QB, D])
        stats = sb("stats", [T, QB, 10])
        x3 = sb("x3", [T, QB, D])
        x3t = sb("x3t", [128, KC, QT])
        u = sb("u", [128, DT, QB, TAPS - 1 + T])
        conv = sb("conv", [128, DT, QT])
        us = sb("us", [128, DT, QT])
        rs = sb("rs", [128, DT, QT])
        xd = sb("xd", [XD, QT])
        z = sb("z", [128, DT, QT])
        soft = sb("soft", [128, DT, QT])
        delta = sb("delta", [128, DT, QT])
        du = sb("du", [128, DT, QT])
        bc = sb("bc", [128, 2 * NST, QT])
        decay = sb("decay", [128, 2, QT])
        bu = sb("bu", [128, 3, QT])
        state = sb("state", [128, 2, QT])
        out_c = sb("out_c", [128, 2, QT])
        x4 = sb("x4", [T, QB, D])
        bank = [ctx.enter_context(nc.psum_tensor(f"c_bank{n}", [128, 512], F32)) for n in range(8)]

        weights = sem("weights", 1)
        ready = sem("ready", 1)
        loaded = sem("loaded", 3 * (QB // GB), 16)
        gathered = sem("gathered", QB)
        g_read = sem("g_read", QB, early=True)
        x3_done = sem("x3_done", QB)
        x3t_done = sem("x3t_done", 1)
        x3t_sb = sem("x3t_sb", 1)
        xr = sem("xr", 2 * DT)
        xr_sb = sem("xr_sb", 2 * DT, early=True)
        conv_done = sem("conv_done", DT)
        us_done = sem("us_done", DT)
        xd_done = sem("xd_done", 1)
        xd_sb = sem("xd_sb", 1)
        dz = sem("dz", DT)
        z_done = sem("z_done", DT, early=True)
        alink = sem("alink", 2 * DT)
        sp_done = sem("sp_done", DT)
        du_done = sem("du_done", DT, early=True)
        bc_done = sem("bc_done", 2 * NST)
        bc_sb = sem("bc_sb", 2 * NST, early=True)
        decayed = sem("decayed", DT * NST)
        bu_done = sem("bu_done", DT * NST)
        scanned = sem("scanned", DT * NST, early=True)
        weighted = sem("weighted", DT * NST, early=True)
        summed = sem("summed", DT * NST, early=True)
        y_done = sem("y_done", DT, early=True)
        out_done = sem("out_done", QB)
        x4_done = sem("x4_done", QB, early=True)
        stored = sem("stored", 1, 16)
        saved = sem("saved", 1, early=True)
        vlink = sem("vlink", 61)
        gather_bank = [0, 1, 6, 7]
        block = ctx.enter_context(nc.Block())
        flat = lambda a: a.rearrange("p a b -> p (a b)")

        loads = [(win[:, :, :], d["win"]), (convw[:, :, :], d["convw"]), (convb[:, :], d["convb"]), (wx[:, :, :], d["wx"]),
                 (wdt[:, :], d["wdt"]), (bdt[:, :], d["bdt"]), (alog[:, :, :], d["alog"]), (dp[:, :], d["dp"]),
                 (wout[:, :, :], d["wout"]), (ident[:, :], d["ident"]), (row_of[:, :, :], d["row_of"])]

        @block.sync
        def _(sp):
            for dst, src in loads:
                sp.dma_start(dst, src).then_inc(weights.sem, 16)
            with sp.Fori(0, B // QB) as i:
                sp.wait_ge(g_read.sem, g_read.at(i, 0))
                for g in range(QB // GB):
                    sp.dma_start(x2[:, g, :, :], d["s_x2"][i * (QB // GB) + g]).then_inc(loaded.sem, 16)
                    sp.dma_start(eo[:, g, :, :], d["s_eo_by_group"][i * (QB // GB) + g]).then_inc(loaded.sem, 16)
                    sp.dma_start(ct[:, g, :, :, :], d["s_ct"][i * (QB // GB) + g]).then_inc(loaded.sem, 16)

        @block.gpsimd
        def _(pool):
            nc.gpsimd.memset(u[:, :, :, :].rearrange("p a b c -> p (a b c)"), 0.0)
            nc.gpsimd.memset(flat(decay[:, :, :]), 0.0).then_inc(ready.sem, 1)
            with pool.Fori(0, B // QB) as i:
                for k in range(DT * NST):
                    pool.wait_ge(scanned.sem, scanned.at(i, k + 1))
                    pool.wait_ge(summed.sem, summed.at(i, max(k - 1, 0)))
                    nc.gpsimd.tensor_tensor(out_c[:, k % 2, :], state[:, k % 2, :], bc[:, NST + k % NST, :], ALU.mult).then_inc(weighted.sem, 1)
                pool.wait_ge(x4_done.sem, x4_done.at(i, QB))
                pool.dma_start(d["s_x4_by_four"][i], x4[:, :, :]).then_inc(stored.sem, 16)
                pool.wait_ge(stored.sem, stored.at(i, 1))
                pool.sem_inc(saved.sem, 1)

        @block.tensor
        def _(pe):
            mm = nc.tensor.matmul
            pe.wait_ge(weights.sem, 16 * len(loads))
            with pe.Fori(0, B // QB) as i:
                pe.wait_ge(loaded.sem, loaded.at(i, 6))
                pe.wait_ge(x4_done.sem, x4_done.at(i, 0))
                for b in range(QB):
                    for s in range(ST):
                        last = mm(bank[gather_bank[b]][0:T, 0:D], ct[:, b // GB, b % GB, s, :], eo[:, b // GB, s, :], start=s == 0, stop=s == ST - 1)
                    last.then_inc(gathered.sem, 1)
                for b in range(QB):
                    pe.wait_ge(x3_done.sem, x3_done.at(i, b + 1))
                    for kc in range(KC):
                        last = nc.tensor.transpose(bank[2 + kc][:, b * T:(b + 1) * T], x3[:, b, kc * 128:(kc + 1) * 128], ident[0:T, 0:T])
                last.then_inc(x3t_done.sem, 1)
                pe.wait_ge(x3t_sb.sem, x3t_sb.at(i, 1))
                for k in range(2 * DT):
                    pe.wait_ge(xr_sb.sem, xr_sb.at(i, max(k - 1, 0)))
                    for kc in range(KC):
                        last = mm(bank[4 + k % 2][:, 0:QT], win[:, kc, k * 128:(k + 1) * 128], x3t[:, kc, :], start=kc == 0, stop=kc == KC - 1)
                    last.then_inc(xr.sem, 1)
                for k in range(DT):
                    pe.wait_ge(us_done.sem, us_done.at(i, k + 1))
                    last = mm(bank[6][0:XD, 0:QT], wx[:, k, :], us[:, k, :], start=k == 0, stop=k == DT - 1)
                last.then_inc(xd_done.sem, 1)
                pe.wait_ge(xd_sb.sem, xd_sb.at(i, 1))
                pe.wait_ge(xr_sb.sem, xr_sb.at(i, 2 * DT))

                def spread(k):
                    pe.wait_ge(bc_sb.sem, bc_sb.at(i, max(k + 1 - SPREAD, 0)))
                    mm(bank[k % SPREAD][:, 0:QT], row_of[RANK:XD, (k % 2) * NST + k // 2, :], xd[RANK:XD, :], start=True, stop=True,
                       tile_position=(RANK, 0)).then_inc(bc_done.sem, 1)

                for k in range(4):
                    spread(k)
                for k in range(DT):
                    pe.wait_ge(z_done.sem, z_done.at(i, max(k - 1, 0)))
                    mm(bank[4 + k % 2][:, 0:QT], wdt[:, k * 128:(k + 1) * 128], xd[0:RANK, :], start=True, stop=True).then_inc(dz.sem, 1)

                pe.wait_ge(z_done.sem, z_done.at(i, DT))
                for k in range(4, SPREAD):
                    spread(k)
                for k in range(DT * NST):
                    for n in range(SPREAD + 2 * k, SPREAD + 2 * k + 2):
                        if n < 2 * NST:
                            spread(n)
                    n, dt = k % NST, k // NST
                    if n == 0:
                        pe.wait_ge(y_done.sem, y_done.at(i, max(dt - 1, 0)))
                    pe.wait_ge(weighted.sem, weighted.at(i, k + 1))
                    mm(bank[6 + dt % 2][:, 0:QT], ident[:, :], out_c[:, k % 2, :], start=n == 0, stop=n == NST - 1).then_inc(summed.sem, 1)
                pe.wait_ge(y_done.sem, y_done.at(i, DT))
                for b in range(QB):
                    for k in range(DT):
                        last = mm(bank[b][0:T, 0:D], rs[:, k, b * T:(b + 1) * T], wout[:, k, :], start=k == 0, stop=k == DT - 1)
                    last.then_inc(out_done.sem, 1)

        @block.scalar
        def _(act):
            fn = nc.scalar.activation
            act.wait_ge(weights.sem, 16 * len(loads))
            fn(flat(aneg[:, :, :]), flat(alog[:, :, :]), ACT.Exp).then_inc(ready.sem, 1)
            act.wait_ge(ready.sem, 3)
            with act.Fori(0, B // QB) as i:
                act.wait_ge(x3t_done.sem, x3t_done.at(i, 1))
                fn(x3t[:, 0, :], bank[2][:, 0:QT], ACT.Copy)
                fn(x3t[:, 1, :], bank[3][:, 0:QT], ACT.Copy).then_inc(x3t_sb.sem, 1)
                for k in range(2 * DT):
                    act.wait_ge(xr.sem, xr.at(i, k + 1))
                    src = bank[4 + k % 2][:, 0:QT]
                    if k < DT:
                        fn(u[:, k, :, TAPS - 1:], src.rearrange("p (b t) -> p b t", b=QB), ACT.Copy).then_inc(xr_sb.sem, 1)
                    else:
                        fn(rs[:, k - DT, :], src, ACT.Silu).then_inc(xr_sb.sem, 1)
                for k in range(DT):
                    act.wait_ge(conv_done.sem, conv_done.at(i, k + 1))
                    fn(us[:, k, :], conv[:, k, :], ACT.Silu, bias=convb[:, k:k + 1]).then_inc(us_done.sem, 1)
                act.wait_ge(xd_done.sem, xd_done.at(i, 1))
                fn(xd[:, :], bank[6][0:XD, 0:QT], ACT.Copy).then_inc(xd_sb.sem, 1)

                def take_rows(k):
                    for n in range(2):
                        act.wait_ge(bc_done.sem, bc_done.at(i, 2 * k + n + 1))
                        fn(bc[:, n * NST + k, :], bank[(2 * k + n) % SPREAD][:, 0:QT], ACT.Copy).then_inc(bc_sb.sem, 1)

                take_rows(0)
                take_rows(1)
                for k in range(DT):
                    act.wait_ge(z_done.sem, z_done.at(i, k + 1))
                    fn(soft[:, k, :], z[:, k, :], ACT.Abs).then_inc(alink.sem, 1)
                for k in range(DT):
                    act.wait_ge(alink.sem, alink.at(i, k + 1))
                    fn(soft[:, k, :], soft[:, k, :], ACT.Exp, scale=-1.0).then_inc(alink.sem, 1)
                for k in range(DT):
                    act.wait_ge(alink.sem, alink.at(i, DT + k + 1))
                    fn(soft[:, k, :], soft[:, k, :], ACT.Ln, bias=1.0).then_inc(sp_done.sem, 1)
                for k in range(DT * NST):
                    if 2 <= k < NST:
                        take_rows(k)
                    if k % NST == 0:
                        act.wait_ge(du_done.sem, du_done.at(i, k // NST + 1))
                    act.wait_ge(scanned.sem, scanned.at(i, max(k - 1, 0)))
                    by_seq = lambda a: a.rearrange("p (b t) -> p b t", b=QB)[:, :, 1:]
                    fn(by_seq(decay[:, k % 2, :]), by_seq(delta[:, k // NST, :]), ACT.Exp,
                       scale=aneg[:, k // NST, k % NST:k % NST + 1]).then_inc(decayed.sem, 1)

        @block.vector
        def _(dve):
            V = nc.vector
            dve.wait_ge(weights.sem, 16 * len(loads))
            dve.wait_ge(ready.sem, 2)
            V.tensor_scalar(flat(aneg[:, :, :]), flat(aneg[:, :, :]), -1.0, None, ALU.mult).then_inc(ready.sem, 1)
            with dve.Fori(0, B // QB) as i:
                link = lambda ins: vlink.chain(dve, i, ins)
                dve.wait_ge(loaded.sem, loaded.at(i, 6))
                for b in range(QB):
                    dve.wait_ge(gathered.sem, gathered.at(i, b + 1))
                    V.tensor_tensor(t[:, b, :], bank[gather_bank[b]][0:T, 0:D], x2[:, b // GB, b % GB, :], ALU.add).then_inc(g_read.sem, 1)
                dve.wait_ge(g_read.sem, g_read.at(i, QB))
                layer_norms(dve, nc, vlink, i, [t[:, b, :] for b in range(QB)], stats, [x3[:, b, :] for b in range(QB)], x3_done)
                for k in range(DT):
                    dve.wait_ge(xr_sb.sem, xr_sb.at(i, k + 1))
                    c3 = conv[:, k, :].rearrange("p (b t) -> p b t", b=QB)
                    link(V.tensor_scalar(c3, u[:, k, :, 0:T], convw[:, k, 0:1], None, ALU.mult))
                    for tap in range(1, TAPS):
                        last = V.scalar_tensor_tensor(c3, u[:, k, :, tap:tap + T], convw[:, k, tap:tap + 1], c3, ALU.mult, ALU.add)
                        if tap < TAPS - 1:
                            link(last)
                    last.then_inc(conv_done.sem, 1)
                for k in range(DT):
                    dve.wait_ge(dz.sem, dz.at(i, k + 1))
                    V.tensor_scalar(z[:, k, :], bank[4 + k % 2][:, 0:QT], bdt[:, k:k + 1], None, ALU.add).then_inc(z_done.sem, 1)
                for k in range(DT):
                    dve.wait_ge(sp_done.sem, sp_done.at(i, k + 1))
                    link(V.scalar_tensor_tensor(delta[:, k, :], z[:, k, :], 0.0, soft[:, k, :], ALU.max, ALU.add))
                    V.tensor_tensor(du[:, k, :], delta[:, k, :], us[:, k, :], ALU.mult).then_inc(du_done.sem, 1)
                dve.wait_ge(du_done.sem, du_done.at(i, DT))

                def times_b(k):
                    if k < NST:
                        dve.wait_ge(bc_sb.sem, bc_sb.at(i, 2 * k + 1))
                    dve.wait_ge(scanned.sem, scanned.at(i, max(k - 2, 0)))
                    V.tensor_tensor(bu[:, k % 3, :], du[:, k // NST, :], bc[:, k % NST, :], ALU.mult).then_inc(bu_done.sem, 1)

                def gate(dt):
                    dve.wait_ge(summed.sem, summed.at(i, (dt + 1) * NST))
                    link(V.scalar_tensor_tensor(conv[:, dt, :], us[:, dt, :], dp[:, dt:dt + 1], bank[6 + dt % 2][:, 0:QT], ALU.mult, ALU.add))
                    V.tensor_tensor(rs[:, dt, :], conv[:, dt, :], rs[:, dt, :], ALU.mult).then_inc(y_done.sem, 1)

                times_b(0)
                for k in range(DT * NST):
                    if k + 1 < DT * NST:
                        times_b(k + 1)
                    dve.wait_ge(bu_done.sem, bu_done.at(i, k + 1))
                    dve.wait_ge(decayed.sem, decayed.at(i, k + 1))
                    dve.wait_ge(weighted.sem, weighted.at(i, max(k - 1, 0)))
                    V.tensor_tensor_scan(state[:, k % 2, :], decay[:, k % 2, :], bu[:, k % 3, :], 0.0, ALU.mult, ALU.add).then_inc(scanned.sem, 1)
                    if k % NST == 4 and k > NST:
                        gate(k // NST - 1)
                gate(DT - 1)
                dve.wait_ge(saved.sem, saved.at(i, 0))
                for b in range(QB):
                    dve.wait_ge(out_done.sem, out_done.at(i, b + 1))
                    last = V.tensor_tensor(t[:, b, :], bank[b][0:T, 0:D], x3[:, b, :], ALU.add)
                link(last)
                layer_norms(dve, nc, vlink, i, [t[:, b, :] for b in range(QB)], stats, [x4[:, b, :] for b in range(QB)], x4_done)
            assert vlink.seen == vlink.per, vlink.seen

ROUNDS = 3
RMS_EPS = 1e-6
SLOT_INPUTS = ["ctxt", "ctx_rows", "wk", "wv", "wq", "wih", "whh", "L1_xattn_gru_bih", "L1_xattn_gru_bhh", "snorm", "inorm", "ident"]


def slot_phase(nc, d, own):
    ctx = ExitStack()
    with ctx:
        def sb(name, shape, dt=F32):
            return ctx.enter_context(nc.sbuf_tensor("d_" + name, shape, dt))

        def sem(name, per, unit=1, early=False):
            return Steps(own("d_" + name, early), per, unit, early)

        wk = sb("wk", [128, KC, D])
        wv = sb("wv", [128, KC, D])
        wq = sb("wq", [128, KC, D])
        wih = sb("wih", [128, KC, 3 * D])
        whh = sb("whh", [128, KC, 3 * D])
        bih = sb("bih", [T, 3 * D])
        bhh = sb("bhh", [T, 3 * D])
        snorm = sb("snorm", [128, KC])
        inorm = sb("inorm", [128, KC])
        ident = sb("ident", [128, 128])

        ctxt = sb("ctxt", [128, QB, KC, S2])
        rows = sb("rows", [KP, QB, KT, D])
        x4 = sb("x4", [T, QB, D])
        csq = sb("csq", [KP, QB, KT, D])
        ssq = sb("ssq", [T, QB, D])
        csum = sb("csum", [KP, QB, KT])
        cinv = sb("cinv", [KP, QB, KT])
        ctmp = sb("ctmp", [KP, QB, KT])
        cscale = sb("cscale", [KP, QB, KT])
        kt = sb("kt", [128, QB, KC, S2])
        v = sb("v", [KP, QB, KT, D + 1])
        ssum = sb("ssum", [T, QB])
        sinv = sb("sinv", [T, QB])
        stmp = sb("stmp", [T, QB])
        s = sb("s", [T, QB, D])
        sn = sb("sn", [T, QB, D])
        stn = sb("stn", [128, QB, 2 * KC, T])
        qt = sb("qt", [128, QB, KC, T])
        smax = sb("smax", [KP, QB, KT])
        nmax = sb("nmax", [KP, QB, KT])
        esum = sb("esum", [KP, QB, KT])
        einv = sb("einv", [KP, QB, KT])
        e = sb("e", [KP, QB, KT, T])
        den = sb("den", [T, QB])
        upd = sb("upd", [T, QB, D])
        ut = sb("ut", [128, QB, KC, T])
        rz = sb("rz", [T, QB, 2 * D])
        hn = sb("hn", [T, QB, D])
        xn = sb("xn", [T, QB, D])
        cand = sb("cand", [T, QB, D])
        t = sb("t", [T, QB, D])
        stats = sb("stats", [T, QB, 10])
        x5 = sb("x5", [T, QB, D])
        small = [ctx.enter_context(nc.psum_tensor(f"d_small{j}", [128, 512], F32)) for j in range(GB)]
        wide = [ctx.enter_context(nc.psum_tensor(f"d_wide{j}", [128, 512], F32)) for j in range(GB)]
        gates = [ctx.enter_context(nc.psum_tensor(f"d_gates{j}", [128, 512], F32)) for j in range(GB)]
        news = [ctx.enter_context(nc.psum_tensor(f"d_news{j}", [128, 512], F32)) for j in range(GB)]

        N = ROUNDS * QB
        weights = sem("weights", 1)
        ready = sem("ready", 1)
        in_ctx = [sem(f"in_ctx{j}", 2, 16) for j in range(QB)]
        in_x = [sem(f"in_x{j}", 1, 16) for j in range(QB)]
        squares = sem("squares", QB)
        kproj = sem("kproj", QB)
        k_sb = sem("k_sb", QB)
        vproj = sem("vproj", QB * KT)
        v_sb = sem("v_sb", QB * KT, early=True)
        s_sq = sem("s_sq", N)
        sn_done = sem("sn_done", N)
        stn_done = sem("stn_done", N)
        stn_sb = sem("stn_sb", N)
        q_done = sem("q_done", N)
        q_sb = sem("q_sb", N)
        score = sem("score", N)
        max_done = sem("max_done", N)
        exp_done = sem("exp_done", N)
        attn = sem("attn", N)
        u_done = sem("u_done", N)
        upd_done = sem("upd_done", N)
        ut_done = sem("ut_done", N)
        ut_sb = sem("ut_sb", N)
        gru = sem("gru", N)
        rz_sb = sem("rz_sb", N)
        rz_tanh = sem("rz_tanh", N)
        pre_n = sem("pre_n", N)
        n_tanh = sem("n_tanh", N)
        s_done = sem("s_done", N, early=True)
        x5_done = sem("x5_done", QB, early=True)
        stored = sem("stored", 1, 16)
        saved = sem("saved", 1, early=True)
        vlink = sem("vlink", 253)
        block = ctx.enter_context(nc.Block())
        loads = [(wk[:, :, :], d["wk"]), (wv[:, :, :], d["wv"]), (wq[:, :, :], d["wq"]), (wih[:, :, :], d["wih"]), (whh[:, :, :], d["whh"]),
                 (bih[:, :], d["L1_xattn_gru_bih"].partition_broadcast(T)), (bhh[:, :], d["L1_xattn_gru_bhh"].partition_broadcast(T)),
                 (snorm[:, :], d["snorm"]), (inorm[:, :], d["inorm"]), (ident[:, :], d["ident"])]

        pairs = [range(g, g + GB) for g in range(0, QB, GB)]

        def slots(r, j):
            return x4[:, j, :] if r == 0 else s[:, j, :]

        @block.sync
        def _(sp):
            for dst, src in loads:
                sp.dma_start(dst, src).then_inc(weights.sem, 16)
            with sp.Fori(0, B // QB) as i:
                sp.wait_ge(v_sb.sem, v_sb.at(i, 0))
                for j in range(QB):
                    sp.dma_start(ctxt[:, j, :, :], d["ctxt"][i * QB + j]).then_inc(in_ctx[j].sem, 16)
                    sp.dma_start(rows[:, j, :, :], d["ctx_rows"][i * QB + j]).then_inc(in_ctx[j].sem, 16)
                sp.wait_ge(x5_done.sem, x5_done.at(i, 0))
                for j in range(QB):
                    sp.dma_start(x4[:, j, :], d["s_x4"][i * QB + j]).then_inc(in_x[j].sem, 16)

        @block.gpsimd
        def _(pool):
            with pool.Fori(0, B // QB) as i:
                pool.wait_ge(x5_done.sem, x5_done.at(i, QB))
                pool.dma_start(d["s_x5_by_four"][i], x5[:, :, :]).then_inc(stored.sem, 16)
                pool.wait_ge(stored.sem, stored.at(i, 1))
                pool.sem_inc(saved.sem, 1)

        @block.tensor
        def _(pe):
            mm = nc.tensor.matmul
            pe.wait_ge(ready.sem, 1)
            with pe.Fori(0, B // QB) as i:
                for j in range(QB):
                    b = j % GB
                    pe.wait_ge(in_ctx[j].sem, in_ctx[j].at(i, 2))
                    pe.wait_ge(s_done.sem, s_done.at(i, 0))
                    if j >= GB:
                        pe.wait_ge(v_sb.sem, v_sb.at(i, (j - GB + 1) * KT))
                    for oc, bank in enumerate((gates[b], news[b])):
                        for kc in range(KC):
                            last = mm(bank[:, 0:S2], wk[:, kc, oc * 128:(oc + 1) * 128], ctxt[:, j, kc, :], start=kc == 0, stop=kc == KC - 1)
                    last.then_inc(kproj.sem, 1)
                    for k, bank in enumerate((small[b], wide[b], gates[b])):
                        if k == 2:
                            pe.wait_ge(k_sb.sem, k_sb.at(i, j + 1))
                        for kc in range(KC):
                            last = mm(bank[0:KP, 0:D], ctxt[:, j, kc, k * KP:(k + 1) * KP], wv[:, kc, :], start=kc == 0, stop=kc == KC - 1)
                        last.then_inc(vproj.sem, 1)

                def front(r, pair):
                    for j in pair:
                        n = r * QB + j
                        pe.wait_ge(sn_done.sem, sn_done.at(i, n + 1))
                        if r == 0:
                            pe.wait_ge(v_sb.sem, v_sb.at(i, QB * KT))
                        for m, src in enumerate((slots(r, j), sn[:, j, :])):
                            for kc in range(KC):
                                c = m * KC + kc
                                last = nc.tensor.transpose(small[j % GB][:, c * T:(c + 1) * T], src[:, kc * 128:(kc + 1) * 128], ident[0:T, 0:T])
                        last.then_inc(stn_done.sem, 1)
                    for j in pair:
                        n = r * QB + j
                        pe.wait_ge(stn_sb.sem, stn_sb.at(i, n + 1))
                        for oc in range(KC):
                            for kc in range(KC):
                                last = mm(small[j % GB][:, oc * T:(oc + 1) * T], wq[:, kc, oc * 128:(oc + 1) * 128], stn[:, j, KC + kc, :],
                                          start=kc == 0, stop=kc == KC - 1)
                        last.then_inc(q_done.sem, 1)
                    for j in pair:
                        n = r * QB + j
                        pe.wait_ge(q_sb.sem, q_sb.at(i, n + 1))
                        if j >= GB:
                            pe.wait_ge(exp_done.sem, exp_done.at(i, n - GB + 1))
                        for k in range(KT):
                            for kc in range(KC):
                                last = mm(wide[j % GB][0:KP, k * T:(k + 1) * T], kt[:, j, kc, k * KP:(k + 1) * KP], qt[:, j, kc, :],
                                          start=kc == 0, stop=kc == KC - 1)
                        last.then_inc(score.sem, 1)

                def back(r, pair):
                    for j in pair:
                        n = r * QB + j
                        pe.wait_ge(attn.sem, attn.at(i, n + 1))
                        for k in range(KT):
                            last = mm(small[j % GB][0:T, 0:D + 1], e[:, j, k, :], v[:, j, k, :], start=k == 0, stop=k == KT - 1)
                        last.then_inc(u_done.sem, 1)
                    for j in pair:
                        if j >= GB:
                            pe.wait_ge(rz_sb.sem, rz_sb.at(i, r * QB + j - GB + 1))
                        for kc in range(KC):
                            mm(gates[j % GB][0:T, :], stn[:, j, kc, :], whh[:, kc, 0:2 * D], start=kc == 0, stop=False)
                        for kc in range(KC):
                            mm(news[j % GB][0:T, D:2 * D], stn[:, j, kc, :], whh[:, kc, 2 * D:3 * D], start=kc == 0, stop=kc == KC - 1)
                    for j in pair:
                        n = r * QB + j
                        pe.wait_ge(upd_done.sem, upd_done.at(i, n + 1))
                        if j < GB:
                            pe.wait_ge(exp_done.sem, exp_done.at(i, n + GB + 1))
                        for kc in range(KC):
                            last = nc.tensor.transpose(wide[j % GB][:, kc * T:(kc + 1) * T], upd[:, j, kc * 128:(kc + 1) * 128], ident[0:T, 0:T])
                        last.then_inc(ut_done.sem, 1)
                    for j in pair:
                        n = r * QB + j
                        pe.wait_ge(ut_sb.sem, ut_sb.at(i, n + 1))
                        for kc in range(KC):
                            mm(gates[j % GB][0:T, :], ut[:, j, kc, :], wih[:, kc, 0:2 * D], start=False, stop=kc == KC - 1)
                        for kc in range(KC):
                            last = mm(news[j % GB][0:T, 0:D], ut[:, j, kc, :], wih[:, kc, 2 * D:3 * D], start=kc == 0, stop=kc == KC - 1)
                        last.then_inc(gru.sem, 1)

                for r in range(ROUNDS):
                    for pair in pairs:
                        front(r, pair)
                    for pair in pairs:
                        back(r, pair)

        @block.scalar
        def _(act):
            fn = nc.scalar.activation
            act.wait_ge(ready.sem, 1)
            with act.Fori(0, B // QB) as i:
                for j in range(QB):
                    act.wait_ge(in_ctx[j].sem, in_ctx[j].at(i, 2))
                    for k in range(KT):
                        last = fn(csq[:, j, k, :], rows[:, j, k, :], ACT.Square, accum_out=csum[:, j, k:k + 1])
                    last.then_inc(squares.sem, 1)
                    act.wait_ge(kproj.sem, kproj.at(i, j + 1))
                    fn(kt[:, j, 0, :], gates[j % GB][:, 0:S2], ACT.Copy)
                    fn(kt[:, j, 1, :], news[j % GB][:, 0:S2], ACT.Copy).then_inc(k_sb.sem, 1)

                def square(r, pair):
                    for j in pair:
                        if r == 0:
                            act.wait_ge(in_x[j].sem, in_x[j].at(i, 1))
                        else:
                            act.wait_ge(s_done.sem, s_done.at(i, (r - 1) * QB + j + 1))
                        fn(ssq[:, j, :], slots(r, j), ACT.Square, accum_out=ssum[:, j:j + 1]).then_inc(s_sq.sem, 1)

                def front(r, pair):
                    for j in pair:
                        act.wait_ge(stn_done.sem, stn_done.at(i, r * QB + j + 1))
                        fn(stn[:, j, :, :].rearrange("p c t -> p (c t)"), small[j % GB][:, 0:2 * KC * T], ACT.Copy).then_inc(stn_sb.sem, 1)
                    for j in pair:
                        act.wait_ge(q_done.sem, q_done.at(i, r * QB + j + 1))
                        fn(qt[:, j, :, :].rearrange("p c t -> p (c t)"), small[j % GB][:, 0:KC * T], ACT.Copy).then_inc(q_sb.sem, 1)
                    for j in pair:
                        act.wait_ge(max_done.sem, max_done.at(i, r * QB + j + 1))
                        for k in range(KT):
                            last = fn(e[:, j, k, :], wide[j % GB][0:KP, k * T:(k + 1) * T], ACT.Exp, bias=nmax[:, j, k:k + 1],
                                      scale=cscale[:, j, k:k + 1], accum_out=esum[:, j, k:k + 1])
                        last.then_inc(exp_done.sem, 1)

                def back(r, pair):
                    for j in pair:
                        act.wait_ge(ut_done.sem, ut_done.at(i, r * QB + j + 1))
                        fn(ut[:, j, :, :].rearrange("p c t -> p (c t)"), wide[j % GB][:, 0:KC * T], ACT.Copy).then_inc(ut_sb.sem, 1)
                    for j in pair:
                        act.wait_ge(rz_sb.sem, rz_sb.at(i, r * QB + j + 1))
                        fn(rz[:, j, :], rz[:, j, :], ACT.Tanh, scale=0.5).then_inc(rz_tanh.sem, 1)
                    for j in pair:
                        act.wait_ge(pre_n.sem, pre_n.at(i, r * QB + j + 1))
                        fn(cand[:, j, :], xn[:, j, :], ACT.Tanh).then_inc(n_tanh.sem, 1)

                for pair in pairs:
                    square(0, pair)
                for r in range(ROUNDS):
                    for pair in pairs:
                        front(r, pair)
                    for pair in pairs:
                        back(r, pair)
                        if r + 1 < ROUNDS:
                            square(r + 1, pair)

        @block.vector
        def _(dve):
            V = nc.vector
            dve.wait_ge(weights.sem, 16 * len(loads))
            V.memset(v[:, :, :, :].rearrange("p a b c -> p (a b c)"), 1.0)
            for kc in range(KC):
                V.tensor_scalar(wk[:, kc, :], wk[:, kc, :], inorm[:, kc:kc + 1], None, ALU.mult)
                V.tensor_scalar(wv[:, kc, :], wv[:, kc, :], inorm[:, kc:kc + 1], None, ALU.mult)
                V.tensor_scalar(wq[:, kc, :], wq[:, kc, :], snorm[:, kc:kc + 1], None, ALU.mult)
            V.tensor_tensor(bih[:, 0:2 * D], bih[:, 0:2 * D], bhh[:, 0:2 * D], ALU.add).then_inc(ready.sem, 1)
            dve.wait_ge(ready.sem, 1)
            with dve.Fori(0, B // QB) as i:
                link = lambda ins: vlink.chain(dve, i, ins)
                for j in range(QB):
                    dve.wait_ge(squares.sem, squares.at(i, j + 1))
                    link(V.tensor_scalar(csum[:, j, :], csum[:, j, :], 1.0 / D, RMS_EPS, ALU.mult, ALU.add))
                    inverse_root(dve, nc, vlink, i, csum[:, j, :], cinv[:, j, :], ctmp[:, j, :])
                    link(V.tensor_scalar(cscale[:, j, :], cinv[:, j, :], D ** -0.5, None, ALU.mult))
                    for k, bank in enumerate((small[j % GB], wide[j % GB], gates[j % GB])):
                        dve.wait_ge(vproj.sem, vproj.at(i, j * KT + k + 1))
                        V.tensor_scalar(v[:, j, k, 0:D], bank[0:KP, 0:D], cinv[:, j, k:k + 1], None, ALU.mult).then_inc(v_sb.sem, 1)

                def norm(r, pair):
                    both = slice(pair[0], pair[0] + GB)
                    dve.wait_ge(s_sq.sem, s_sq.at(i, r * QB + pair[-1] + 1))
                    link(V.tensor_scalar(ssum[:, both], ssum[:, both], 1.0 / D, RMS_EPS, ALU.mult, ALU.add))
                    inverse_root(dve, nc, vlink, i, ssum[:, both], sinv[:, both], stmp[:, both])
                    for j in pair:
                        V.tensor_scalar(sn[:, j, :], slots(r, j), sinv[:, j:j + 1], None, ALU.mult).then_inc(sn_done.sem, 1)

                def front(r, pair):
                    for j in pair:
                        dve.wait_ge(score.sem, score.at(i, r * QB + j + 1))
                        link(V.tensor_reduce(smax[:, j, :], wide[j % GB][0:KP, 0:KT * T].rearrange("p (k t) -> p k t", k=KT), AX.X, ALU.max))
                        V.scalar_tensor_tensor(nmax[:, j, :], smax[:, j, :], -1.0, cscale[:, j, :], ALU.mult, ALU.mult).then_inc(max_done.sem, 1)
                    for j in pair:
                        dve.wait_ge(exp_done.sem, exp_done.at(i, r * QB + j + 1))
                        link(V.reciprocal(einv[:, j, :], esum[:, j, :]))
                        V.tensor_tensor(e[:, j, :, :], e[:, j, :, :], einv[:, j, :].unsqueeze(2).broadcast_to([KP, KT, T]), ALU.mult).then_inc(attn.sem, 1)

                def back(r, pair):
                    for j in pair:
                        dve.wait_ge(u_done.sem, u_done.at(i, r * QB + j + 1))
                        link(V.tensor_scalar(den[:, j:j + 1], small[j % GB][0:T, D:D + 1], RMS_EPS, None, ALU.add))
                        link(V.reciprocal(den[:, j:j + 1], den[:, j:j + 1]))
                        V.tensor_scalar(upd[:, j, :], small[j % GB][0:T, 0:D], den[:, j:j + 1], None, ALU.mult).then_inc(upd_done.sem, 1)
                    for j in pair:
                        dve.wait_ge(gru.sem, gru.at(i, r * QB + j + 1))
                        V.tensor_tensor(hn[:, j, :], news[j % GB][0:T, D:2 * D], bhh[:, 2 * D:3 * D], ALU.add)
                        link(V.tensor_tensor(xn[:, j, :], news[j % GB][0:T, 0:D], bih[:, 2 * D:3 * D], ALU.add))
                        V.tensor_tensor(rz[:, j, :], gates[j % GB][0:T, :], bih[:, 0:2 * D], ALU.add).then_inc(rz_sb.sem, 1)
                    for j in pair:
                        dve.wait_ge(rz_tanh.sem, rz_tanh.at(i, r * QB + j + 1))
                        link(V.tensor_scalar(rz[:, j, :], rz[:, j, :], 0.5, 0.5, ALU.mult, ALU.add))
                        link(V.tensor_tensor(hn[:, j, :], rz[:, j, 0:D], hn[:, j, :], ALU.mult))
                        V.tensor_tensor(xn[:, j, :], xn[:, j, :], hn[:, j, :], ALU.add).then_inc(pre_n.sem, 1)
                    for j in pair:
                        dve.wait_ge(n_tanh.sem, n_tanh.at(i, r * QB + j + 1))
                        link(V.tensor_tensor(t[:, j, :], slots(r, j), cand[:, j, :], ALU.subtract))
                        link(V.tensor_tensor(t[:, j, :], t[:, j, :], rz[:, j, D:2 * D], ALU.mult))
                        V.tensor_tensor(s[:, j, :], t[:, j, :], cand[:, j, :], ALU.add).then_inc(s_done.sem, 1)

                for pair in pairs:
                    norm(0, pair)
                for r in range(ROUNDS):
                    for pair in pairs:
                        front(r, pair)
                    for pair in pairs:
                        back(r, pair)
                        if r + 1 < ROUNDS:
                            norm(r + 1, pair)
                dve.wait_ge(saved.sem, saved.at(i, 0))
                dve.wait_ge(s_done.sem, s_done.at(i, N))
                link(V.tensor_tensor(t[:, :, :], x4[:, :, :], s[:, :, :], ALU.add))
                layer_norms(dve, nc, vlink, i, [t[:, j, :] for j in range(QB)], stats, [x5[:, j, :] for j in range(QB)], x5_done)
            assert vlink.seen == vlink.per, vlink.seen

DFF = 1024
FT = DFF // 128
NT = B * T // 128
TOP = 24
XW = D + 2
MOST = 2 * NT + E - 1
PER = 6
JOBS = (MOST + PER - 1) // PER * PER
NV = E + 1
HASH_INPUTS = ["ident", "W1", "b1", "W2", "L1_ffn_b2", "count_to", "eights", "expert_no", "expert_before", "token_no", "before128", "ones128",
               "v_no", "v_before", "tile_start", "pair_before", "pair_is", "pair_base", "pair_v", "pair_vals", "job_no"]


def hashed_phase(nc, d, own):
    ctx = ExitStack()
    with ctx:
        def sb(name, shape, dt=F32):
            return ctx.enter_context(nc.sbuf_tensor("e_" + name, shape, dt))

        def sem(name, per, unit=1, early=False):
            return Steps(own("e_" + name, early), per, unit, early)

        ident = sb("ident", [128, 128])
        before128 = sb("before128", [128, 128])
        ones128 = sb("ones128", [128, 128])
        token_no = sb("token_no", [128, NT])
        count_to = sb("count_to", [128, TOP])
        eights = sb("eights", [128, TOP // 4])
        expert_no = sb("expert_no", [128, E])
        expert_before = sb("expert_before", [128, E])
        v_no = sb("v_no", [128, NV + 1])
        v_before = sb("v_before", [128, NV + 1])
        tile_start = sb("tile_start", [128, NT])
        pair_before = sb("pair_before", [128, NT])
        pair_is = sb("pair_is", [128, NT])
        pair_base = sb("pair_base", [128, 1])
        pair_v = sb("pair_v", [128, 1])
        pair_vals = sb("pair_vals", [128, 3])
        job_no = sb("job_no", [128, JOBS + 2])
        b2 = sb("b2", [E, D])
        x = sb("x", [128, NT, XW])
        xt = sb("xt", [128, NT, KC, 128])
        acc = sb("acc", [128, NT, D])
        h1 = sb("h1", [128, NT])
        h2 = sb("h2", [128, NT])
        h3 = sb("h3", [128, NT])
        cmp = sb("cmp", [128, NT, TOP])
        is_h = sb("is_h", [128, E, NT])
        total = sb("total", [128, E, NT])
        upto = sb("upto", [128, E, NT])
        place = sb("place", [128, NT])
        place_i = sb("place_i", [128, NT], I32)
        lowest = sb("lowest", [128, NT])
        highest = sb("highest", [128, NT])
        reach = sb("reach", [128, 4, NT])
        pair = sb("pair", [128, 8])
        is_job = sb("is_job", [128, JOBS + 2])
        table = sb("table", [1, 3, JOBS + 2], I32)
        origin = sb("origin", [128, NT], I32)
        eq1 = sb("eq1", [128, NT, NV + 1])
        share = sb("share", [128, NT, E])
        share_v = sb("share_v", [128, NT, NV + 1])
        share_t = sb("share_t", [E, NT, 128])
        w1 = sb("w1", [128, E * KC * DFF])
        w2 = sb("w2", [128, E * FT * D])
        b1 = sb("b1", [128, E * FT])
        xj = sb("xj", [128, 2, KC, 128])
        b1j = sb("b1j", [128, 3, FT])
        hid = sb("hid", [128, DFF])
        hid_t = sb("hid_t", [128, 2, FT, 128])
        stats = sb("stats", [128, NT, 10])
        up = [ctx.enter_context(nc.psum_tensor(f"e_up{n}", [128, 512], F32)) for n in range(4)]
        turn = [ctx.enter_context(nc.psum_tensor(f"e_turn{n}", [128, 512], F32)) for n in range(2)]
        down = [ctx.enter_context(nc.psum_tensor(f"e_down{n}", [128, 512], F32)) for n in range(2)]

        first = sem("first", 1)
        loaded = sem("loaded", 1, 16)
        hashed = sem("hashed", 1)
        ranked = sem("ranked", 1)
        placed = sem("placed", 1)
        sent = sem("sent", 1, 16)
        sorted_in = sem("sorted_in", 1, 16)
        jobs_known = sem("jobs_known", 1)
        drawn = sem("drawn", 1)
        tabled = sem("tabled", 1)
        turned = sem("turned", 1)
        xt_sb = sem("xt_sb", 1)
        shares = sem("shares", 1)
        share_turned = sem("share_turned", 1)
        share_sb = sem("share_sb", 1)
        bias_done = sem("bias_done", 1)
        acc0 = sem("acc0", 1)
        job_in = sem("job_in", PER)
        up_done = sem("up_done", PER * 2, early=3)
        hid_sb = sem("hid_sb", PER * 2, early=3)
        hid_turned = sem("hid_turned", PER * 2, early=True)
        relu_done = sem("relu_done", PER * 2, early=3)
        down_done = sem("down_done", PER, early=3)
        added = sem("added", PER, early=3)
        normed = sem("normed", NT)
        stored = sem("stored", 1, 16)
        vlink = sem("vlink", 1)
        block = ctx.enter_context(nc.Block())
        loads = [(x[:, :, 0:D], d["s_x5_by_tile"]), (token_no[:, :], d["token_no"]), (ident[:, :], d["ident"]), (count_to[:, :], d["count_to"]),
                 (eights[:, :], d["eights"]), (expert_no[:, :], d["expert_no"]), (expert_before[:, :], d["expert_before"]), (b2[:, :], d["L1_ffn_b2"]),
                 (before128[:, :], d["before128"]), (ones128[:, :], d["ones128"]), (v_no[:, :], d["v_no"]), (v_before[:, :], d["v_before"]),
                 (tile_start[:, :], d["tile_start"]), (pair_before[:, :], d["pair_before"]), (pair_is[:, :], d["pair_is"]),
                 (pair_base[:, :], d["pair_base"]), (pair_v[:, :], d["pair_v"]), (pair_vals[:, :], d["pair_vals"]), (job_no[:, :], d["job_no"])]
        LW = 3 * E

        @block.sync
        def _(sp):
            for dst, src in loads:
                sp.dma_start(dst, src).then_inc(first.sem, 16)
            for e in range(E):
                sp.dma_start(w1[:, e * KC * DFF:(e + 1) * KC * DFF].rearrange("p (k f) -> p k f", k=KC), d["W1"][e]).then_inc(loaded.sem, 16)
                sp.dma_start(b1[:, e * FT:(e + 1) * FT], d["b1"][e]).then_inc(loaded.sem, 16)
            for e in range(E):
                sp.dma_start(w2[:, e * FT * D:(e + 1) * FT * D].rearrange("p (f o) -> p f o", f=FT), d["W2"][e]).then_inc(loaded.sem, 16)

        @block.gpsimd
        def _(pool):
            pool.wait_ge(placed.sem, 1)
            for t in range(NT):
                pool.indirect_dma_start(d["s_sorted"], bass.IndirectOffsetOnAxis(ap=place_i[:, t:t + 1], axis=0), x[:, t, :], None).then_inc(sent.sem, 16)
            pool.wait_ge(sent.sem, 16 * NT)
            pool.dma_start(x[:, :, :], d["s_sorted_by_tile"]).then_inc(sorted_in.sem, 16)
            for t in range(NT):
                pool.wait_ge(normed.sem, t + 1)
                pool.indirect_dma_start(d["out_rows"], bass.IndirectOffsetOnAxis(ap=origin[:, t:t + 1], axis=0), acc[:, t, :], None).then_inc(stored.sem, 16)
            pool.wait_ge(stored.sem, 16 * NT)

        @block.tensor
        def _(pe):
            mm = nc.tensor.matmul
            pe.wait_ge(first.sem, 16 * len(loads))
            pe.wait_ge(hashed.sem, 1)
            flat = is_h[:, :, :].rearrange("p e t -> p (e t)")
            mm(up[0][:, 0:E * NT], before128[:, :], flat, start=True, stop=True)
            mm(up[1][:, 0:E * NT], ones128[:, :], flat, start=True, stop=True).then_inc(ranked.sem, 1)
            pe.wait_ge(jobs_known.sem, 1)
            for c in range(3):
                last = mm(down[0][0:1, c * (JOBS + 2):(c + 1) * (JOBS + 2)], pair_vals[:, c:c + 1], is_job[:, :], start=True, stop=True)
            last.then_inc(drawn.sem, 1)
            pe.wait_ge(sorted_in.sem, 16)
            for t in range(NT):
                for kc in range(KC):
                    k = t * KC + kc
                    if k % 4 == 0 and k >= 16:
                        pe.wait_ge(xt_sb.sem, k // 4 - 3)
                    last = nc.tensor.transpose(up[k // 4 % 4][:, (k % 4) * 128:(k % 4 + 1) * 128], x[:, t, kc * 128:(kc + 1) * 128], ident[:, :])
                    if k % 4 == 3:
                        last.then_inc(turned.sem, 1)
            pe.wait_ge(shares.sem, 1)
            pe.wait_ge(tabled.sem, 1)
            pe.wait_ge(xt_sb.sem, NT * KC // 4)
            for t in range(NT):
                last = nc.tensor.transpose(up[t // 4][0:E, (t % 4) * 128:(t % 4 + 1) * 128], share[:, t, :], ident[:, :])
            last.then_inc(share_turned.sem, 1)
            pe.wait_ge(share_sb.sem, 1)
            for t in range(NT):
                if t >= 2:
                    pe.wait_ge(acc0.sem, t - 1)
                mm(down[t % 2][:, 0:D], share_t[:, t, :], b2[:, :], start=True, stop=True).then_inc(bias_done.sem, 1)
            pe.wait_ge(acc0.sem, NT)
            pe.wait_ge(loaded.sem, 16 * LW)

            def expert(i, k):
                return pe.value_load(table[0:1, 1, bass.ds(i * PER + k, 1)], min_val=0, max_val=E - 1)

            def rise(i, k, e):
                pe.wait_ge(job_in.sem, job_in.at(i, k + 1))
                pe.wait_ge(hid_sb.sem, hid_sb.at(i, 2 * k - 2))
                for half in range(2):
                    for kc in range(KC):
                        last = mm(up[(2 * k + half) % 4][:, :], xj[:, k % 2, kc, :], w1[:, bass.ds(e * (KC * DFF) + (kc * DFF + half * 512), 512)], start=kc == 0, stop=kc == KC - 1)
                    last.then_inc(up_done.sem, 1)

            def turn_over(i, k):
                for half in range(2):
                    n = 2 * k + half
                    pe.wait_ge(hid_sb.sem, hid_sb.at(i, n + 1))
                    pe.wait_ge(relu_done.sem, relu_done.at(i, n - 1))
                    for f in range(4):
                        c = half * 512 + f * 128
                        last = nc.tensor.transpose(turn[half][:, f * 128:(f + 1) * 128], hid[:, c:c + 128], ident[:, :])
                    last.then_inc(hid_turned.sem, 1)

            def fall(i, k, e):
                pe.wait_ge(added.sem, added.at(i, k - 1))
                pe.wait_ge(relu_done.sem, relu_done.at(i, 2 * k + 2))
                for f in range(FT):
                    last = mm(down[k % 2][:, 0:D], hid_t[:, k % 2, f, :], w2[:, bass.ds(e * (FT * D) + f * D, D)], start=f == 0, stop=f == FT - 1)
                last.then_inc(down_done.sem, 1)

            rise(0, 0, expert(0, 0))
            with pe.Fori(0, JOBS // PER) as i:
                own_e = expert(i, 0)
                for k in range(PER):
                    next_e = expert(i, k + 1)
                    turn_over(i, k)
                    rise(i, k + 1, next_e)
                    fall(i, k, own_e)
                    own_e = next_e

        @block.scalar
        def _(act):
            fn = nc.scalar.activation
            for k in range(NT * KC // 4):
                act.wait_ge(turned.sem, k + 1)
                fn(xt[:, 2 * k:2 * k + 2, :, :].rearrange("p t k c -> p (t k c)"), up[k % 4][:, :], ACT.Copy).then_inc(xt_sb.sem, 1)
            act.wait_ge(share_turned.sem, 1)
            for k in range((NT + 3) // 4):
                m = min(4, NT - 4 * k)
                last = fn(share_t[:, 4 * k:4 * k + m, :].rearrange("p t c -> p (t c)"), up[k][0:E, 0:m * 128], ACT.Copy)
            last.then_inc(share_sb.sem, 1)
            with act.Fori(0, JOBS // PER) as i:
                for k in range(PER):
                    act.wait_ge(down_done.sem, down_done.at(i, k - 1))
                    for f in range(FT):
                        if f % 4 == 0:
                            act.wait_ge(hid_turned.sem, hid_turned.at(i, 2 * k + f // 4 + 1))
                        last = fn(hid_t[:, k % 2, f, :], turn[f // 4][:, (f % 4) * 128:(f % 4 + 1) * 128], ACT.Relu, bias=b1j[:, k % 3, f:f + 1])
                        if f % 4 == 3:
                            last.then_inc(relu_done.sem, 1)

        @block.vector
        def _(dve):
            V = nc.vector
            link = lambda ins: vlink.chain(dve, 0, ins)
            dve.wait_ge(first.sem, 16 * len(loads))
            link(V.tensor_tensor(h1[:, :], x[:, :, 0], x[:, :, 1], ALU.add))
            link(V.tensor_scalar(h2[:, :], h1[:, :], -1.0, None, ALU.mult))
            link(V.tensor_tensor(h2[:, :], h1[:, :], h2[:, :], ALU.max))
            link(V.tensor_tensor(cmp[:, :, :], h2[:, :].unsqueeze(2).broadcast_to([128, NT, TOP]), count_to[:, :].unsqueeze(1).broadcast_to([128, NT, TOP]), ALU.is_ge))
            link(V.tensor_reduce(h3[:, :], cmp[:, :, :], AX.X, ALU.add))
            link(V.tensor_scalar(h1[:, :], h1[:, :], 0.0, None, ALU.is_lt))
            link(V.tensor_scalar(h1[:, :], h1[:, :], -2.0, 1.0, ALU.mult, ALU.add))
            link(V.tensor_tensor(h1[:, :], h1[:, :], h3[:, :], ALU.mult))
            link(V.tensor_scalar(h1[:, :], h1[:, :], float(TOP), None, ALU.add))
            link(V.tensor_tensor(cmp[:, :, 0:TOP // 4], h1[:, :].unsqueeze(2).broadcast_to([128, NT, TOP // 4]), eights[:, :].unsqueeze(1).broadcast_to([128, NT, TOP // 4]), ALU.is_ge))
            link(V.tensor_reduce(h3[:, :], cmp[:, :, 0:TOP // 4], AX.X, ALU.add))
            link(V.scalar_tensor_tensor(x[:, :, D + 1], h3[:, :], -8.0, h1[:, :], ALU.mult, ALU.add))
            V.tensor_copy(x[:, :, D], token_no[:, :])
            by_hash = lambda a: a.unsqueeze(1).broadcast_to([128, E, NT])
            V.tensor_tensor(is_h[:, :, :], by_hash(x[:, :, D + 1]), expert_no[:, :].unsqueeze(2).broadcast_to([128, E, NT]), ALU.is_equal).then_inc(hashed.sem, 1)
            dve.wait_ge(ranked.sem, 1)
            flat = lambda a: a.rearrange("p e t -> p (e t)")
            link(V.tensor_copy(flat(total[:, :, :]), up[1][:, 0:E * NT]))
            link(V.tensor_tensor_scan(flat(upto[:, :, :]), ones128[:, 0:E * NT], flat(total[:, :, :]), 0.0, ALU.mult, ALU.add))
            link(V.tensor_tensor(flat(total[:, :, :]), flat(upto[:, :, :]), flat(total[:, :, :]), ALU.subtract))
            link(V.tensor_tensor(flat(total[:, :, :]), up[0][:, 0:E * NT], flat(total[:, :, :]), ALU.add))
            link(V.tensor_tensor(total[:, :, :], total[:, :, :], is_h[:, :, :], ALU.mult))
            link(V.tensor_reduce(place[:, :], total[:, :, :].rearrange("p e t -> p t e"), AX.X, ALU.add))
            V.tensor_copy(place_i[:, :], place[:, :]).then_inc(placed.sem, 1)
            ends = upto[:, :, NT - 1].unsqueeze(1).broadcast_to([128, NT, E])
            c8 = cmp[:, :, 0:E]
            for out, shift in ((lowest, 0.0), (highest, 127.0)):
                link(V.tensor_scalar(h1[:, :], tile_start[:, :], shift, None, ALU.add))
                link(V.tensor_tensor(c8, h1[:, :].unsqueeze(2).broadcast_to([128, NT, E]), ends, ALU.is_ge))
                link(V.tensor_reduce(out[:, :], c8, AX.X, ALU.add))
            link(V.tensor_tensor(h1[:, :], highest[:, :], lowest[:, :], ALU.subtract))
            V.tensor_tensor(reach[:, 0, :], h1[:, :], pair_before[:, :], ALU.mult)
            V.tensor_tensor(reach[:, 1, :], lowest[:, :], pair_is[:, :], ALU.mult)
            link(V.tensor_tensor(reach[:, 2, :], highest[:, :], pair_is[:, :], ALU.mult))
            link(V.tensor_reduce(pair[:, 0:3], reach[:, 0:3, :], AX.X, ALU.add))
            link(V.tensor_tensor(pair[:, 3:4], pair[:, 0:1], pair_base[:, :], ALU.add))
            link(V.tensor_tensor(pair[:, 3:4], pair[:, 3:4], pair[:, 1:2], ALU.subtract))
            link(V.tensor_tensor(pair[:, 4:5], pair_v[:, :], pair[:, 1:2], ALU.is_ge))
            link(V.tensor_scalar(pair[:, 5:6], pair[:, 2:3], 1.0, None, ALU.add))
            link(V.tensor_tensor(pair[:, 5:6], pair[:, 5:6], pair_v[:, :], ALU.is_ge))
            link(V.tensor_tensor(pair[:, 4:5], pair[:, 4:5], pair[:, 5:6], ALU.mult))
            V.tensor_scalar(is_job[:, :], job_no[:, :], pair[:, 3:4], pair[:, 4:5], ALU.is_equal, ALU.mult).then_inc(jobs_known.sem, 1)
            dve.wait_ge(drawn.sem, 1)
            V.tensor_copy(table[:, 0:2, :].rearrange("p c n -> p (c n)"), down[0][0:1, 0:2 * (JOBS + 2)]).then_inc(tabled.sem, 1)
            V.tensor_scalar(table[:, 2, :], down[0][0:1, 2 * (JOBS + 2):3 * (JOBS + 2)], float(NV), None, ALU.add).then_inc(tabled.sem, 1)
            dve.wait_ge(sorted_in.sem, 16)
            V.tensor_copy(origin[:, :], x[:, :, D])
            for out, own_no, next_no, n in ((share, expert_no, expert_before, E), (share_v, v_no, v_before, NV + 1)):
                of_h = x[:, :, D + 1].unsqueeze(2).broadcast_to([128, NT, n])
                V.tensor_tensor(eq1[:, :, 0:n], of_h, own_no[:, :].unsqueeze(1).broadcast_to([128, NT, n]), ALU.is_equal)
                link(V.tensor_tensor(out[:, :, :], of_h, next_no[:, :].unsqueeze(1).broadcast_to([128, NT, n]), ALU.is_equal))
                link(V.tensor_tensor(out[:, :, :], out[:, :, :], eq1[:, :, 0:n], ALU.add))
                V.tensor_scalar(out[:, :, :], out[:, :, :], 0.5, None, ALU.mult).then_inc(shares.sem, 1)
            for t in range(NT):
                dve.wait_ge(bias_done.sem, t + 1)
                V.tensor_tensor(acc[:, t, :], down[t % 2][:, 0:D], x[:, t, 0:D], ALU.add).then_inc(acc0.sem, 1)
            dve.wait_ge(acc0.sem, NT)
            dve.wait_ge(shares.sem, 2)
            dve.wait_ge(tabled.sem, 2)
            dve.wait_ge(xt_sb.sem, NT * KC // 4)
            dve.wait_ge(loaded.sem, 16 * LW)

            def fetch(i, k):
                tile = dve.value_load(table[0:1, 0, bass.ds(i * PER + k, 1)], min_val=0, max_val=NT - 1)
                e = dve.value_load(table[0:1, 1, bass.ds(i * PER + k, 1)], min_val=0, max_val=E - 1)
                if not (isinstance(i, int) and k < 2):
                    dve.wait_ge(up_done.sem, up_done.at(i, 2 * k - 2))
                V.tensor_scalar(xj[:, k % 2, :, :].rearrange("p k c -> p (k c)"), xt[:, bass.ds(tile, 1), :, :].rearrange("p t k c -> p (t k c)"), 1.0, None, ALU.mult)
                if not (isinstance(i, int) and k < 2):
                    dve.wait_ge(relu_done.sem, relu_done.at(i, 2 * k - 4))
                V.tensor_scalar(b1j[:, k % 3, :], b1[:, bass.ds(e * FT, FT)], 1.0, None, ALU.mult).then_inc(job_in.sem, 1)

            def take(i, k):
                if not (isinstance(i, int) and k == 0):
                    dve.wait_ge(hid_turned.sem, hid_turned.at(i, 2 * k))
                for half in range(2):
                    n = 2 * k + half
                    dve.wait_ge(up_done.sem, up_done.at(i, n + 1))
                    V.tensor_copy(hid[:, half * 512:(half + 1) * 512], up[n % 4][:, :]).then_inc(hid_sb.sem, 1)

            def gather(i, k):
                tile = dve.value_load(table[0:1, 0, bass.ds(i * PER + k, 1)], min_val=0, max_val=NT - 1)
                column = dve.value_load(table[0:1, 2, bass.ds(i * PER + k, 1)], min_val=0, max_val=NV)
                dve.wait_ge(down_done.sem, down_done.at(i, k + 1))
                dve.wait_ge(added.sem, added.at(i, k))
                V.scalar_tensor_tensor(acc[:, bass.ds(tile, 1), :].rearrange("p t o -> p (t o)"), down[k % 2][:, 0:D],
                                       share_v[:, bass.ds(tile, 1), bass.ds(column, 1)].rearrange("p t o -> p (t o)"),
                                       acc[:, bass.ds(tile, 1), :].rearrange("p t o -> p (t o)"), ALU.mult, ALU.add).then_inc(added.sem, 1)

            fetch(0, 0)
            fetch(0, 1)
            take(0, 0)
            with dve.Fori(0, JOBS // PER) as i:
                for k in range(PER):
                    fetch(i, k + 2)
                    take(i, k + 1)
                    gather(i, k)
            dve.wait_ge(added.sem, added.at(JOBS // PER, 0))
            layer_norms(dve, nc, vlink, 0, [acc[:, t, :] for t in range(NT)], stats, [acc[:, t, :] for t in range(NT)], normed)


def _constants():
    import numpy as np

    inv = (1.0 / 10000.0 ** (np.arange(0, DH, 2, dtype=np.float32) / DH)).astype(np.float32)
    ang = np.arange(T, dtype=np.float32)[:, None] * inv[None, :]
    s = np.sin(ang)
    c = {
        "cos": np.concatenate([np.cos(ang)] * 2, axis=1), "sin": np.concatenate([-s, s], axis=1),
        "ident": np.eye(128), "earlier": np.triu(np.ones((T, T)), 1), "ones": np.ones((T, T)),
        "count_to": np.tile(np.arange(1, TOP + 1), (128, 1)), "eights": np.tile(np.arange(8, 2 * TOP + 1, 8), (128, 1)),
        "expert_no": np.tile(np.arange(E), (128, 1)), "expert_before": np.tile((np.arange(E) - 1) % E, (128, 1)),
        "rev": np.tile(np.arange(E, 0, -1), (T, 1)), "slot_no": np.tile(np.arange(CAP), (T, 1)),
        "causal": np.triu(np.full((T, T), NEG), 1), "row_of": np.arange(XD)[:, None, None] - RANK == np.arange(2 * NST)[None, :, None] + np.zeros((1, 1, 128)),
        "maskrow": (np.arange(128) % PAD == DH)[None, :],
    }
    wide = lambda v: np.tile(v, (128, 1))
    v_no = np.append(np.arange(NV), -5)
    tile, v = np.divmod(np.arange(128), NV)
    v = np.where(tile < NT, v, -5)
    c.update(
        token_no=np.arange(B * T).reshape(NT, 128).T, before128=np.triu(np.ones((128, 128)), 1), ones128=np.ones((128, 128)),
        v_no=wide(v_no), v_before=wide(np.append(np.arange(NV) - 1, -5)), tile_start=wide(128 * np.arange(NT)),
        pair_before=np.arange(NT)[None, :] < tile[:, None], pair_is=np.arange(NT)[None, :] == tile[:, None],
        pair_base=(2 * tile + v)[:, None], pair_v=v[:, None], pair_vals=np.stack([tile, v % E, v - NV], axis=1), job_no=wide(np.arange(JOBS + 2)),
    )
    return {k: np.ascontiguousarray(v, dtype=np.float32) for k, v in c.items()}


def _layouts(a):
    import numpy as np

    def chunks(w):
        return w.reshape(-1, 128, w.shape[1]).transpose(1, 0, 2)

    def pad_heads(w):
        out = np.zeros(w.shape[:-1] + (HEADS, PAD), w.dtype)
        out[..., :DH] = w.reshape(w.shape[:-1] + (HEADS, DH))
        return out

    def pad_rows(w):
        out = np.zeros((HEADS, PAD, w.shape[1]), w.dtype)
        out[:, :DH] = w.reshape(HEADS, DH, -1)
        return out.reshape(HG, 128, -1).transpose(1, 0, 2)

    def columns(v):
        return v.reshape(-1, 128).T

    rows = lambda v: v.reshape(DT, 128, -1).transpose(1, 0, 2)
    bq = pad_heads(a["L0_xattn_bq"])
    bq[:, DH] = 1.0
    out = dict(a)
    out.update(
        xt=a["x"].reshape(B, T, KC, 128).transpose(0, 3, 2, 1), ctxt=a["ctx_1024"].reshape(B, S2, KC, 128).transpose(0, 3, 2, 1),
        mask=np.ascontiguousarray(a["mask_BxS2_bk0"]).reshape(-1).view(np.int32),
        wqkv=chunks(a["L0_attn_qkv_w"].T), wproj=pad_rows(a["L0_attn_proj_w"].T),
        wqx=chunks(pad_heads(a["L0_xattn_Wq"].T).reshape(D, -1)), bqx=columns(bq.reshape(-1)),
        wkx=chunks(pad_heads(a["L0_xattn_Wk"].T).reshape(D, -1)), bkx=columns(pad_heads(a["L0_xattn_bk"]).reshape(-1)),
        wvx=chunks(a["L0_xattn_Wv"].T), wox=pad_rows(a["L0_xattn_Wo"].T), router=chunks(a["L0_ffn_router_w"]),
        w0=a["L0_ffn_w0_kernel"].reshape(E, KC, 128, HID).transpose(0, 2, 1, 3), w1=a["L0_ffn_w1_kernel"].reshape(E, KC, 128, HID).transpose(0, 2, 1, 3),
        wo=a["L0_ffn_wo_kernel"].reshape(E, HT, HP, D).transpose(0, 2, 1, 3),
        win=chunks(a["L1_attn_W_in"].T), convw=rows(a["L1_attn_conv_w"].reshape(DIN, TAPS)), convb=columns(a["L1_attn_conv_b"]),
        wx=chunks(a["L1_attn_W_x"].T), wdt=a["L1_attn_W_dt"].T, bdt=columns(a["L1_attn_b_dt"]), alog=rows(a["L1_attn_A_log"]),
        ctx_rows=a["ctx_1024"].reshape(B, KT, KP, D).transpose(0, 2, 1, 3), wk=chunks(a["L1_xattn_Wk"].T), wv=chunks(a["L1_xattn_Wv"].T),
        wq=chunks(a["L1_xattn_Wq"].T), wih=chunks(a["L1_xattn_gru_wih"].T), whh=chunks(a["L1_xattn_gru_whh"].T),
        snorm=columns(a["L1_xattn_slot_norm_w"]), inorm=columns(a["L1_xattn_input_norm_w"]),
        W1=a["L1_ffn_W1"].reshape(E, KC, 128, DFF).transpose(0, 2, 1, 3), W2=a["L1_ffn_W2"].reshape(E, FT, 128, D).transpose(0, 2, 1, 3),
        b1=a["L1_ffn_b1"].reshape(E, FT, 128).transpose(0, 2, 1),
        dp=columns(a["L1_attn_Dp"]), wout=chunks(a["L1_attn_W_out"].T),
    )
    out.update(_constants())
    return out


def _views(d):
    if "mask" in d:
        d["mask"] = d["mask"].bitcast(U8).rearrange("(b o s) -> b o s", o=1, s=S2)
    if "s_xe" in d:
        d["s_xe_by_expert"] = d["s_xe"].rearrange("g p k (e c) -> e k p g c", e=E)
    if "s_eo" in d:
        d["s_eo_by_expert"] = d["s_eo"].rearrange("(s g) (e c) d -> e g c s d", g=2, e=E)
        d["s_eo_by_group"] = d["s_eo"].rearrange("g (s p) d -> g p s d", p=T)
    if "s_x4" in d:
        d["s_x4_by_four"] = d["s_x4"].rearrange("(i b) t d -> i t b d", b=QB)
    if "s_x5" in d:
        d["s_x5_by_four"] = d["s_x5"].rearrange("(i b) t d -> i t b d", b=QB)
        d["s_x5_by_tile"] = d["s_x5"].rearrange("b t d -> (b t) d").rearrange("(n p) d -> p n d", p=128)
    if "s_sorted" in d:
        d["s_sorted_by_tile"] = d["s_sorted"].rearrange("(n p) d -> p n d", p=128)
    if "out" in d:
        d["out_rows"] = d["out"].rearrange("b t d -> (b t) d")


_A = ["xt", "x", "ctxt", "mask", "wqkv", "L0_attn_qkv_b", "wproj", "L0_attn_proj_b", "wqx", "bqx", "wkx", "bkx", "wvx", "L0_xattn_bv",
      "wox", "L0_xattn_bo", "router", "cos", "sin", "ident", "earlier", "ones", "rev", "slot_no", "causal", "maskrow"]
_B = ["w0", "w1", "wo"]
_C = ["win", "convw", "convb", "wx", "wdt", "bdt", "alog", "dp", "wout", "row_of"]
_INS = list(dict.fromkeys(_A + _B + _C + SLOT_INPUTS + HASH_INPUTS))
_SCRATCH = {"s_x2": (G, T, GB, D), "s_xe": (G, 128, KC, SL), "s_ct": (G, T, GB, ST, T), "s_eo": (G, SL, D), "s_x4": (B, T, D), "s_x5": (B, T, D), "s_sorted": (B * T, XW)}


def kernel(**inputs):
    import numpy as np
    import concourse.bacc as bacc
    from concourse.bass_utils import run_bass_kernel_spmd

    nc = bacc.Bacc("TRN2", target_bir_lowering=False, num_devices=1)
    laid = _layouts({k: np.asarray(v) for k, v in inputs.items()})
    arrays = {f"in_{n}": np.ascontiguousarray(laid[n]) for n in _INS}
    d = {n: nc.dram_tensor(f"in_{n}", arrays[f"in_{n}"].shape, mybir.dt.from_np(arrays[f"in_{n}"].dtype), kind="ExternalInput").ap() for n in _INS}
    for n, shape in _SCRATCH.items():
        d[n] = nc.dram_tensor(n, shape, F32, kind="Internal").ap()
    d["out"] = nc.dram_tensor("out", (B, T, D), F32, kind="ExternalOutput").ap()
    _views(d)
    for phase in (attention_phase, expert_phase, mixer_phase, slot_phase, hashed_phase):
        run_phase(nc, phase, d)
    return run_bass_kernel_spmd(nc, [arrays], core_ids=[0]).results[0]["out"]
```

```python
import concourse.bass as bass
from concourse import mybir
from contextlib import ExitStack

F32 = mybir.dt.float32
F32R = mybir.dt.float32r
BF16 = mybir.dt.bfloat16
U8 = mybir.dt.uint8
I32 = mybir.dt.int32
ALU = mybir.AluOpType
ACT = mybir.ActivationFunctionType
AX = mybir.AxisListType

B, T, D = 16, 112, 256
S2 = 375
KC = D // 128
HEADS, DH, PAD = 16, 16, 32
HG = HEADS * PAD // 128
KT, KP = 3, S2 // 3
G, GB = 8, 2
E = 8
CAP = 56
SL = E * CAP
ST = SL // T
HID = 1368
HT, HP = 12, HID // 12
NEG = -1.0e30
LN_EPS = 1e-5


class Steps:

    def __init__(self, sem, per, unit=1, early=False):
        self.sem, self.per, self.unit, self.start, self.seen = sem, per, unit, int(early), 0

    def at(self, i, k):
        assert k * self.unit + self.start > 0 or isinstance(i, int), self.sem.name
        return i * (self.per * self.unit) + (k * self.unit + self.start)

    def chain(self, eng, i, instruction):
        self.seen += 1
        instruction.then_inc(self.sem, 1)
        eng.wait_ge(self.sem, self.at(i, self.seen))


def run_phase(nc, phase, d):
    used = []

    def own(name, early):
        used.append(nc.alloc_semaphore(name=name))
        if early:
            nc.sync.sem_inc(used[-1], int(early))
        return used[-1]

    phase(nc, d, own)
    nc.clear_and_free_semaphores(used)
    nc.all_engine_barrier()


def inverse_root(dve, nc, links, i, value, root, tmp):
    V = nc.vector
    links.chain(dve, i, V.tensor_scalar(root.bitcast(I32), value.bitcast(I32), -0.5, float(0x5F3759DF), ALU.mult, ALU.add))
    k = 1.0
    for step in range(3):
        if value.shape[-1] == 1:
            links.chain(dve, i, V.scalar_tensor_tensor(tmp, root, value, root, ALU.mult, ALU.mult))
        else:
            links.chain(dve, i, V.tensor_tensor(tmp, root, root, ALU.mult))
            links.chain(dve, i, V.tensor_tensor(tmp, tmp, value, ALU.mult))
        if step < 2:
            links.chain(dve, i, V.scalar_tensor_tensor(root, tmp, 3 * k * k, root, ALU.subtract, ALU.mult))
            k = -2 * k ** 3
    links.chain(dve, i, V.tensor_scalar(tmp, tmp, -0.5 / k ** 3, 1.5 / k, ALU.mult, ALU.add))
    links.chain(dve, i, V.tensor_tensor(root, root, tmp, ALU.mult))


def layer_norms(dve, nc, links, i, rows, stats, outs, done):
    for n, t in enumerate(rows):
        last = nc.vector.bn_stats(stats[:, n, 0:6], t)
        if n < len(rows) - 1:
            last.then_inc(links.sem, 1)
    links.seen += len(rows) - 1
    links.chain(dve, i, last)
    nc.vector.memset(stats[:, 0, 9:10], 0.0)
    for n in range(len(rows)):
        last = nc.vector.bn_aggr(stats[:, n, 6:8], stats[:, n, 0:6])
        if n < len(rows) - 1:
            last.then_inc(links.sem, 1)
    links.seen += len(rows) - 1
    links.chain(dve, i, last)
    n = len(rows)
    links.chain(dve, i, nc.vector.tensor_scalar(stats[:, 0:n, 7], stats[:, 0:n, 7], LN_EPS, None, ALU.add))
    inverse_root(dve, nc, links, i, stats[:, 0:n, 7], stats[:, 0:n, 8], stats[:, 0:n, 9])
    for n, (t, out, signal) in enumerate(zip(rows, outs, done)):
        nc.vector.tensor_scalar(out, t, stats[:, n, 6:7], stats[:, n, 8:9], ALU.subtract, ALU.mult).then_inc(signal.sem, 1)


def attention_phase(nc, d, own):
    ctx = ExitStack()
    with ctx:
        def sb(name, shape, dt=F32):
            return ctx.enter_context(nc.sbuf_tensor("a_" + name, shape, dt))

        def sem(name, per, unit=1, early=False):
            return Steps(own("a_" + name, early), per, unit, early)

        wqkv = sb("wqkv", [128, KC, 3 * D])
        bqkv = sb("bqkv", [T, 3 * D])
        wproj = sb("wproj", [128, HG, D])
        bproj = sb("bproj", [T, D])
        wqx = sb("wqx", [128, KC, HG * 128])
        bqx = sb("bqx", [128, HG])
        wkx = sb("wkx", [128, KC, HG * 128])
        bkx = sb("bkx", [128, HG])
        wvx = sb("wvx", [128, KC, D])
        bvx = sb("bvx", [KP, D])
        wox = sb("wox", [128, HG, D])
        box = sb("box", [T, D])
        cos = sb("cos", [T, DH])
        sin = sb("sin", [T, DH])
        ident = sb("ident", [128, 128])
        ident_f = sb("ident_f", [T, T])
        causal_f = sb("causal_f", [T, T])
        maskrow_f = sb("maskrow_f", [1, 128])
        identb = sb("identb", [T, T], BF16)
        causalb = sb("causalb", [T, 4, T], BF16)
        maskrowb = sb("maskrowb", [1, 128], BF16)

        xt = sb("xt", [128, GB, KC, T])
        x = sb("x", [T, GB, D])
        ctxt = sb("ctxt", [128, GB, KC, S2])
        mask8 = sb("mask8", [1, GB, S2], U8)
        maskb = sb("maskb", [1, GB, S2], BF16)

        qkb = sb("qkb", [T, 2 * D])
        rot1 = sb("rot1", [T, 2 * D])
        rot2 = sb("rot2", [T, 2 * D])
        qkp = sb("qkp", [T, 2 * HEADS, PAD])
        vp = sb("vp", [T, HEADS, PAD])
        qc = sb("qc", [128, HG, T])
        kc_t = sb("kc_t", [128, HG, T])
        qt = sb("qt", [128, HG, T])
        rowmax = sb("rowmax", [T, HEADS])
        negmax = sb("negmax", [T, HEADS])
        rowsum = sb("rowsum", [T, HEADS])
        rowinv = sb("rowinv", [T, HEADS])
        inv_wide = sb("inv_wide", [T, HEADS, PAD])
        p = sb("p", [T, 2, 4, T])
        pt = sb("pt", [T, 2, 4, T])
        inv_t = sb("inv_t", [128, HG, T])
        ot = sb("ot", [128, HG, T])
        xb = sb("xb", [T, D])
        t = sb("t", [T, D])
        stats = sb("stats", [T, 1, 10])
        x1 = sb("x1", [T, D])
        x1t = sb("x1t", [128, KC, T])
        ktx = sb("ktx", [128, HG, S2])
        vx = sb("vx", [KP, KT, HEADS, PAD])
        px = sb("px", [T, 4, S2])
        ptx = sb("ptx", [KP, 2, KT, T])
        x2 = sb("x2", [T, GB, D])

        def ps(name, shape):
            return ctx.enter_context(nc.psum_tensor("a_" + name, shape, F32))

        score = [ps(f"score{n}", [128, 512]) for n in range(4)]
        trans = [ps(f"trans{n}", [128, 512]) for n in range(2)]
        outt = ps("outt", [128, 512])
        misc = ps("misc", [128, 512])

        weights = sem("weights", 1)
        ready = sem("ready", 1)
        in_x = [sem(f"in_x{j}", 2, 16) for j in range(GB)]
        in_ctx = [sem(f"in_ctx{j}", 2, 16) for j in range(GB)]
        x_done = sem("x_done", GB, early=True)
        mask_done = sem("mask_done", GB, early=True)
        qkv = sem("qkv", GB, early=True)
        qk_raw = sem("qk_raw", GB)
        qk_taken = sem("qk_taken", GB)
        roped = sem("roped", GB)
        q_t = sem("q_t", GB)
        q_sb = sem("q_sb", GB)
        qk_t = sem("qk_t", GB)
        qk_sb = sem("qk_sb", GB)
        s_done = sem("s_done", GB * HG)
        m_done = sem("m_done", GB * HG)
        p_done = sem("p_done", GB * HG)
        pt_done = sem("pt_done", GB * HG)
        pt_sb = [sem("pt_sb_act", GB * 2), sem("pt_sb_dve", GB * 2)]
        o_done = sem("o_done", GB * 2)
        inv_done = sem("inv_done", GB * 2)
        invt_done = sem("invt_done", GB * 2)
        invt_sb = sem("invt_sb", GB * 2)
        o_sb = sem("o_sb", GB * 2, early=True)
        proj = sem("proj", GB * 2)
        x1_done = sem("x1_done", GB)
        x1t_done = sem("x1t_done", GB)
        x1t_sb = sem("x1t_sb", GB)
        kx = sem("kx", GB * HG)
        kx_sb = sem("kx_sb", GB * HG)
        vxp = sem("vxp", GB * KT, early=True)
        vx_sb = sem("vx_sb", GB * KT, early=True)
        qx = sem("qx", GB)
        qx_sb = sem("qx_sb", GB)
        sx = sem("sx", GB * HEADS)
        mx = sem("mx", GB * HEADS // 2)
        pxd = sem("pxd", GB * HEADS, early=True)
        ptxd = sem("ptxd", GB * HEADS)
        ptx_sb = [sem("ptx_sb_dve", GB * HEADS // 2), sem("ptx_sb_act", GB * HEADS // 2)]
        x2_done = sem("x2_done", GB)
        stored = sem("stored", 1, 16)
        saved = sem("saved", 1, early=True)
        vlink = sem("vlink", 78)
        vfirst = sem("vfirst", 1)
        block = ctx.enter_context(nc.Block())

        def column(h):
            return 4 * (h % 4) + h // 4

        loads = [
            (wqkv[:, :, :], d["wqkv"]), (bqkv[:, :], d["L0_attn_qkv_b"].partition_broadcast(T)),
            (wproj[:, :, :], d["wproj"]), (bproj[:, :], d["L0_attn_proj_b"].partition_broadcast(T)),
            (wqx[:, :, :], d["wqx"]), (bqx[:, :], d["bqx"]), (wkx[:, :, :], d["wkx"]), (bkx[:, :], d["bkx"]),
            (wvx[:, :, :], d["wvx"]), (bvx[:, :], d["L0_xattn_bv"].partition_broadcast(KP)),
            (wox[:, :, :], d["wox"]), (box[:, :], d["L0_xattn_bo"].partition_broadcast(T)),
            (cos[:, :], d["cos"]), (sin[:, :], d["sin"]),
            (ident[:, :], d["ident"]), (ident_f[:, :], d["ident"][0:T, 0:T]),
            (causal_f[:, :], d["causal"]), (maskrow_f[:, :], d["maskrow"]),
        ]

        @block.sync
        def _(sp):
            for dst, src in loads:
                sp.dma_start(dst, src).then_inc(weights.sem, 16)
            with sp.Fori(0, G) as i:
                for j in range(GB):
                    sp.wait_ge(qkv.sem, qkv.at(i, 0))
                    sp.wait_ge(x_done.sem, x_done.at(i, 0))
                    sp.dma_start(xt[:, j, :, :], d["xt"][i * GB + j]).then_inc(in_x[j].sem, 16)
                    sp.dma_start(x[:, j, :], d["x"][i * GB + j]).then_inc(in_x[j].sem, 16)
                    sp.wait_ge(vxp.sem, vxp.at(i, 0))
                    sp.wait_ge(mask_done.sem, mask_done.at(i, 0))
                    sp.dma_start(ctxt[:, j, :, :], d["ctxt"][i * GB + j]).then_inc(in_ctx[j].sem, 16)
                    sp.dma_start(mask8[:, j, :], d["mask"][i * GB + j]).then_inc(in_ctx[j].sem, 16)
            sp.wait_ge(qkv.sem, qkv.at(G, 0))
            sp.wait_ge(x_done.sem, x_done.at(G, 0))
            sp.dma_start(xt[:, 0, :, :], d["xt"][0]).then_inc(in_x[0].sem, 16)
            sp.dma_start(x[:, 0, :], d["x"][0]).then_inc(in_x[0].sem, 16)
            sp.wait_ge(in_x[0].sem, in_x[0].at(G, 2))

        @block.gpsimd
        def _(pool):
            with pool.Fori(0, G) as i:
                pool.wait_ge(x2_done.sem, x2_done.at(i, GB))
                pool.dma_start(d["s_x2"][i], x2[:, :, :]).then_inc(stored.sem, 16)
                pool.wait_ge(stored.sem, stored.at(i, 1))
                pool.sem_inc(saved.sem, 1)

        @block.tensor
        def _(pe):
            pe.wait_ge(weights.sem, 16 * len(loads))
            pe.wait_ge(ready.sem, 1)
            mm = nc.tensor.matmul

            def raw_qk(i, n):
                pe.wait_ge(in_x[n % GB].sem, in_x[n % GB].at(i, 2 + 2 * (n // GB)))
                for kc in range(KC):
                    last = mm(misc[0:T, :], xt[:, n % GB, kc, :], wqkv[:, kc, 0:2 * D], start=kc == 0, stop=kc == KC - 1)
                last.then_inc(qk_raw.sem, 1)

            def raw_v(i, n):
                pe.wait_ge(qk_taken.sem, qk_taken.at(i, n + 1))
                for kc in range(KC):
                    last = mm(misc[0:T, 0:D], xt[:, n % GB, kc, :], wqkv[:, kc, 2 * D:3 * D], start=kc == 0, stop=kc == KC - 1)
                last.then_inc(qkv.sem, 1)

            def heads_of(i, n, part):
                if part == 0:
                    pe.wait_ge(roped.sem, roped.at(i, n + 1))
                else:
                    pe.wait_ge(q_sb.sem, q_sb.at(i, n + 1))
                for hg in range(HG):
                    h = part * HEADS + 4 * hg
                    last = nc.tensor.transpose(misc[:, hg * T:(hg + 1) * T], qkp[:, h:h + 4, :].rearrange("p h d -> p (h d)"), ident[0:T, 0:T])
                last.then_inc((q_t, qk_t)[part].sem, 1)

            def scores(i, n, r):
                if r == 0:
                    pe.wait_ge(qk_sb.sem, qk_sb.at(i, n + 1))
                mm(score[r][0:T, 0:4 * T], identb[:, :], causalb[:, :, :].rearrange("p h k -> p (h k)"), start=True, stop=False)
                q = 32 * r
                for hg in range(HG):
                    last = mm(score[r][0:T, hg * T:(hg + 1) * T], qc[q:q + 32, hg, :], kc_t[q:q + 32, hg, :], start=False, stop=hg == HG - 1, tile_position=(q, 0))
                last.then_inc(s_done.sem, 1)

            raw_qk(0, 0)
            raw_v(0, 0)
            heads_of(0, 0, 0)
            heads_of(0, 0, 1)
            scores(0, 0, 0)
            scores(0, 0, 1)
            with pe.Fori(0, G) as i:
                for j in range(GB):
                    def turn(r):
                        pe.wait_ge(p_done.sem, p_done.at(i, j * 4 + r + 1))
                        for hg in range(HG):
                            last = nc.tensor.transpose(trans[r % 2][0:T, hg * T:(hg + 1) * T], p[:, r % 2, hg, :], ident[0:T, 0:T])
                        last.then_inc(pt_done.sem, 1)

                    def values(r):
                        pe.wait_ge(pt_sb[r // 2].sem, pt_sb[r // 2].at(i, j * 2 + r % 2 + 1))
                        for hg in range(HG):
                            last = mm(outt[32 * r:32 * r + 32, hg * T:(hg + 1) * T], vp[:, 4 * hg + r, :], pt[:, r % 2, hg, :],
                                      start=True, stop=True, tile_position=(0, 32 * r))
                        if r == 3:
                            last.then_inc(o_done.sem, 1)

                    pe.wait_ge(o_sb.sem, o_sb.at(i, 2 * j))
                    turn(0)
                    scores(i, j, 2)
                    turn(1)
                    scores(i, j, 3)
                    values(0)
                    turn(2)
                    values(1)
                    turn(3)
                    values(2)
                    values(3)

                    def finish(n, w):
                        if n == 1:
                            pe.wait_ge(qk_sb.sem, qk_sb.at(i, j + 2))
                        pe.wait_ge(inv_done.sem, inv_done.at(i, 2 * j + n + 1))
                        for hg in range(HG):
                            last = nc.tensor.transpose(misc[:, hg * T:(hg + 1) * T],
                                                       inv_wide[:, 4 * hg:4 * hg + 4, :].rearrange("p h d -> p (h d)"), ident[0:T, 0:T])
                        last.then_inc(invt_done.sem, 1)
                        if n == 1:
                            scores(i, j + 1, 0)
                            scores(i, j + 1, 1)
                        pe.wait_ge(o_sb.sem, o_sb.at(i, 2 * j + n + 1))
                        for hg in range(HG):
                            last = mm(misc[0:T, 0:D], ot[:, hg, :], w[:, hg, :], start=hg == 0, stop=hg == HG - 1)
                        last.then_inc(proj.sem, 1)

                    finish(0, wproj)

                    pe.wait_ge(in_ctx[j].sem, in_ctx[j].at(i, 2))
                    pe.wait_ge(mask_done.sem, mask_done.at(i, j + 1))
                    for hg in range(HG):
                        for kc in range(KC):
                            mm(score[hg][:, 0:S2], wkx[:, kc, hg * 128:(hg + 1) * 128], ctxt[:, j, kc, :], start=kc == 0, stop=False)
                        mm(score[hg][:, 0:S2], maskrowb[:, :], maskb[:, j, :], start=False, stop=True).then_inc(kx.sem, 1)
                    for k in range(KT):
                        pe.wait_ge(vx_sb.sem, vx_sb.at(i, max(j * KT + k - 1, 0)))
                        for kc in range(KC):
                            last = mm(trans[k % 2][0:KP, 0:D], ctxt[:, j, kc, k * KP:(k + 1) * KP], wvx[:, kc, :], start=kc == 0, stop=kc == KC - 1)
                        last.then_inc(vxp.sem, 1)

                    pe.wait_ge(x1_done.sem, x1_done.at(i, j + 1))
                    pe.wait_ge(vx_sb.sem, vx_sb.at(i, j * KT + KT))
                    for kc in range(KC):
                        last = nc.tensor.transpose(trans[0][:, kc * T:(kc + 1) * T], x1[:, kc * 128:(kc + 1) * 128], ident[0:T, 0:T])
                    last.then_inc(x1t_done.sem, 1)
                    pe.wait_ge(x1t_sb.sem, x1t_sb.at(i, j + 1))
                    for hg in range(HG):
                        for kc in range(KC):
                            last = mm(trans[1][:, hg * T:(hg + 1) * T], wqx[:, kc, hg * 128:(hg + 1) * 128], x1t[:, kc, :], start=kc == 0, stop=kc == KC - 1)
                    last.then_inc(qx.sem, 1)

                    def xscore(h):
                        if h == 0:
                            pe.wait_ge(qx_sb.sem, qx_sb.at(i, j + 1))
                            pe.wait_ge(kx_sb.sem, kx_sb.at(i, j * HG + HG))
                        if h >= 4:
                            pe.wait_ge(pxd.sem, pxd.at(i, j * HEADS + h - 3))
                        q = 32 * (h % 4)
                        mm(score[h % 4][0:T, 0:S2], qt[q:q + 32, h // 4, :], ktx[q:q + 32, h // 4, :], start=True, stop=True,
                           tile_position=(q, 0)).then_inc(sx.sem, 1)

                    def xturn(h):
                        pe.wait_ge(pxd.sem, pxd.at(i, j * HEADS + h + 1))
                        if h >= 2:
                            pe.wait_ge(ptx_sb[h % 2].sem, ptx_sb[h % 2].at(i, j * HEADS // 2 + h // 2))
                        for k in range(KT):
                            last = nc.tensor.transpose(trans[h % 2][0:KP, k * T:(k + 1) * T], px[:, h % 4, k * KP:(k + 1) * KP], ident[0:T, 0:T])
                        last.then_inc(ptxd.sem, 1)

                    def xvalues(h):
                        pe.wait_ge(ptx_sb[h % 2].sem, ptx_sb[h % 2].at(i, j * HEADS // 2 + h // 2 + 1))
                        for k in range(KT):
                            q = 32 * (h % 4)
                            last = mm(outt[q:q + 32, (h // 4) * T:(h // 4 + 1) * T], vx[:, k, h, :], ptx[:, h % 2, k, :],
                                      start=k == 0, stop=k == KT - 1, tile_position=(0, q))
                        if h == HEADS - 1:
                            last.then_inc(o_done.sem, 1)

                    for h in range(4):
                        xscore(h)
                    for h in range(0, HEADS, 2):
                        if h == 0:
                            raw_qk(i, j + 1)
                        if h == 4:
                            raw_v(i, j + 1)
                        if h == 10:
                            heads_of(i, j + 1, 0)
                        if h == 12:
                            heads_of(i, j + 1, 1)
                        xturn(h)
                        xturn(h + 1)
                        if h + 4 < HEADS:
                            xscore(h + 4)
                            xscore(h + 5)
                        xvalues(h)
                        xvalues(h + 1)
                    finish(1, wox)

        @block.scalar
        def _(act):
            act.wait_ge(weights.sem, 16 * len(loads))
            fn = nc.scalar.activation

            def take_heads(i, n, part):
                done, to, taken = ((q_t, qc, q_sb), (qk_t, kc_t, qk_sb))[part]
                act.wait_ge(done.sem, done.at(i, n + 1))
                fn(to[:, :, :].rearrange("p h t -> p (h t)"), misc[:, 0:HG * T], ACT.Copy).then_inc(taken.sem, 1)

            take_heads(0, 0, 0)
            take_heads(0, 0, 1)
            with act.Fori(0, G) as i:
                for j in range(GB):
                    for r in range(4):
                        if r == 2:
                            for q in range(2):
                                act.wait_ge(pt_done.sem, pt_done.at(i, j * HG + q + 1))
                                fn(pt[:, q, :, :].rearrange("p h k -> p (h k)"), trans[q][0:T, 0:4 * T], ACT.Copy).then_inc(pt_sb[0].sem, 1)
                        act.wait_ge(m_done.sem, m_done.at(i, j * 4 + r + 1))
                        for hg in range(HG):
                            c = column(4 * hg + r)
                            last = fn(p[:, r % 2, hg, :], score[r][0:T, hg * T:(hg + 1) * T], ACT.Exp, bias=negmax[:, c:c + 1],
                                      scale=0.25, accum_out=rowsum[:, c:c + 1])
                        last.then_inc(p_done.sem, 1)

                    def inverse_sums(n):
                        act.wait_ge(invt_done.sem, invt_done.at(i, 2 * j + n + 1))
                        fn(inv_t[:, :, :].rearrange("p h t -> p (h t)"), misc[:, 0:HG * T], ACT.Copy).then_inc(invt_sb.sem, 1)

                    inverse_sums(0)
                    for hg in range(HG):
                        act.wait_ge(kx.sem, kx.at(i, j * HG + hg + 1))
                        fn(ktx[:, hg, :], score[hg][:, 0:S2], ACT.Identity, bias=bkx[:, hg:hg + 1]).then_inc(kx_sb.sem, 1)
                    act.wait_ge(x1t_done.sem, x1t_done.at(i, j + 1))
                    fn(x1t[:, :, :].rearrange("p c t -> p (c t)"), trans[0][:, 0:KC * T], ACT.Copy).then_inc(x1t_sb.sem, 1)
                    act.wait_ge(qx.sem, qx.at(i, j + 1))
                    for hg in range(HG):
                        last = fn(qt[:, hg, :], trans[1][:, hg * T:(hg + 1) * T], ACT.Identity, bias=bqx[:, hg:hg + 1])
                    last.then_inc(qx_sb.sem, 1)
                    def take_turned(h):
                        act.wait_ge(ptxd.sem, ptxd.at(i, j * HEADS + h + 1))
                        fn(ptx[:, 1, :, :].rearrange("p k t -> p (k t)"), trans[1][0:KP, 0:KT * T], ACT.Copy).then_inc(ptx_sb[1].sem, 1)

                    for h in range(HEADS):
                        if h % 2 == 0:
                            act.wait_ge(mx.sem, mx.at(i, (j * HEADS + h) // 2 + 1))
                        if h >= 4:
                            act.wait_ge(ptxd.sem, ptxd.at(i, j * HEADS + h - 3))
                        fn(px[:, h % 4, :], score[h % 4][0:T, 0:S2], ACT.Exp, bias=negmax[:, column(h):column(h) + 1], scale=0.25,
                           accum_out=rowsum[:, column(h):column(h) + 1]).then_inc(pxd.sem, 1)
                        if h % 2 == 1 and h >= 3:
                            take_turned(h - 2)
                        if h in (11, 13):
                            take_heads(i, j + 1, (h - 11) // 2)
                    take_turned(HEADS - 1)
                    inverse_sums(1)

        @block.vector
        def _(dve):
            V = nc.vector
            dve.wait_ge(weights.sem, 16 * len(loads))
            V.memset(qkp[:, :, :].rearrange("p h d -> p (h d)"), 0.0)
            V.memset(vp[:, :, :].rearrange("p h d -> p (h d)"), 0.0)
            V.memset(vx[:, :, :, :].rearrange("p k h d -> p (k h d)"), 0.0)
            V.tensor_copy(identb[:, :], ident_f[:, :])
            V.tensor_copy(maskrowb[:, :], maskrow_f[:, :])
            V.tensor_copy(causalb[:, :, :], causal_f[:, :].unsqueeze(1).broadcast_to([T, 4, T])).then_inc(ready.sem, 1)
            dve.wait_ge(ready.sem, 1)
            heads = lambda a: a.rearrange("p (h d) -> p h d", d=DH)
            q3 = heads(qkb[:, :])
            r2 = heads(rot2[:, :])

            def take_qk(i, n):
                dve.wait_ge(qk_raw.sem, qk_raw.at(i, n + 1))
                V.tensor_tensor(qkb[:, :], misc[0:T, :], bqkv[:, 0:2 * D], ALU.add).then_inc(qk_taken.sem, 1)

            def rotate(i, n, link):
                dve.wait_ge(qk_taken.sem, qk_taken.at(i, n + 1))
                V.tensor_tensor(heads(rot1[:, :]), q3, cos[:, :].unsqueeze(1).broadcast_to([T, 2 * HEADS, DH]), ALU.mult)
                V.tensor_tensor(r2[:, :, 0:8], q3[:, :, 8:16], sin[:, 0:8].unsqueeze(1).broadcast_to([T, 2 * HEADS, 8]), ALU.mult)
                link(V.tensor_tensor(r2[:, :, 8:16], q3[:, :, 0:8], sin[:, 8:16].unsqueeze(1).broadcast_to([T, 2 * HEADS, 8]), ALU.mult))

            def take_v(i, n):
                V.tensor_tensor(qkp[:, :, 0:DH], heads(rot1[:, :]), r2, ALU.add)
                dve.wait_ge(qkv.sem, qkv.at(i, n + 1))
                V.tensor_tensor(vp[:, :, 0:DH], heads(misc[0:T, 0:D]), heads(bqkv[:, 2 * D:3 * D]), ALU.add).then_inc(roped.sem, 1)

            def maxima(i, n, hg, link):
                dve.wait_ge(s_done.sem, s_done.at(i, n * 4 + hg + 1))
                link(V.tensor_reduce(rowmax[:, 4 * hg:4 * hg + 4], score[hg][0:T, 0:4 * T].rearrange("p (h k) -> p h k", h=4), AX.X, ALU.max))
                V.tensor_scalar(negmax[:, 4 * hg:4 * hg + 4], rowmax[:, 4 * hg:4 * hg + 4], -0.25, None, ALU.mult).then_inc(m_done.sem, 1)

            link0 = lambda ins: vfirst.chain(dve, 0, ins)
            take_qk(0, 0)
            rotate(0, 0, link0)
            take_v(0, 0)
            maxima(0, 0, 0, link0)
            maxima(0, 0, 1, link0)
            with dve.Fori(0, G) as i:
                link = lambda ins: vlink.chain(dve, i, ins)
                for j in range(GB):
                    dve.wait_ge(in_x[j].sem, in_x[j].at(i, 2))
                    V.tensor_tensor(xb[:, :], x[:, j, :], bproj[:, :], ALU.add).then_inc(x_done.sem, 1)
                    dve.wait_ge(in_ctx[j].sem, in_ctx[j].at(i, 2))
                    V.tensor_scalar(maskb[:, j, :], mask8[:, j, :], NEG, None, ALU.mult).then_inc(mask_done.sem, 1)
                    maxima(i, j, 2, link)
                    maxima(i, j, 3, link)
                    for hg in range(2, HG):
                        dve.wait_ge(pt_done.sem, pt_done.at(i, j * HG + hg + 1))
                        V.tensor_copy(pt[:, hg % 2, :, :].rearrange("p h k -> p (h k)"), trans[hg % 2][0:T, 0:4 * T]).then_inc(pt_sb[1].sem, 1)

                    def normalise(n, last_p, bias_x, out, done):
                        dve.wait_ge(last_p.sem, last_p.at(i, (j + 1) * (last_p.per // GB)))
                        link(V.reciprocal(rowinv[:, :], rowsum[:, :]))
                        V.tensor_copy(inv_wide[:, :, :].rearrange("p (g r) d -> p g r d", r=4), rowinv[:, :].rearrange("p (r g) -> p g r", r=4).unsqueeze(3).broadcast_to([T, HG, 4, PAD])).then_inc(inv_done.sem, 1)
                        dve.wait_ge(o_done.sem, o_done.at(i, 2 * j + n + 1))
                        dve.wait_ge(invt_sb.sem, invt_sb.at(i, 2 * j + n + 1))
                        V.tensor_tensor(ot[:, :, :].rearrange("p h t -> p (h t)"), outt[:, 0:HG * T],
                                        inv_t[:, :, :].rearrange("p h t -> p (h t)"), ALU.mult).then_inc(o_sb.sem, 1)
                        if n == 1:
                            maxima(i, j + 1, 0, link)
                            maxima(i, j + 1, 1, link)
                        dve.wait_ge(proj.sem, proj.at(i, 2 * j + n + 1))
                        link(V.tensor_tensor(t[:, :], misc[0:T, 0:D], bias_x, ALU.add))
                        layer_norms(dve, nc, vlink, i, [t[:, :]], stats, [out], [done])

                    normalise(0, p_done, xb[:, :], x1[:, :], x1_done)
                    dve.wait_ge(x1_done.sem, x1_done.at(i, j + 1))
                    V.tensor_tensor(xb[:, :], x1[:, :], box[:, :], ALU.add)
                    for k in range(KT):
                        dve.wait_ge(vxp.sem, vxp.at(i, j * KT + k + 1))
                        V.tensor_tensor(vx[:, k, :, 0:DH], trans[k % 2][0:KP, 0:D].rearrange("p (h d) -> p h d", d=DH),
                                        bvx[:, :].rearrange("p (h d) -> p h d", d=DH), ALU.add).then_inc(vx_sb.sem, 1)

                    def xmax(h):
                        dve.wait_ge(sx.sem, sx.at(i, j * HEADS + h + 2))
                        for n in range(2):
                            last = V.tensor_reduce(rowmax[:, column(h + n):column(h + n) + 1], score[(h + n) % 4][0:T, 0:S2], AX.X, ALU.max)
                        link(last)
                        V.tensor_scalar(negmax[:, column(h):column(h) + 5:4], rowmax[:, column(h):column(h) + 5:4], -0.25, None, ALU.mult).then_inc(mx.sem, 1)

                    xmax(0)
                    xmax(2)
                    for h in range(0, HEADS, 2):
                        dve.wait_ge(ptxd.sem, ptxd.at(i, j * HEADS + h + 1))
                        V.tensor_copy(ptx[:, 0, :, :].rearrange("p k t -> p (k t)"), trans[0][0:KP, 0:KT * T]).then_inc(ptx_sb[0].sem, 1)
                        if h + 4 < HEADS:
                            xmax(h + 4)
                        if h == 0:
                            take_qk(i, j + 1)
                        if h == 2:
                            rotate(i, j + 1, link)
                        if h == 4:
                            take_v(i, j + 1)
                    if j == 0:
                        dve.wait_ge(saved.sem, saved.at(i, 0))
                    normalise(1, pxd, xb[:, :], x2[:, j, :], x2_done)
            assert vlink.seen == vlink.per, vlink.seen



ROUTE_INPUTS = ["router", "ident", "earlier", "ones", "rev", "slot_no"]


def routing_phase(nc, d, own):
    NS = GB * G
    NG = 2
    ctx = ExitStack()
    with ctx:
        def sb(name, shape, dt=F32):
            return ctx.enter_context(nc.sbuf_tensor("r_" + name, shape, dt))

        def sem(name, per, unit=1, early=False):
            return Steps(own("r_" + name, early), per, unit, early)

        router = sb("router", [128, KC, E])
        ident = sb("ident", [128, 128])
        earlier = sb("earlier", [T, T])
        ones = sb("ones", [T, T])
        rev = sb("rev", [T, E])
        slot_no = sb("slot_no", [T, CAP])
        x2 = sb("x2", [T, G, GB, D])
        x2t = sb("x2t", [128, NS, KC, T])
        lg = sb("lg", [T, NS, E])
        raw = sb("raw", [T, NS, E])
        tmp = sb("tmp", [T, NS, E])
        cand = sb("cand", [T, NS, E])
        pick = sb("pick", [T, NS, 2, E])
        kept = sb("kept", [T, NS, 2, E])
        pos = sb("pos", [T, NS, 2, E])
        s1 = sb("s1", [T, NS, 6])
        gate = sb("gate", [T, NS, 2])
        place = sb("place", [T, NS, 2])
        xg = sb("xg", [T, NG, GB, D])
        onehot = sb("onehot", [T, NG, GB, 2, CAP])
        comb = sb("comb", [T, NG, GB, E, CAP])
        comb2 = sb("comb2", [T, NG, GB, E, CAP])
        disp = sb("disp", [T, NG, GB, SL])
        xe = sb("xe", [128, NG, KC, SL])
        combt = sb("combt", [T, NG, GB, ST, T])
        bank = [ctx.enter_context(nc.psum_tensor(f"r_bank{n}", [128, 512], F32)) for n in range(8)]

        first = sem("first", 1)
        turned = sem("turned", 1)
        x2t_sb = sem("x2t_sb", 1)
        lg_done = sem("lg_done", 1)
        lg_sub = sem("lg_sub", 1)
        lg_exp = sem("lg_exp", 1)
        picked = sem("picked", 1)
        counted = sem("counted", 1)
        kept1 = sem("kept1", 1)
        total1 = sem("total1", 1)
        xg_in = [sem(f"xg_in{h}", 1, 16) for h in range(NG)]
        routed = sem("routed", NG)
        xe_done = sem("xe_done", NG, early=2)
        ct_done = sem("ct_done", NG, early=2)
        evacuated = sem("evacuated", NG, early=2)
        stored = sem("stored", 2 * NG, 16)
        saved = sem("saved", NG, early=2)
        vlink = sem("vlink", 1)
        glink = sem("glink", 1)
        block = ctx.enter_context(nc.Block())
        loads = [(router[:, :, :], d["router"]), (ident[:, :], d["ident"]), (earlier[:, :], d["earlier"]), (ones[:, :], d["ones"]),
                 (rev[:, :], d["rev"]), (slot_no[:, :], d["slot_no"])] + [(x2[:, g, :, :], d["s_x2"][g]) for g in range(G)]
        wide = lambda a: a.unsqueeze(2).broadcast_to([T, NS, E])

        @block.sync
        def _(sp):
            for dst, src in loads:
                sp.dma_start(dst, src).then_inc(first.sem, 16)
            with sp.Fori(0, G // NG) as i:
                for h in range(NG):
                    sp.wait_ge(xe_done.sem, xe_done.at(i, h - 1))
                    sp.dma_start(xg[:, h, :, :], d["s_x2"][i * NG + h]).then_inc(xg_in[h].sem, 16)

        @block.gpsimd
        def _(pool):
            pool.wait_ge(total1.sem, 1)
            with pool.Fori(0, G // NG) as i:
                for h in range(NG):
                    pool.wait_ge(evacuated.sem, evacuated.at(i, h + 1))
                    pool.dma_start(d["s_xe"][i * NG + h], xe[:, h, :, :]).then_inc(stored.sem, 16)
                    pool.dma_start(d["s_ct"][i * NG + h], combt[:, h, :, :, :]).then_inc(stored.sem, 16)
                    pool.wait_ge(stored.sem, stored.at(i, 2 * h + 2))
                    pool.sem_inc(saved.sem, 1)

        @block.tensor
        def _(pe):
            mm = nc.tensor.matmul
            pe.wait_ge(first.sem, 16 * len(loads))
            for n in range(NS // 2):
                if n >= 4:
                    pe.wait_ge(x2t_sb.sem, n - 3)
                for m in range(2):
                    j, g = divmod(2 * n + m, G)
                    for kc in range(KC):
                        last = nc.tensor.transpose(bank[n % 4][:, (m * KC + kc) * T:(m * KC + kc + 1) * T], x2[:, g, j, kc * 128:(kc + 1) * 128], ident[0:T, 0:T])
                last.then_inc(turned.sem, 1)
            for n in range(NS):
                pe.wait_ge(x2t_sb.sem, n // 2 + 1)
                for kc in range(KC):
                    last = mm(bank[4][0:T, n * E:(n + 1) * E], x2t[:, n, kc, :], router[:, kc, :], start=kc == 0, stop=kc == KC - 1)
            last.then_inc(lg_done.sem, 1)
            pe.wait_ge(picked.sem, 1)
            picks = [pick[:, j * G:(j + 1) * G, :, :].rearrange("p n c e -> p (n c e)") for j in range(GB)]
            W = G * 2 * E
            mm(bank[5][0:T, 0:W], earlier[:, :], picks[0], start=True, stop=True)
            mm(bank[5][0:T, W:2 * W], earlier[:, :], picks[1], start=True, stop=False)
            mm(bank[5][0:T, W:2 * W], ones[:, :], picks[0], start=False, stop=True).then_inc(counted.sem, 1)
            pe.wait_ge(kept1.sem, 1)
            for j in range(GB):
                last = mm(bank[6][0:T, 0:G * E], ones[:, :], kept[:, j * G:(j + 1) * G, 0, :], start=j == 0, stop=j == GB - 1)
            last.then_inc(total1.sem, 1)
            with pe.Fori(0, G // NG) as i:
                for h in range(NG):
                    pe.wait_ge(xg_in[h].sem, xg_in[h].at(i, 1))
                    pe.wait_ge(routed.sem, routed.at(i, h + 1))
                    pe.wait_ge(evacuated.sem, evacuated.at(i, h - 1))
                    for fc in range(KC):
                        for j in range(GB):
                            last = mm(bank[4 * h + fc][:, 0:SL], xg[:, h, j, fc * 128:(fc + 1) * 128], disp[:, h, j, :], start=j == 0, stop=j == GB - 1)
                    last.then_inc(xe_done.sem, 1)
                    for j in range(GB):
                        for s in range(ST):
                            last = nc.tensor.transpose(bank[4 * h + 2 + j][0:T, s * T:(s + 1) * T],
                                                       comb[:, h, j, 2 * s:2 * s + 2, :].rearrange("p e c -> p (e c)"), ident[0:T, 0:T])
                    last.then_inc(ct_done.sem, 1)

        @block.scalar
        def _(act):
            fn = nc.scalar.activation
            for n in range(NS // 2):
                act.wait_ge(turned.sem, n + 1)
                fn(x2t[:, 2 * n:2 * n + 2, :, :].rearrange("p n k t -> p (n k t)"), bank[n % 4][:, 0:2 * KC * T], ACT.Copy).then_inc(x2t_sb.sem, 1)
            act.wait_ge(lg_sub.sem, 1)
            fn(raw[:, :, :], lg[:, :, :], ACT.Exp).then_inc(lg_exp.sem, 1)
            with act.Fori(0, G // NG) as i:
                for h in range(NG):
                    act.wait_ge(saved.sem, saved.at(i, h - 1))
                    act.wait_ge(xe_done.sem, xe_done.at(i, h + 1))
                    for fc in range(KC):
                        fn(xe[:, h, fc, :], bank[4 * h + fc][:, 0:SL], ACT.Copy)
                    act.wait_ge(ct_done.sem, ct_done.at(i, h + 1))
                    for j in range(GB):
                        last = fn(combt[:, h, j, :, :].rearrange("p s t -> p (s t)"), bank[4 * h + 2 + j][0:T, 0:ST * T], ACT.Copy)
                    last.then_inc(evacuated.sem, 1)

        @block.vector
        def _(dve):
            V = nc.vector
            link = lambda ins: vlink.chain(dve, 0, ins)
            dve.wait_ge(lg_done.sem, 1)
            link(V.tensor_copy(lg[:, :, :].rearrange("p n e -> p (n e)"), bank[4][0:T, 0:NS * E]))
            link(V.tensor_reduce(s1[:, :, 0], lg[:, :, :], AX.X, ALU.max))
            V.tensor_tensor(lg[:, :, :], lg[:, :, :], wide(s1[:, :, 0]), ALU.subtract).then_inc(lg_sub.sem, 1)
            dve.wait_ge(lg_exp.sem, 1)
            link(V.tensor_reduce(s1[:, :, 1], raw[:, :, :], AX.X, ALU.add))
            link(V.reciprocal(s1[:, :, 2], s1[:, :, 1]))
            link(V.tensor_tensor(raw[:, :, :], raw[:, :, :], wide(s1[:, :, 2]), ALU.mult))
            for c in range(2):
                link(V.tensor_reduce(s1[:, :, 3 + c], raw[:, :, :], AX.X, ALU.max))
                link(V.tensor_tensor(tmp[:, :, :], raw[:, :, :], wide(s1[:, :, 3 + c]), ALU.is_equal))
                link(V.tensor_tensor(cand[:, :, :], tmp[:, :, :], rev[:, :].unsqueeze(1).broadcast_to([T, NS, E]), ALU.mult))
                link(V.tensor_reduce(s1[:, :, 5], cand[:, :, :], AX.X, ALU.max))
                last = V.tensor_tensor(pick[:, :, c, :], cand[:, :, :], wide(s1[:, :, 5]), ALU.is_equal)
                if c == 0:
                    link(last)
                    link(V.tensor_scalar(tmp[:, :, :], pick[:, :, 0, :], -1.0, 1.0, ALU.mult, ALU.add))
                    link(V.tensor_tensor(raw[:, :, :], raw[:, :, :], tmp[:, :, :], ALU.mult))
            last.then_inc(picked.sem, 1)
            dve.wait_ge(counted.sem, 1)
            link(V.tensor_copy(pos[:, :, :, :].rearrange("p n c e -> p (n c e)"), bank[5][0:T, 0:NS * 2 * E]))
            link(V.tensor_scalar(tmp[:, :, :], pos[:, :, 0, :], float(CAP), None, ALU.is_lt))
            V.tensor_tensor(kept[:, :, 0, :], pick[:, :, 0, :], tmp[:, :, :], ALU.mult).then_inc(kept1.sem, 1)
            dve.wait_ge(total1.sem, 1)
            link(V.tensor_copy(cand[:, 0:G, :].rearrange("p n e -> p (n e)"), bank[6][0:T, 0:G * E]))
            for j in range(GB):
                last = V.tensor_tensor(pos[:, j * G:(j + 1) * G, 1, :], pos[:, j * G:(j + 1) * G, 1, :], cand[:, 0:G, :], ALU.add)
            link(last)
            link(V.tensor_scalar(tmp[:, :, :], pos[:, :, 1, :], float(CAP), None, ALU.is_lt))
            link(V.tensor_tensor(kept[:, :, 1, :], pick[:, :, 1, :], tmp[:, :, :], ALU.mult))
            link(V.tensor_reduce(gate[:, :, :], kept[:, :, :, :], AX.X, ALU.add))
            link(V.tensor_tensor(gate[:, :, :], gate[:, :, :], s1[:, :, 3:5], ALU.mult))
            link(V.tensor_tensor(pos[:, :, :, :], pos[:, :, :, :], kept[:, :, :, :], ALU.mult))
            link(V.tensor_reduce(place[:, :, :], pos[:, :, :, :], AX.X, ALU.add))
            glink.per = NG * (2 + GB)
            with dve.Fori(0, G // NG) as i:
                for h in range(NG):
                    at = lambda j: bass.ds(i * NG + (j * G + h), 1)
                    dve.wait_ge(xe_done.sem, xe_done.at(i, h - 1))
                    dve.wait_ge(ct_done.sem, ct_done.at(i, h - 1))
                    for j in range(GB):
                        for c in range(2):
                            last = V.tensor_scalar(onehot[:, h, j, c, :], slot_no[:, :], place[:, at(j), c], gate[:, at(j), c], ALU.is_equal, ALU.mult)
                    glink.chain(dve, i, last)
                    for j in range(GB):
                        V.tensor_tensor(comb[:, h, j, :, :], kept[:, at(j), 0, :].rearrange("p n e -> p (n e)").unsqueeze(2).broadcast_to([T, E, CAP]),
                                        onehot[:, h, j, 0, :].unsqueeze(1).broadcast_to([T, E, CAP]), ALU.mult)
                        last = V.tensor_tensor(comb2[:, h, j, :, :], kept[:, at(j), 1, :].rearrange("p n e -> p (n e)").unsqueeze(2).broadcast_to([T, E, CAP]),
                                               onehot[:, h, j, 1, :].unsqueeze(1).broadcast_to([T, E, CAP]), ALU.mult)
                    glink.chain(dve, i, last)
                    for j in range(GB):
                        glink.chain(dve, i, V.tensor_tensor(comb[:, h, j, :, :], comb[:, h, j, :, :], comb2[:, h, j, :, :], ALU.add))
                        last = V.tensor_scalar(disp[:, h, j, :], comb[:, h, j, :, :].rearrange("p e c -> p (e c)"), 0.0, None, ALU.not_equal)
                    last.then_inc(routed.sem, 1)


def expert_phase(nc, d, own):
    NP = 2
    ctx = ExitStack()
    with ctx:
        def sb(name, shape, dt=F32):
            return ctx.enter_context(nc.sbuf_tensor("b_" + name, shape, dt))

        def sem(name, per, unit=1, early=False):
            return Steps(own("b_" + name, early), per, unit, early)

        w_in = sb("w_in", [128, 2, KC, HID])
        xe_in = sb("xe_in", [128, KC, G, CAP])
        w_hi = [sb(f"w_hi{n}", [128, 2, KC, HID], F32R) for n in range(NP)]
        w_lo = [sb(f"w_lo{n}", [128, 2, KC, HID], F32R) for n in range(NP)]
        xe_hi = [sb(f"xe_hi{n}", [128, KC, SL], F32R) for n in range(NP)]
        xe_lo = [sb(f"xe_lo{n}", [128, KC, SL], F32R) for n in range(NP)]
        wo = [sb(f"wo_{n}", [HP, HT, D]) for n in range(NP)]
        act_out = sb("act_out", [HP, 2, SL])
        hid = sb("hid", [HP, HT, SL])
        eo = [sb(f"eo_{n}", [T, ST, D]) for n in range(NP)]
        up = [ctx.enter_context(nc.psum_tensor(f"b_up{n}", [128, 512], F32)) for n in range(4)]
        down = [ctx.enter_context(nc.psum_tensor(f"b_down{n}", [128, 512], F32)) for n in range(4)]

        staged = [sem(f"staged{n}", 4, 16) for n in range(NP)]
        wo_in = [sem(f"wo_in{n}", 1, 16) for n in range(NP)]
        coarse = sem("coarse", NP)
        split = sem("split", NP)
        up_done = sem("up_done", NP * HT)
        gelu = sem("gelu", NP * HT)
        hid_done = sem("hid_done", NP * HT, early=True)
        down_done = sem("down_done", NP * ST)
        eo_sb = sem("eo_sb", NP * ST, early=True)
        stored = [sem(f"stored{n}", 2, 16) for n in range(NP)]
        saved = sem("saved", NP, early=True)
        block = ctx.enter_context(nc.Block())

        @block.sync
        def _(sp):
            def stage(e, n):
                for m, w in enumerate(("w0", "w1")):
                    sp.dma_start(w_in[:, m, :, :], d[w][e]).then_inc(staged[n].sem, 16)
                for kc in range(KC):
                    sp.dma_start(xe_in[:, kc, :, :], d["s_xe_by_expert"][e][kc]).then_inc(staged[n].sem, 16)

            stage(0, 0)
            for n in range(NP):
                sp.dma_start(wo[n][:, :, :], d["wo"][n]).then_inc(wo_in[n].sem, 16)
            with sp.Fori(0, E // NP - 1) as i:
                for n in range(NP):
                    sp.wait_ge(split.sem, split.at(i, n + 1))
                    stage(i * NP + (n + 1), (n + 1) % NP)
                    sp.wait_ge(down_done.sem, down_done.at(i, (n + 1) * ST))
                    sp.dma_start(wo[n][:, :, :], d["wo"][i * NP + (NP + n)]).then_inc(wo_in[n].sem, 16)
            sp.wait_ge(split.sem, split.at(E // NP - 1, 1))
            stage(E - 1, 1)
            sp.wait_ge(split.sem, split.at(E // NP - 1, 2))
            stage(0, 0)
            sp.wait_ge(staged[0].sem, staged[0].at(E // NP, 4))

        @block.gpsimd
        def _(pool):
            with pool.Fori(0, E // NP) as i:
                for n in range(NP):
                    pool.wait_ge(eo_sb.sem, eo_sb.at(i, (n + 1) * ST))
                    for g in range(2):
                        pool.dma_start(d["s_eo_by_expert"][i * NP + n][g], eo[n][g * CAP:(g + 1) * CAP, :, :]).then_inc(stored[n].sem, 16)
                    pool.wait_ge(stored[n].sem, stored[n].at(i, 2))
                    pool.sem_inc(saved.sem, 1)

        @block.tensor
        def _(pe):
            mm = nc.tensor.matmul
            with pe.Fori(0, E // NP) as i:
                for n in range(NP):
                    pe.wait_ge(split.sem, split.at(i, n + 1))
                    for h in range(HT):
                        pe.wait_ge(hid_done.sem, hid_done.at(i, max(n * HT + h - 1, 0)))
                        for m in range(2):
                            parts = [(w, x, kc) for kc in range(KC) for w, x in ((w_hi[n], xe_hi[n]), (w_hi[n], xe_lo[n]), (w_lo[n], xe_hi[n]))]
                            for k, (w, x, kc) in enumerate(parts):
                                last = mm(up[2 * (h % 2) + m][0:HP, 0:SL], w[:, m, kc, h * HP:(h + 1) * HP], x[:, kc, :],
                                          start=k == 0, stop=k == len(parts) - 1)
                        last.then_inc(up_done.sem, 1)
                    pe.wait_ge(wo_in[n].sem, wo_in[n].at(i, 1))
                    for s in range(ST):
                        pe.wait_ge(eo_sb.sem, eo_sb.at(i, max(n * ST + s - 3, 0)))
                        for h in range(HT):
                            if s == 0:
                                pe.wait_ge(hid_done.sem, hid_done.at(i, n * HT + h + 1))
                            last = mm(down[s][0:T, 0:D], hid[:, h, s * T:(s + 1) * T], wo[n][:, h, :], start=h == 0, stop=h == HT - 1)
                        last.then_inc(down_done.sem, 1)

        @block.scalar
        def _(act):
            def coarse_parts(i, n):
                b = n % NP
                act.wait_ge(staged[b].sem, staged[b].at(i, 4 + 4 * (n // NP)))
                nc.scalar.activation(xe_hi[b][:, :, :], xe_in[:, :, :, :].rearrange("p k g c -> p k (g c)"), ACT.Copy)
                for m in range(2):
                    last = nc.scalar.activation(w_hi[b][:, m, :, :].rearrange("p k h -> p (k h)"), w_in[:, m, :, :].rearrange("p k h -> p (k h)"), ACT.Copy)
                last.then_inc(coarse.sem, 1)

            coarse_parts(0, 0)
            with act.Fori(0, E // NP) as i:
                for n in range(NP):
                    for h in range(HT):
                        act.wait_ge(up_done.sem, up_done.at(i, n * HT + h + 1))
                        nc.scalar.activation(act_out[:, h % 2, :], up[2 * (h % 2)][0:HP, 0:SL], ACT.Gelu_apprx_tanh).then_inc(gelu.sem, 1)
                    coarse_parts(i, n + 1)

        @block.vector
        def _(dve):
            def fine_parts(i, n):
                b = n % NP
                dve.wait_ge(coarse.sem, coarse.at(i, n + 1))
                nc.vector.tensor_tensor(xe_lo[b][:, :, :], xe_in[:, :, :, :].rearrange("p k g c -> p k (g c)"), xe_hi[b][:, :, :].bitcast(F32), ALU.subtract)
                for m in range(2):
                    for kc in range(KC):
                        last = nc.vector.tensor_tensor(w_lo[b][:, m, kc, :], w_in[:, m, kc, :], w_hi[b][:, m, kc, :].bitcast(F32), ALU.subtract)
                last.then_inc(split.sem, 1)

            fine_parts(0, 0)
            with dve.Fori(0, E // NP) as i:
                for n in range(NP):
                    for h in range(HT):
                        dve.wait_ge(gelu.sem, gelu.at(i, n * HT + h + 1))
                        nc.vector.tensor_tensor(hid[:, h, :], up[2 * (h % 2) + 1][0:HP, 0:SL], act_out[:, h % 2, :], ALU.mult).then_inc(hid_done.sem, 1)
                    fine_parts(i, n + 1)
                    dve.wait_ge(saved.sem, saved.at(i, 0))
                    for s in range(ST):
                        dve.wait_ge(down_done.sem, down_done.at(i, n * ST + s + 1))
                        nc.vector.tensor_copy(eo[n][:, s, :], down[s][0:T, 0:D]).then_inc(eo_sb.sem, 1)

DIN, NST, RANK, TAPS = 512, 16, 64, 4
DT = DIN // 128
QB = 4
QT = QB * T
XD = RANK + 2 * NST
SPREAD = 6


def mixer_phase(nc, d, own):
    ctx = ExitStack()
    with ctx:
        def sb(name, shape, dt=F32):
            return ctx.enter_context(nc.sbuf_tensor("c_" + name, shape, dt))

        def sem(name, per, unit=1, early=False):
            return Steps(own("c_" + name, early), per, unit, early)

        win = sb("win", [128, KC, 2 * DIN])
        convw = sb("convw", [128, DT, TAPS])
        convb = sb("convb", [128, DT])
        wx = sb("wx", [128, DT, XD])
        wdt = sb("wdt", [RANK, DIN])
        bdt = sb("bdt", [128, DT])
        alog = sb("alog", [128, DT, NST])
        aneg = sb("aneg", [128, DT, NST])
        dp = sb("dp", [128, DT])
        wout = sb("wout", [128, DT, D])
        ident = sb("ident", [128, 128])
        row_of = sb("row_of", [XD, 2 * NST, 128], F32R)

        x2 = sb("x2", [T, QB // GB, GB, D])
        eo = sb("eo", [T, QB // GB, ST, D])
        ct = sb("ct", [T, QB // GB, GB, ST, T])
        t = sb("t", [T, QB, D])
        t_next = sb("t_next", [T, QB, D])
        stats = sb("stats", [T, 2 * QB, 10])
        x3 = sb("x3", [T, QB, D])
        x3t = sb("x3t", [128, KC, QT])
        u = sb("u", [128, DT, QB, TAPS - 1 + T])
        conv = sb("conv", [128, DT, QT])
        us = sb("us", [128, DT, QT])
        rs = sb("rs", [128, DT, QT])
        xd = sb("xd", [XD, QT])
        xd_hi = sb("xd_hi", [XD, QT], F32R)
        xd_lo = sb("xd_lo", [XD, QT], F32R)
        z = sb("z", [128, DT, QT])
        soft = sb("soft", [128, DT, QT])
        delta = sb("delta", [128, DT, QT])
        du = sb("du", [128, DT, QT])
        bc = sb("bc", [128, 2 * NST, QT])
        decay = sb("decay", [128, 2, QT])
        bu = sb("bu", [128, 3, QT])
        state = sb("state", [128, 2, QT])
        out_c = sb("out_c", [128, 2, QT])
        x4 = sb("x4", [T, QB, D])
        bank = [ctx.enter_context(nc.psum_tensor(f"c_bank{n}", [128, 512], F32)) for n in range(8)]

        weights = sem("weights", 1)
        ready = sem("ready", 1)
        loaded = sem("loaded", 3 * (QB // GB), 16)
        gathered = sem("gathered", QB)
        g_read = sem("g_read", QB, early=True)
        x3_done = sem("x3_done", QB)
        x3t_done = sem("x3t_done", 1)
        x3t_sb = sem("x3t_sb", 1)
        xr = sem("xr", 2 * DT)
        xr_sb = sem("xr_sb", 2 * DT, early=True)
        conv_done = sem("conv_done", DT)
        us_done = sem("us_done", DT)
        xd_done = sem("xd_done", 1)
        xd_sb = sem("xd_sb", 1)
        xd_split = sem("xd_split", 1)
        dz = sem("dz", DT)
        z_done = sem("z_done", DT, early=True)
        alink = sem("alink", 2 * DT)
        sp_done = sem("sp_done", DT)
        du_done = sem("du_done", DT, early=True)
        bc_done = sem("bc_done", 2 * NST)
        bc_sb = sem("bc_sb", 2 * NST, early=True)
        decayed = sem("decayed", DT * NST)
        bu_done = sem("bu_done", DT * NST)
        scanned = sem("scanned", DT * NST, early=True)
        weighted = sem("weighted", DT * NST, early=True)
        summed = sem("summed", DT * NST, early=True)
        y_done = sem("y_done", DT, early=True)
        out_done = sem("out_done", QB)
        x4_done = sem("x4_done", QB, early=True)
        stored = sem("stored", 1, 16)
        saved = sem("saved", 1, early=True)
        vlink = sem("vlink", 49)
        vfirst = sem("vfirst", 1)
        back_in = [bank[4 + b // 2][0:T, b % 2 * D:(b % 2 + 1) * D] for b in range(QB)]
        block = ctx.enter_context(nc.Block())
        flat = lambda a: a.rearrange("p a b -> p (a b)")

        row_f = bc[0:XD, :, 0:128]
        loads = [(win[:, :, :], d["win"]), (convw[:, :, :], d["convw"]), (convb[:, :], d["convb"]), (wx[:, :, :], d["wx"]),
                 (wdt[:, :], d["wdt"]), (bdt[:, :], d["bdt"]), (alog[:, :, :], d["alog"]), (dp[:, :], d["dp"]),
                 (wout[:, :, :], d["wout"]), (ident[:, :], d["ident"]), (row_f, d["row_of"])]

        @block.sync
        def _(sp):
            for dst, src in loads:
                sp.dma_start(dst, src).then_inc(weights.sem, 16)
            with sp.Fori(0, B // QB) as i:
                sp.wait_ge(g_read.sem, g_read.at(i, 0))
                for g in range(QB // GB):
                    sp.dma_start(x2[:, g, :, :], d["s_x2"][i * (QB // GB) + g]).then_inc(loaded.sem, 16)
                    sp.dma_start(eo[:, g, :, :], d["s_eo_by_group"][i * (QB // GB) + g]).then_inc(loaded.sem, 16)
                    sp.dma_start(ct[:, g, :, :, :], d["s_ct"][i * (QB // GB) + g]).then_inc(loaded.sem, 16)
            sp.wait_ge(g_read.sem, g_read.at(B // QB, 0))
            for g in range(QB // GB):
                sp.dma_start(x2[:, g, :, :], d["s_x2"][g]).then_inc(loaded.sem, 16)
                sp.dma_start(eo[:, g, :, :], d["s_eo_by_group"][g]).then_inc(loaded.sem, 16)
                sp.dma_start(ct[:, g, :, :, :], d["s_ct"][g]).then_inc(loaded.sem, 16)
            sp.wait_ge(loaded.sem, loaded.at(B // QB, 6))

        @block.gpsimd
        def _(pool):
            nc.gpsimd.memset(u[:, :, :, :].rearrange("p a b c -> p (a b c)"), 0.0)
            nc.gpsimd.memset(flat(decay[:, :, :]), 0.0).then_inc(ready.sem, 1)
            with pool.Fori(0, B // QB) as i:
                for k in range(DT * NST):
                    pool.wait_ge(scanned.sem, scanned.at(i, k + 1))
                    pool.wait_ge(summed.sem, summed.at(i, max(k - 1, 0)))
                    nc.gpsimd.tensor_tensor(out_c[:, k % 2, :], state[:, k % 2, :], bc[:, NST + k % NST, :], ALU.mult).then_inc(weighted.sem, 1)
                pool.wait_ge(x4_done.sem, x4_done.at(i, QB))
                pool.dma_start(d["s_x4_by_four"][i], x4[:, :, :]).then_inc(stored.sem, 16)
                pool.wait_ge(stored.sem, stored.at(i, 1))
                pool.sem_inc(saved.sem, 1)

        @block.tensor
        def _(pe):
            mm = nc.tensor.matmul
            pe.wait_ge(weights.sem, 16 * len(loads))
            pe.wait_ge(ready.sem, 3)

            def gather(i, n):
                pe.wait_ge(loaded.sem, loaded.at(i, 6 * (n + 1)))
                for b in range(QB):
                    for s in range(ST):
                        last = mm(back_in[b], ct[:, b // GB, b % GB, s, :], eo[:, b // GB, s, :], start=s == 0, stop=s == ST - 1)
                    last.then_inc(gathered.sem, 1)

            gather(0, 0)
            with pe.Fori(0, B // QB) as i:
                pe.wait_ge(x4_done.sem, x4_done.at(i, 0))
                for b in range(QB):
                    pe.wait_ge(x3_done.sem, x3_done.at(i, b + 1))
                    for kc in range(KC):
                        last = nc.tensor.transpose(bank[2 + kc][:, b * T:(b + 1) * T], x3[:, b, kc * 128:(kc + 1) * 128], ident[0:T, 0:T])
                last.then_inc(x3t_done.sem, 1)
                pe.wait_ge(x3t_sb.sem, x3t_sb.at(i, 1))
                for k in range(2 * DT):
                    pe.wait_ge(xr_sb.sem, xr_sb.at(i, max(k - 1, 0)))
                    for kc in range(KC):
                        last = mm(bank[4 + k % 2][:, 0:QT], win[:, kc, k * 128:(k + 1) * 128], x3t[:, kc, :], start=kc == 0, stop=kc == KC - 1)
                    last.then_inc(xr.sem, 1)
                for k in range(DT):
                    pe.wait_ge(us_done.sem, us_done.at(i, k + 1))
                    last = mm(bank[6][0:XD, 0:QT], wx[:, k, :], us[:, k, :], start=k == 0, stop=k == DT - 1)
                last.then_inc(xd_done.sem, 1)
                pe.wait_ge(xd_sb.sem, xd_sb.at(i, 1))
                pe.wait_ge(xr_sb.sem, xr_sb.at(i, 2 * DT))

                def spread(k):
                    pe.wait_ge(bc_sb.sem, bc_sb.at(i, max(k + 1 - SPREAD, 0)))
                    row = row_of[:, (k % 2) * NST + k // 2, :]
                    mm(bank[k % SPREAD][:, 0:QT], row, xd_hi[:, :], start=True, stop=False)
                    mm(bank[k % SPREAD][:, 0:QT], row, xd_lo[:, :], start=False, stop=True).then_inc(bc_done.sem, 1)

                pe.wait_ge(xd_split.sem, xd_split.at(i, 1))
                for k in range(4):
                    spread(k)
                for k in range(DT):
                    pe.wait_ge(z_done.sem, z_done.at(i, max(k - 1, 0)))
                    mm(bank[4 + k % 2][:, 0:QT], wdt[:, k * 128:(k + 1) * 128], xd[0:RANK, :], start=True, stop=True).then_inc(dz.sem, 1)

                pe.wait_ge(z_done.sem, z_done.at(i, DT))
                for k in range(4, SPREAD):
                    spread(k)
                for k in range(DT * NST):
                    for n in range(SPREAD + 2 * k, SPREAD + 2 * k + 2):
                        if n < 2 * NST:
                            spread(n)
                    if k == DT * NST - 8:
                        pe.wait_ge(bc_sb.sem, bc_sb.at(i, 2 * NST))
                        gather(i, 1)
                    n, dt = k % NST, k // NST
                    if n == 0:
                        pe.wait_ge(y_done.sem, y_done.at(i, max(dt - 1, 0)))
                    pe.wait_ge(weighted.sem, weighted.at(i, k + 1))
                    mm(bank[6 + dt % 2][:, 0:QT], ident[:, :], out_c[:, k % 2, :], start=n == 0, stop=n == NST - 1).then_inc(summed.sem, 1)
                pe.wait_ge(y_done.sem, y_done.at(i, DT))
                for b in range(QB):
                    for k in range(DT):
                        last = mm(bank[b][0:T, 0:D], rs[:, k, b * T:(b + 1) * T], wout[:, k, :], start=k == 0, stop=k == DT - 1)
                    last.then_inc(out_done.sem, 1)

        @block.scalar
        def _(act):
            fn = nc.scalar.activation
            act.wait_ge(weights.sem, 16 * len(loads))
            fn(flat(aneg[:, :, :]), flat(alog[:, :, :]), ACT.Exp).then_inc(ready.sem, 1)
            act.wait_ge(ready.sem, 3)
            with act.Fori(0, B // QB) as i:
                act.wait_ge(x3t_done.sem, x3t_done.at(i, 1))
                fn(x3t[:, 0, :], bank[2][:, 0:QT], ACT.Copy)
                fn(x3t[:, 1, :], bank[3][:, 0:QT], ACT.Copy).then_inc(x3t_sb.sem, 1)
                for k in range(2 * DT):
                    act.wait_ge(xr.sem, xr.at(i, k + 1))
                    src = bank[4 + k % 2][:, 0:QT]
                    if k < DT:
                        fn(u[:, k, :, TAPS - 1:], src.rearrange("p (b t) -> p b t", b=QB), ACT.Copy).then_inc(xr_sb.sem, 1)
                    else:
                        fn(rs[:, k - DT, :], src, ACT.Silu).then_inc(xr_sb.sem, 1)
                for k in range(DT):
                    act.wait_ge(conv_done.sem, conv_done.at(i, k + 1))
                    fn(us[:, k, :], conv[:, k, :], ACT.Silu, bias=convb[:, k:k + 1]).then_inc(us_done.sem, 1)
                act.wait_ge(xd_done.sem, xd_done.at(i, 1))
                fn(xd_hi[:, :], bank[6][0:XD, 0:QT], ACT.Copy)
                fn(xd[:, :], bank[6][0:XD, 0:QT], ACT.Copy).then_inc(xd_sb.sem, 1)

                def take_rows(k):
                    for n in range(2):
                        act.wait_ge(bc_done.sem, bc_done.at(i, 2 * k + n + 1))
                        fn(bc[:, n * NST + k, :], bank[(2 * k + n) % SPREAD][:, 0:QT], ACT.Copy).then_inc(bc_sb.sem, 1)

                take_rows(0)
                take_rows(1)
                for k in range(DT):
                    act.wait_ge(z_done.sem, z_done.at(i, k + 1))
                    fn(soft[:, k, :], z[:, k, :], ACT.Abs).then_inc(alink.sem, 1)
                for k in range(DT):
                    act.wait_ge(alink.sem, alink.at(i, k + 1))
                    fn(soft[:, k, :], soft[:, k, :], ACT.Exp, scale=-1.0).then_inc(alink.sem, 1)
                for k in range(DT):
                    act.wait_ge(alink.sem, alink.at(i, DT + k + 1))
                    fn(soft[:, k, :], soft[:, k, :], ACT.Ln, bias=1.0).then_inc(sp_done.sem, 1)
                for k in range(DT * NST):
                    if 2 <= k < NST:
                        take_rows(k)
                    if k % NST == 0:
                        act.wait_ge(du_done.sem, du_done.at(i, k // NST + 1))
                    act.wait_ge(scanned.sem, scanned.at(i, max(k - 1, 0)))
                    by_seq = lambda a: a.rearrange("p (b t) -> p b t", b=QB)[:, :, 1:]
                    fn(by_seq(decay[:, k % 2, :]), by_seq(delta[:, k // NST, :]), ACT.Exp,
                       scale=aneg[:, k // NST, k % NST:k % NST + 1]).then_inc(decayed.sem, 1)

        @block.vector
        def _(dve):
            V = nc.vector
            dve.wait_ge(weights.sem, 16 * len(loads))
            V.tensor_copy(row_of[:, :, :], row_f)
            dve.wait_ge(ready.sem, 2)
            V.tensor_scalar(flat(aneg[:, :, :]), flat(aneg[:, :, :]), -1.0, None, ALU.mult).then_inc(ready.sem, 1)
            tiles = lambda a: [a[:, b, :] for b in range(QB)]

            def take_gathered(i, n):
                dve.wait_ge(loaded.sem, loaded.at(i, 6 * (n + 1)))
                dve.wait_ge(gathered.sem, gathered.at(i, (n + 1) * QB))
                for b in range(QB):
                    V.tensor_tensor(t_next[:, b, :], back_in[b], x2[:, b // GB, b % GB, :], ALU.add).then_inc(g_read.sem, 1)
                dve.wait_ge(g_read.sem, g_read.at(i, (n + 1) * QB))

            take_gathered(0, 0)
            layer_norms(dve, nc, vfirst, 0, tiles(t_next), stats, tiles(x3), [x3_done] * QB)
            with dve.Fori(0, B // QB) as i:
                link = lambda ins: vlink.chain(dve, i, ins)
                for k in range(DT):
                    dve.wait_ge(xr_sb.sem, xr_sb.at(i, k + 1))
                    c3 = conv[:, k, :].rearrange("p (b t) -> p b t", b=QB)
                    link(V.tensor_scalar(c3, u[:, k, :, 0:T], convw[:, k, 0:1], None, ALU.mult))
                    for tap in range(1, TAPS):
                        last = V.scalar_tensor_tensor(c3, u[:, k, :, tap:tap + T], convw[:, k, tap:tap + 1], c3, ALU.mult, ALU.add)
                        if tap < TAPS - 1:
                            link(last)
                    last.then_inc(conv_done.sem, 1)
                dve.wait_ge(xd_sb.sem, xd_sb.at(i, 1))
                V.tensor_tensor(xd_lo[:, :], xd[:, :], xd_hi[:, :].bitcast(F32), ALU.subtract).then_inc(xd_split.sem, 1)
                for k in range(DT):
                    dve.wait_ge(dz.sem, dz.at(i, k + 1))
                    V.tensor_scalar(z[:, k, :], bank[4 + k % 2][:, 0:QT], bdt[:, k:k + 1], None, ALU.add).then_inc(z_done.sem, 1)
                for k in range(DT):
                    dve.wait_ge(sp_done.sem, sp_done.at(i, k + 1))
                    link(V.scalar_tensor_tensor(delta[:, k, :], z[:, k, :], 0.0, soft[:, k, :], ALU.max, ALU.add))
                    V.tensor_tensor(du[:, k, :], delta[:, k, :], us[:, k, :], ALU.mult).then_inc(du_done.sem, 1)
                dve.wait_ge(du_done.sem, du_done.at(i, DT))

                def times_b(k):
                    if k < NST:
                        dve.wait_ge(bc_sb.sem, bc_sb.at(i, 2 * k + 1))
                    dve.wait_ge(scanned.sem, scanned.at(i, max(k - 2, 0)))
                    V.tensor_tensor(bu[:, k % 3, :], du[:, k // NST, :], bc[:, k % NST, :], ALU.mult).then_inc(bu_done.sem, 1)

                def gate(dt):
                    dve.wait_ge(summed.sem, summed.at(i, (dt + 1) * NST))
                    link(V.scalar_tensor_tensor(conv[:, dt, :], us[:, dt, :], dp[:, dt:dt + 1], bank[6 + dt % 2][:, 0:QT], ALU.mult, ALU.add))
                    V.tensor_tensor(rs[:, dt, :], conv[:, dt, :], rs[:, dt, :], ALU.mult).then_inc(y_done.sem, 1)

                times_b(0)
                for k in range(DT * NST):
                    if k + 1 < DT * NST:
                        times_b(k + 1)
                    dve.wait_ge(bu_done.sem, bu_done.at(i, k + 1))
                    dve.wait_ge(decayed.sem, decayed.at(i, k + 1))
                    dve.wait_ge(weighted.sem, weighted.at(i, max(k - 1, 0)))
                    V.tensor_tensor_scan(state[:, k % 2, :], decay[:, k % 2, :], bu[:, k % 3, :], 0.0, ALU.mult, ALU.add).then_inc(scanned.sem, 1)
                    if k % NST == 4 and k > NST:
                        gate(k // NST - 1)
                gate(DT - 1)
                take_gathered(i, 1)
                dve.wait_ge(saved.sem, saved.at(i, 0))
                for b in range(QB):
                    dve.wait_ge(out_done.sem, out_done.at(i, b + 1))
                    last = V.tensor_tensor(t[:, b, :], bank[b][0:T, 0:D], x3[:, b, :], ALU.add)
                link(last)
                layer_norms(dve, nc, vlink, i, tiles(t_next) + tiles(t), stats, tiles(x3) + tiles(x4), [x3_done] * QB + [x4_done] * QB)
            assert vlink.seen == vlink.per, vlink.seen

ROUNDS = 3
RMS_EPS = 1e-6
SLOT_INPUTS = ["ctxt", "ctx_rows", "wk", "wv", "wq", "wih", "whh", "L1_xattn_gru_bih", "L1_xattn_gru_bhh", "snorm", "inorm", "ident"]


def slot_phase(nc, d, own):
    ctx = ExitStack()
    with ctx:
        def sb(name, shape, dt=F32):
            return ctx.enter_context(nc.sbuf_tensor("d_" + name, shape, dt))

        def sem(name, per, unit=1, early=False):
            return Steps(own("d_" + name, early), per, unit, early)

        wk = sb("wk", [128, KC, D])
        wv = sb("wv", [128, KC, D])
        wq = sb("wq", [128, KC, D])
        wih = sb("wih", [128, KC, 3 * D])
        whh = sb("whh", [128, KC, 3 * D])
        bih = sb("bih", [T, 3 * D])
        bhh = sb("bhh", [T, 3 * D])
        snorm = sb("snorm", [128, KC])
        inorm = sb("inorm", [128, KC])
        ident = sb("ident", [128, 128])

        ctxt = sb("ctxt", [128, QB, KC, S2])
        rows = sb("rows", [KP, QB, KT, D])
        x4 = sb("x4", [T, QB, D])
        csq = sb("csq", [KP, QB, KT, D])
        ssq = sb("ssq", [T, QB, D])
        csum = sb("csum", [KP, QB, KT])
        cinv = sb("cinv", [KP, QB, KT])
        ctmp = sb("ctmp", [KP, QB, KT])
        cscale = sb("cscale", [KP, QB, KT])
        kt = sb("kt", [128, QB, KC, S2])
        v = sb("v", [KP, QB, KT, D + 1])
        ssum = sb("ssum", [T, QB])
        sinv = sb("sinv", [T, QB])
        stmp = sb("stmp", [T, QB])
        s = sb("s", [T, QB, D])
        sn = sb("sn", [T, QB, D])
        stn = sb("stn", [128, QB, 2 * KC, T])
        qt = sb("qt", [128, QB, KC, T])
        smax = sb("smax", [KP, QB, KT])
        nmax = sb("nmax", [KP, QB, KT])
        esum = sb("esum", [KP, QB, KT])
        einv = sb("einv", [KP, QB, KT])
        e = sb("e", [KP, QB, KT, T])
        den = sb("den", [T, QB])
        upd = sb("upd", [T, QB, D])
        ut = sb("ut", [128, QB, KC, T])
        rz = sb("rz", [T, QB, 2 * D])
        hn = sb("hn", [T, QB, D])
        xn = sb("xn", [T, QB, D])
        cand = sb("cand", [T, QB, D])
        t = sb("t", [T, QB, D])
        stats = sb("stats", [T, QB, 10])
        x5 = sb("x5", [T, QB, D])
        small = [ctx.enter_context(nc.psum_tensor(f"d_small{j}", [128, 512], F32)) for j in range(GB)]
        wide = [ctx.enter_context(nc.psum_tensor(f"d_wide{j}", [128, 512], F32)) for j in range(GB)]
        gates = [ctx.enter_context(nc.psum_tensor(f"d_gates{j}", [128, 512], F32)) for j in range(GB)]
        news = [ctx.enter_context(nc.psum_tensor(f"d_news{j}", [128, 512], F32)) for j in range(GB)]

        N = ROUNDS * QB
        weights = sem("weights", 1)
        ready = sem("ready", 1)
        in_ctx = [sem(f"in_ctx{j}", 2, 16) for j in range(QB)]
        in_x = [sem(f"in_x{j}", 1, 16) for j in range(QB)]
        squares = sem("squares", QB)
        kproj = sem("kproj", QB)
        k_sb = sem("k_sb", QB)
        vproj = sem("vproj", QB * KT)
        v_sb = sem("v_sb", QB * KT, early=True)
        s_sq = sem("s_sq", N)
        sn_done = sem("sn_done", N)
        stn_done = sem("stn_done", N)
        stn_sb = sem("stn_sb", N)
        q_done = sem("q_done", N)
        q_sb = sem("q_sb", N)
        score = sem("score", N)
        max_done = sem("max_done", N)
        exp_done = sem("exp_done", N)
        attn = sem("attn", N)
        u_done = sem("u_done", N)
        upd_done = sem("upd_done", N)
        ut_done = sem("ut_done", N)
        ut_sb = sem("ut_sb", N)
        gru = sem("gru", N)
        rz_sb = sem("rz_sb", N, early=True)
        rz_tanh = sem("rz_tanh", N)
        pre_n = sem("pre_n", N)
        n_tanh = sem("n_tanh", N)
        s_done = sem("s_done", N, early=True)
        x5_done = sem("x5_done", QB, early=True)
        stored = sem("stored", 1, 16)
        saved = sem("saved", 1, early=True)
        vlink = sem("vlink", 253)
        block = ctx.enter_context(nc.Block())
        loads = [(wk[:, :, :], d["wk"]), (wv[:, :, :], d["wv"]), (wq[:, :, :], d["wq"]), (wih[:, :, :], d["wih"]), (whh[:, :, :], d["whh"]),
                 (bih[:, :], d["L1_xattn_gru_bih"].partition_broadcast(T)), (bhh[:, :], d["L1_xattn_gru_bhh"].partition_broadcast(T)),
                 (snorm[:, :], d["snorm"]), (inorm[:, :], d["inorm"]), (ident[:, :], d["ident"])]

        pairs = [range(g, g + GB) for g in range(0, QB, GB)]

        def slots(r, j):
            return x4[:, j, :] if r == 0 else s[:, j, :]

        @block.sync
        def _(sp):
            for dst, src in loads:
                sp.dma_start(dst, src).then_inc(weights.sem, 16)
            with sp.Fori(0, B // QB) as i:
                sp.wait_ge(v_sb.sem, v_sb.at(i, 0))
                for j in range(QB):
                    sp.dma_start(ctxt[:, j, :, :], d["ctxt"][i * QB + j]).then_inc(in_ctx[j].sem, 16)
                    sp.dma_start(rows[:, j, :, :], d["ctx_rows"][i * QB + j]).then_inc(in_ctx[j].sem, 16)
                sp.wait_ge(x5_done.sem, x5_done.at(i, 0))
                for j in range(QB):
                    sp.dma_start(x4[:, j, :], d["s_x4"][i * QB + j]).then_inc(in_x[j].sem, 16)

        @block.gpsimd
        def _(pool):
            with pool.Fori(0, B // QB) as i:
                pool.wait_ge(x5_done.sem, x5_done.at(i, QB))
                pool.dma_start(d["s_x5_by_four"][i], x5[:, :, :]).then_inc(stored.sem, 16)
                pool.wait_ge(stored.sem, stored.at(i, 1))
                pool.sem_inc(saved.sem, 1)

        @block.tensor
        def _(pe):
            mm = nc.tensor.matmul
            pe.wait_ge(ready.sem, 1)
            with pe.Fori(0, B // QB) as i:
                for j in range(QB):
                    b = j % GB
                    pe.wait_ge(in_ctx[j].sem, in_ctx[j].at(i, 2))
                    pe.wait_ge(rz_sb.sem, rz_sb.at(i, 0))
                    if j >= GB:
                        pe.wait_ge(v_sb.sem, v_sb.at(i, (j - GB + 1) * KT))
                    for oc, bank in enumerate((gates[b], news[b])):
                        for kc in range(KC):
                            last = mm(bank[:, 0:S2], wk[:, kc, oc * 128:(oc + 1) * 128], ctxt[:, j, kc, :], start=kc == 0, stop=kc == KC - 1)
                    last.then_inc(kproj.sem, 1)
                    for k, bank in enumerate((small[b], wide[b], gates[b])):
                        if k == 2:
                            pe.wait_ge(k_sb.sem, k_sb.at(i, j + 1))
                        for kc in range(KC):
                            last = mm(bank[0:KP, 0:D], ctxt[:, j, kc, k * KP:(k + 1) * KP], wv[:, kc, :], start=kc == 0, stop=kc == KC - 1)
                        last.then_inc(vproj.sem, 1)

                def front(r, pair):
                    for j in pair:
                        n = r * QB + j
                        pe.wait_ge(sn_done.sem, sn_done.at(i, n + 1))
                        if r == 0:
                            pe.wait_ge(v_sb.sem, v_sb.at(i, QB * KT))
                        for m, src in enumerate((slots(r, j), sn[:, j, :])):
                            for kc in range(KC):
                                c = m * KC + kc
                                last = nc.tensor.transpose(small[j % GB][:, c * T:(c + 1) * T], src[:, kc * 128:(kc + 1) * 128], ident[0:T, 0:T])
                        last.then_inc(stn_done.sem, 1)
                    for j in pair:
                        n = r * QB + j
                        pe.wait_ge(stn_sb.sem, stn_sb.at(i, n + 1))
                        for oc in range(KC):
                            for kc in range(KC):
                                last = mm(small[j % GB][:, oc * T:(oc + 1) * T], wq[:, kc, oc * 128:(oc + 1) * 128], stn[:, j, KC + kc, :],
                                          start=kc == 0, stop=kc == KC - 1)
                        last.then_inc(q_done.sem, 1)
                    for j in pair:
                        n = r * QB + j
                        pe.wait_ge(q_sb.sem, q_sb.at(i, n + 1))
                        if j >= GB:
                            pe.wait_ge(exp_done.sem, exp_done.at(i, n - GB + 1))
                        for k in range(KT):
                            for kc in range(KC):
                                last = mm(wide[j % GB][0:KP, k * T:(k + 1) * T], kt[:, j, kc, k * KP:(k + 1) * KP], qt[:, j, kc, :],
                                          start=kc == 0, stop=kc == KC - 1)
                        last.then_inc(score.sem, 1)

                def back(r, pair):
                    for j in pair:
                        n = r * QB + j
                        pe.wait_ge(attn.sem, attn.at(i, n + 1))
                        for k in range(KT):
                            last = mm(small[j % GB][0:T, 0:D + 1], e[:, j, k, :], v[:, j, k, :], start=k == 0, stop=k == KT - 1)
                        last.then_inc(u_done.sem, 1)
                    for j in pair:
                        if j >= GB:
                            pe.wait_ge(rz_sb.sem, rz_sb.at(i, r * QB + j - GB + 1))
                        for kc in range(KC):
                            mm(gates[j % GB][0:T, :], stn[:, j, kc, :], whh[:, kc, 0:2 * D], start=kc == 0, stop=False)
                        for kc in range(KC):
                            mm(news[j % GB][0:T, D:2 * D], stn[:, j, kc, :], whh[:, kc, 2 * D:3 * D], start=kc == 0, stop=kc == KC - 1)
                    for j in pair:
                        n = r * QB + j
                        pe.wait_ge(upd_done.sem, upd_done.at(i, n + 1))
                        if j < GB:
                            pe.wait_ge(exp_done.sem, exp_done.at(i, n + GB + 1))
                        for kc in range(KC):
                            last = nc.tensor.transpose(wide[j % GB][:, kc * T:(kc + 1) * T], upd[:, j, kc * 128:(kc + 1) * 128], ident[0:T, 0:T])
                        last.then_inc(ut_done.sem, 1)
                    for j in pair:
                        n = r * QB + j
                        pe.wait_ge(ut_sb.sem, ut_sb.at(i, n + 1))
                        for kc in range(KC):
                            mm(gates[j % GB][0:T, :], ut[:, j, kc, :], wih[:, kc, 0:2 * D], start=False, stop=kc == KC - 1)
                        for kc in range(KC):
                            last = mm(news[j % GB][0:T, 0:D], ut[:, j, kc, :], wih[:, kc, 2 * D:3 * D], start=kc == 0, stop=kc == KC - 1)
                        last.then_inc(gru.sem, 1)

                for r in range(ROUNDS):
                    for pair in pairs:
                        front(r, pair)
                    for pair in pairs:
                        back(r, pair)

        @block.scalar
        def _(act):
            fn = nc.scalar.activation
            act.wait_ge(ready.sem, 1)
            with act.Fori(0, B // QB) as i:
                for j in range(QB):
                    act.wait_ge(in_ctx[j].sem, in_ctx[j].at(i, 2))
                    for k in range(KT):
                        last = fn(csq[:, j, k, :], rows[:, j, k, :], ACT.Square, accum_out=csum[:, j, k:k + 1])
                    last.then_inc(squares.sem, 1)
                    act.wait_ge(kproj.sem, kproj.at(i, j + 1))
                    fn(kt[:, j, 0, :], gates[j % GB][:, 0:S2], ACT.Copy)
                    fn(kt[:, j, 1, :], news[j % GB][:, 0:S2], ACT.Copy).then_inc(k_sb.sem, 1)

                def square(r, pair):
                    for j in pair:
                        if r == 0:
                            act.wait_ge(in_x[j].sem, in_x[j].at(i, 1))
                        else:
                            act.wait_ge(s_done.sem, s_done.at(i, (r - 1) * QB + j + 1))
                        fn(ssq[:, j, :], slots(r, j), ACT.Square, accum_out=ssum[:, j:j + 1]).then_inc(s_sq.sem, 1)

                def take_slots(r, pair):
                    for j in pair:
                        act.wait_ge(stn_done.sem, stn_done.at(i, r * QB + j + 1))
                        fn(stn[:, j, :, :].rearrange("p c t -> p (c t)"), small[j % GB][:, 0:2 * KC * T], ACT.Copy).then_inc(stn_sb.sem, 1)

                def take_queries(r, pair):
                    for j in pair:
                        act.wait_ge(q_done.sem, q_done.at(i, r * QB + j + 1))
                        fn(qt[:, j, :, :].rearrange("p c t -> p (c t)"), small[j % GB][:, 0:KC * T], ACT.Copy).then_inc(q_sb.sem, 1)

                def exps(r, pair):
                    for j in pair:
                        act.wait_ge(max_done.sem, max_done.at(i, r * QB + j + 1))
                        for k in range(KT):
                            last = fn(e[:, j, k, :], wide[j % GB][0:KP, k * T:(k + 1) * T], ACT.Exp, bias=nmax[:, j, k:k + 1],
                                      scale=cscale[:, j, k:k + 1], accum_out=esum[:, j, k:k + 1])
                        last.then_inc(exp_done.sem, 1)

                def take_updates(r, pair):
                    for j in pair:
                        act.wait_ge(ut_done.sem, ut_done.at(i, r * QB + j + 1))
                        fn(ut[:, j, :, :].rearrange("p c t -> p (c t)"), wide[j % GB][:, 0:KC * T], ACT.Copy).then_inc(ut_sb.sem, 1)

                def gates_tanh(r, pair):
                    for j in pair:
                        act.wait_ge(rz_sb.sem, rz_sb.at(i, r * QB + j + 1))
                        fn(rz[:, j, :], rz[:, j, :], ACT.Tanh, scale=0.5).then_inc(rz_tanh.sem, 1)

                def candidates(r, pair):
                    for j in pair:
                        act.wait_ge(pre_n.sem, pre_n.at(i, r * QB + j + 1))
                        fn(cand[:, j, :], xn[:, j, :], ACT.Tanh).then_inc(n_tanh.sem, 1)

                a, b = pairs
                square(0, a)
                take_slots(0, a)
                take_queries(0, a)
                square(0, b)
                take_slots(0, b)
                exps(0, a)
                take_queries(0, b)
                exps(0, b)
                for r in range(ROUNDS):
                    more = r + 1 < ROUNDS
                    take_updates(r, a)
                    gates_tanh(r, a)
                    candidates(r, a)
                    take_updates(r, b)
                    if more:
                        square(r + 1, a)
                    gates_tanh(r, b)
                    if more:
                        take_slots(r + 1, a)
                    candidates(r, b)
                    if more:
                        take_queries(r + 1, a)
                        square(r + 1, b)
                        take_slots(r + 1, b)
                        exps(r + 1, a)
                        take_queries(r + 1, b)
                        exps(r + 1, b)

        @block.vector
        def _(dve):
            V = nc.vector
            dve.wait_ge(weights.sem, 16 * len(loads))
            V.memset(v[:, :, :, :].rearrange("p a b c -> p (a b c)"), 1.0)
            for kc in range(KC):
                V.tensor_scalar(wk[:, kc, :], wk[:, kc, :], inorm[:, kc:kc + 1], None, ALU.mult)
                V.tensor_scalar(wv[:, kc, :], wv[:, kc, :], inorm[:, kc:kc + 1], None, ALU.mult)
                V.tensor_scalar(wq[:, kc, :], wq[:, kc, :], snorm[:, kc:kc + 1], None, ALU.mult)
            V.tensor_tensor(bih[:, 0:2 * D], bih[:, 0:2 * D], bhh[:, 0:2 * D], ALU.add).then_inc(ready.sem, 1)
            dve.wait_ge(ready.sem, 1)
            with dve.Fori(0, B // QB) as i:
                link = lambda ins: vlink.chain(dve, i, ins)
                for j in range(QB):
                    dve.wait_ge(squares.sem, squares.at(i, j + 1))
                    link(V.tensor_scalar(csum[:, j, :], csum[:, j, :], 1.0 / D, RMS_EPS, ALU.mult, ALU.add))
                    inverse_root(dve, nc, vlink, i, csum[:, j, :], cinv[:, j, :], ctmp[:, j, :])
                    link(V.tensor_scalar(cscale[:, j, :], cinv[:, j, :], D ** -0.5, None, ALU.mult))
                    for k, bank in enumerate((small[j % GB], wide[j % GB], gates[j % GB])):
                        dve.wait_ge(vproj.sem, vproj.at(i, j * KT + k + 1))
                        V.tensor_scalar(v[:, j, k, 0:D], bank[0:KP, 0:D], cinv[:, j, k:k + 1], None, ALU.mult).then_inc(v_sb.sem, 1)

                def norm(r, pair):
                    both = slice(pair[0], pair[0] + GB)
                    dve.wait_ge(s_sq.sem, s_sq.at(i, r * QB + pair[-1] + 1))
                    link(V.tensor_scalar(ssum[:, both], ssum[:, both], 1.0 / D, RMS_EPS, ALU.mult, ALU.add))
                    inverse_root(dve, nc, vlink, i, ssum[:, both], sinv[:, both], stmp[:, both])
                    for j in pair:
                        V.tensor_scalar(sn[:, j, :], slots(r, j), sinv[:, j:j + 1], None, ALU.mult).then_inc(sn_done.sem, 1)

                def front(r, pair):
                    for j in pair:
                        dve.wait_ge(score.sem, score.at(i, r * QB + j + 1))
                        link(V.tensor_reduce(smax[:, j, :], wide[j % GB][0:KP, 0:KT * T].rearrange("p (k t) -> p k t", k=KT), AX.X, ALU.max))
                        V.scalar_tensor_tensor(nmax[:, j, :], smax[:, j, :], -1.0, cscale[:, j, :], ALU.mult, ALU.mult).then_inc(max_done.sem, 1)
                    for j in pair:
                        dve.wait_ge(exp_done.sem, exp_done.at(i, r * QB + j + 1))
                        link(V.reciprocal(einv[:, j, :], esum[:, j, :]))
                        V.tensor_tensor(e[:, j, :, :], e[:, j, :, :], einv[:, j, :].unsqueeze(2).broadcast_to([KP, KT, T]), ALU.mult).then_inc(attn.sem, 1)

                def updates(r, pair):
                    for j in pair:
                        dve.wait_ge(u_done.sem, u_done.at(i, r * QB + j + 1))
                        link(V.tensor_scalar(den[:, j:j + 1], small[j % GB][0:T, D:D + 1], RMS_EPS, None, ALU.add))
                        link(V.reciprocal(den[:, j:j + 1], den[:, j:j + 1]))
                        V.tensor_scalar(upd[:, j, :], small[j % GB][0:T, 0:D], den[:, j:j + 1], None, ALU.mult).then_inc(upd_done.sem, 1)

                def take_gates(r, pair):
                    for j in pair:
                        dve.wait_ge(gru.sem, gru.at(i, r * QB + j + 1))
                        V.tensor_tensor(hn[:, j, :], news[j % GB][0:T, D:2 * D], bhh[:, 2 * D:3 * D], ALU.add)
                        link(V.tensor_tensor(xn[:, j, :], news[j % GB][0:T, 0:D], bih[:, 2 * D:3 * D], ALU.add))
                        V.tensor_tensor(rz[:, j, :], gates[j % GB][0:T, :], bih[:, 0:2 * D], ALU.add).then_inc(rz_sb.sem, 1)

                def renew(r, pair):
                    for j in pair:
                        dve.wait_ge(rz_tanh.sem, rz_tanh.at(i, r * QB + j + 1))
                        link(V.tensor_scalar(rz[:, j, :], rz[:, j, :], 0.5, 0.5, ALU.mult, ALU.add))
                        link(V.tensor_tensor(hn[:, j, :], rz[:, j, 0:D], hn[:, j, :], ALU.mult))
                        V.tensor_tensor(xn[:, j, :], xn[:, j, :], hn[:, j, :], ALU.add).then_inc(pre_n.sem, 1)
                    for j in pair:
                        dve.wait_ge(n_tanh.sem, n_tanh.at(i, r * QB + j + 1))
                        link(V.tensor_tensor(t[:, j, :], slots(r, j), cand[:, j, :], ALU.subtract))
                        link(V.tensor_tensor(t[:, j, :], t[:, j, :], rz[:, j, D:2 * D], ALU.mult))
                        V.tensor_tensor(s[:, j, :], t[:, j, :], cand[:, j, :], ALU.add).then_inc(s_done.sem, 1)

                a, b = pairs
                norm(0, a)
                norm(0, b)
                front(0, a)
                front(0, b)
                for r in range(ROUNDS):
                    updates(r, a)
                    take_gates(r, a)
                    updates(r, b)
                    renew(r, a)
                    if r + 1 < ROUNDS:
                        norm(r + 1, a)
                    take_gates(r, b)
                    renew(r, b)
                    if r + 1 < ROUNDS:
                        norm(r + 1, b)
                        front(r + 1, a)
                        front(r + 1, b)
                dve.wait_ge(saved.sem, saved.at(i, 0))
                dve.wait_ge(s_done.sem, s_done.at(i, N))
                link(V.tensor_tensor(t[:, :, :], x4[:, :, :], s[:, :, :], ALU.add))
                layer_norms(dve, nc, vlink, i, [t[:, j, :] for j in range(QB)], stats, [x5[:, j, :] for j in range(QB)], [x5_done] * QB)
            assert vlink.seen == vlink.per, vlink.seen

DFF = 1024
FT = DFF // 128
NT = B * T // 128
TOP = 24
XW = D + 2
MOST = 2 * NT + E - 1
PER = 6
JOBS = (MOST + PER - 1) // PER * PER
NV = E + 1
HASH_INPUTS = ["ident", "W1", "b1", "W2", "L1_ffn_b2", "count_to", "eights", "expert_no", "expert_before", "token_no", "before128", "ones128",
               "v_no", "v_before", "tile_start", "pair_before", "pair_is", "pair_base", "pair_v", "pair_vals", "job_no"]


def hashed_phase(nc, d, own):
    ctx = ExitStack()
    with ctx:
        def sb(name, shape, dt=F32):
            return ctx.enter_context(nc.sbuf_tensor("e_" + name, shape, dt))

        def sem(name, per, unit=1, early=False):
            return Steps(own("e_" + name, early), per, unit, early)

        ident = sb("ident", [128, 128])
        before128 = sb("before128", [128, 128])
        ones128 = sb("ones128", [128, 128])
        token_no = sb("token_no", [128, NT])
        count_to = sb("count_to", [128, TOP])
        eights = sb("eights", [128, TOP // 4])
        expert_no = sb("expert_no", [128, E])
        expert_before = sb("expert_before", [128, E])
        v_no = sb("v_no", [128, NV + 1])
        v_before = sb("v_before", [128, NV + 1])
        tile_start = sb("tile_start", [128, NT])
        pair_before = sb("pair_before", [128, NT])
        pair_is = sb("pair_is", [128, NT])
        pair_base = sb("pair_base", [128, 1])
        pair_v = sb("pair_v", [128, 1])
        pair_vals = sb("pair_vals", [128, 3])
        job_no = sb("job_no", [128, JOBS + 2])
        b2 = sb("b2", [E, D])
        x = sb("x", [128, NT, XW])
        xt = sb("xt", [128, NT, KC, 128])
        acc = sb("acc", [128, NT, D])
        h1 = sb("h1", [128, NT])
        h2 = sb("h2", [128, NT])
        h3 = sb("h3", [128, NT])
        cmp = sb("cmp", [128, NT, TOP])
        is_h = sb("is_h", [128, E, NT])
        total = sb("total", [128, E, NT])
        upto = sb("upto", [128, E, NT])
        place = sb("place", [128, NT])
        place_i = sb("place_i", [128, NT], I32)
        lowest = sb("lowest", [128, NT])
        highest = sb("highest", [128, NT])
        reach = sb("reach", [128, 4, NT])
        pair = sb("pair", [128, 8])
        is_job = sb("is_job", [128, JOBS + 2])
        table = sb("table", [1, 3, JOBS + 2], I32)
        origin = sb("origin", [128, NT], I32)
        eq1 = sb("eq1", [128, NT, NV + 1])
        share = sb("share", [128, NT, E])
        share_v = sb("share_v", [128, NT, NV + 1])
        share_t = sb("share_t", [E, NT, 128])
        w1 = sb("w1", [128, E * KC * DFF])
        w2 = sb("w2", [128, E * FT * D])
        b1 = sb("b1", [128, E * FT])
        xj = sb("xj", [128, 2, KC, 128])
        b1j = sb("b1j", [128, 3, FT])
        hid = sb("hid", [128, DFF])
        hid_t = sb("hid_t", [128, 2, FT, 128])
        stats = sb("stats", [128, NT, 10])
        up = [ctx.enter_context(nc.psum_tensor(f"e_up{n}", [128, 512], F32)) for n in range(4)]
        turn = [ctx.enter_context(nc.psum_tensor(f"e_turn{n}", [128, 512], F32)) for n in range(2)]
        down = [ctx.enter_context(nc.psum_tensor(f"e_down{n}", [128, 512], F32)) for n in range(2)]

        first = sem("first", 1)
        loaded = sem("loaded", 1, 16)
        loaded2 = sem("loaded2", 1, 16)
        hashed = sem("hashed", 1)
        ranked = sem("ranked", 1)
        placed = sem("placed", 1)
        sent = sem("sent", 1, 16)
        sorted_in = sem("sorted_in", 1, 16)
        jobs_known = sem("jobs_known", 1)
        drawn = sem("drawn", 1)
        tabled = sem("tabled", 1)
        turned = sem("turned", 1)
        xt_sb = sem("xt_sb", 1)
        shares = sem("shares", 1)
        share_turned = sem("share_turned", 1)
        share_sb = sem("share_sb", 1)
        bias_done = sem("bias_done", 1)
        acc0 = sem("acc0", 1)
        job_in = sem("job_in", PER)
        up_done = sem("up_done", PER * 2, early=3)
        hid_sb = sem("hid_sb", PER * 2, early=3)
        hid_turned = sem("hid_turned", PER * 2, early=True)
        relu_done = sem("relu_done", PER * 2, early=3)
        down_done = sem("down_done", PER, early=3)
        added = sem("added", PER, early=3)
        normed = sem("normed", NT)
        stored = sem("stored", 1, 16)
        vlink = sem("vlink", 1)
        block = ctx.enter_context(nc.Block())
        loads = [(x[:, :, 0:D], d["s_x5_by_tile"]), (token_no[:, :], d["token_no"]), (ident[:, :], d["ident"]), (count_to[:, :], d["count_to"]),
                 (eights[:, :], d["eights"]), (expert_no[:, :], d["expert_no"]), (expert_before[:, :], d["expert_before"]), (b2[:, :], d["L1_ffn_b2"]),
                 (before128[:, :], d["before128"]), (ones128[:, :], d["ones128"]), (v_no[:, :], d["v_no"]), (v_before[:, :], d["v_before"]),
                 (tile_start[:, :], d["tile_start"]), (pair_before[:, :], d["pair_before"]), (pair_is[:, :], d["pair_is"]),
                 (pair_base[:, :], d["pair_base"]), (pair_v[:, :], d["pair_v"]), (pair_vals[:, :], d["pair_vals"]), (job_no[:, :], d["job_no"])]

        @block.sync
        def _(sp):
            for dst, src in loads:
                sp.dma_start(dst, src).then_inc(first.sem, 16)
            for e in range(E):
                sp.dma_start(w1[:, e * KC * DFF:(e + 1) * KC * DFF].rearrange("p (k f) -> p k f", k=KC), d["W1"][e]).then_inc(loaded.sem, 16)
                sp.dma_start(b1[:, e * FT:(e + 1) * FT], d["b1"][e]).then_inc(loaded.sem, 16)
            sp.wait_ge(sorted_in.sem, 16)
            for e in range(E):
                sp.dma_start(w2[:, e * FT * D:(e + 1) * FT * D].rearrange("p (f o) -> p f o", f=FT), d["W2"][e]).then_inc(loaded2.sem, 16)

        @block.gpsimd
        def _(pool):
            pool.wait_ge(placed.sem, 1)
            for t in range(NT):
                pool.indirect_dma_start(d["s_sorted"], bass.IndirectOffsetOnAxis(ap=place_i[:, t:t + 1], axis=0), x[:, t, :], None).then_inc(sent.sem, 16)
            pool.wait_ge(sent.sem, 16 * NT)
            pool.dma_start(x[:, :, :], d["s_sorted_by_tile"]).then_inc(sorted_in.sem, 16)
            for t in range(NT):
                pool.wait_ge(normed.sem, t + 1)
                pool.indirect_dma_start(d["out_rows"], bass.IndirectOffsetOnAxis(ap=origin[:, t:t + 1], axis=0), acc[:, t, :], None).then_inc(stored.sem, 16)
            pool.wait_ge(stored.sem, 16 * NT)

        @block.tensor
        def _(pe):
            mm = nc.tensor.matmul
            pe.wait_ge(first.sem, 16 * len(loads))
            pe.wait_ge(hashed.sem, 1)
            flat = is_h[:, :, :].rearrange("p e t -> p (e t)")
            mm(up[0][:, 0:E * NT], before128[:, :], flat, start=True, stop=True)
            mm(up[1][:, 0:E * NT], ones128[:, :], flat, start=True, stop=True).then_inc(ranked.sem, 1)
            pe.wait_ge(jobs_known.sem, 1)
            for c in range(3):
                last = mm(down[0][0:1, c * (JOBS + 2):(c + 1) * (JOBS + 2)], pair_vals[:, c:c + 1], is_job[:, :], start=True, stop=True)
            last.then_inc(drawn.sem, 1)
            pe.wait_ge(sorted_in.sem, 16)
            for t in range(NT):
                for kc in range(KC):
                    k = t * KC + kc
                    if k % 4 == 0 and k >= 16:
                        pe.wait_ge(xt_sb.sem, k // 4 - 3)
                    last = nc.tensor.transpose(up[k // 4 % 4][:, (k % 4) * 128:(k % 4 + 1) * 128], x[:, t, kc * 128:(kc + 1) * 128], ident[:, :])
                    if k % 4 == 3:
                        last.then_inc(turned.sem, 1)
            pe.wait_ge(shares.sem, 1)
            pe.wait_ge(tabled.sem, 1)
            pe.wait_ge(xt_sb.sem, NT * KC // 4)
            for t in range(NT):
                last = nc.tensor.transpose(up[t // 4][0:E, (t % 4) * 128:(t % 4 + 1) * 128], share[:, t, :], ident[:, :])
            last.then_inc(share_turned.sem, 1)
            pe.wait_ge(share_sb.sem, 1)
            for t in range(NT):
                if t >= 2:
                    pe.wait_ge(acc0.sem, t - 1)
                mm(down[t % 2][:, 0:D], share_t[:, t, :], b2[:, :], start=True, stop=True).then_inc(bias_done.sem, 1)
            pe.wait_ge(acc0.sem, NT)
            pe.wait_ge(loaded.sem, 16 * 2 * E)

            def expert(i, k):
                return pe.value_load(table[0:1, 1, bass.ds(i * PER + k, 1)], min_val=0, max_val=E - 1)

            def rise(i, k, e):
                pe.wait_ge(job_in.sem, job_in.at(i, k + 1))
                pe.wait_ge(hid_sb.sem, hid_sb.at(i, 2 * k - 2))
                for half in range(2):
                    for kc in range(KC):
                        last = mm(up[(2 * k + half) % 4][:, :], xj[:, k % 2, kc, :], w1[:, bass.ds(e * (KC * DFF) + (kc * DFF + half * 512), 512)], start=kc == 0, stop=kc == KC - 1)
                    last.then_inc(up_done.sem, 1)

            def turn_over(i, k):
                for half in range(2):
                    n = 2 * k + half
                    pe.wait_ge(hid_sb.sem, hid_sb.at(i, n + 1))
                    pe.wait_ge(relu_done.sem, relu_done.at(i, n - 1))
                    for f in range(4):
                        c = half * 512 + f * 128
                        last = nc.tensor.transpose(turn[half][:, f * 128:(f + 1) * 128], hid[:, c:c + 128], ident[:, :])
                    last.then_inc(hid_turned.sem, 1)

            def fall(i, k, e):
                pe.wait_ge(added.sem, added.at(i, k - 1))
                pe.wait_ge(relu_done.sem, relu_done.at(i, 2 * k + 2))
                for f in range(FT):
                    last = mm(down[k % 2][:, 0:D], hid_t[:, k % 2, f, :], w2[:, bass.ds(e * (FT * D) + f * D, D)], start=f == 0, stop=f == FT - 1)
                last.then_inc(down_done.sem, 1)

            rise(0, 0, expert(0, 0))
            pe.wait_ge(loaded2.sem, 16 * E)
            with pe.Fori(0, JOBS // PER) as i:
                own_e = expert(i, 0)
                for k in range(PER):
                    next_e = expert(i, k + 1)
                    turn_over(i, k)
                    rise(i, k + 1, next_e)
                    fall(i, k, own_e)
                    own_e = next_e

        @block.scalar
        def _(act):
            fn = nc.scalar.activation
            for k in range(NT * KC // 4):
                act.wait_ge(turned.sem, k + 1)
                fn(xt[:, 2 * k:2 * k + 2, :, :].rearrange("p t k c -> p (t k c)"), up[k % 4][:, :], ACT.Copy).then_inc(xt_sb.sem, 1)
            act.wait_ge(share_turned.sem, 1)
            for k in range((NT + 3) // 4):
                m = min(4, NT - 4 * k)
                last = fn(share_t[:, 4 * k:4 * k + m, :].rearrange("p t c -> p (t c)"), up[k][0:E, 0:m * 128], ACT.Copy)
            last.then_inc(share_sb.sem, 1)
            with act.Fori(0, JOBS // PER) as i:
                for k in range(PER):
                    act.wait_ge(down_done.sem, down_done.at(i, k - 1))
                    for f in range(FT):
                        if f % 4 == 0:
                            act.wait_ge(hid_turned.sem, hid_turned.at(i, 2 * k + f // 4 + 1))
                        last = fn(hid_t[:, k % 2, f, :], turn[f // 4][:, (f % 4) * 128:(f % 4 + 1) * 128], ACT.Relu, bias=b1j[:, k % 3, f:f + 1])
                        if f % 4 == 3:
                            last.then_inc(relu_done.sem, 1)

        @block.vector
        def _(dve):
            V = nc.vector
            link = lambda ins: vlink.chain(dve, 0, ins)
            dve.wait_ge(first.sem, 16 * len(loads))
            link(V.tensor_tensor(h1[:, :], x[:, :, 0], x[:, :, 1], ALU.add))
            link(V.tensor_scalar(h2[:, :], h1[:, :], -1.0, None, ALU.mult))
            link(V.tensor_tensor(h2[:, :], h1[:, :], h2[:, :], ALU.max))
            link(V.tensor_tensor(cmp[:, :, :], h2[:, :].unsqueeze(2).broadcast_to([128, NT, TOP]), count_to[:, :].unsqueeze(1).broadcast_to([128, NT, TOP]), ALU.is_ge))
            link(V.tensor_reduce(h3[:, :], cmp[:, :, :], AX.X, ALU.add))
            link(V.tensor_scalar(h1[:, :], h1[:, :], 0.0, None, ALU.is_lt))
            link(V.tensor_scalar(h1[:, :], h1[:, :], -2.0, 1.0, ALU.mult, ALU.add))
            link(V.tensor_tensor(h1[:, :], h1[:, :], h3[:, :], ALU.mult))
            link(V.tensor_scalar(h1[:, :], h1[:, :], float(TOP), None, ALU.add))
            link(V.tensor_tensor(cmp[:, :, 0:TOP // 4], h1[:, :].unsqueeze(2).broadcast_to([128, NT, TOP // 4]), eights[:, :].unsqueeze(1).broadcast_to([128, NT, TOP // 4]), ALU.is_ge))
            link(V.tensor_reduce(h3[:, :], cmp[:, :, 0:TOP // 4], AX.X, ALU.add))
            link(V.scalar_tensor_tensor(x[:, :, D + 1], h3[:, :], -8.0, h1[:, :], ALU.mult, ALU.add))
            V.tensor_copy(x[:, :, D], token_no[:, :])
            by_hash = lambda a: a.unsqueeze(1).broadcast_to([128, E, NT])
            V.tensor_tensor(is_h[:, :, :], by_hash(x[:, :, D + 1]), expert_no[:, :].unsqueeze(2).broadcast_to([128, E, NT]), ALU.is_equal).then_inc(hashed.sem, 1)
            dve.wait_ge(ranked.sem, 1)
            flat = lambda a: a.rearrange("p e t -> p (e t)")
            link(V.tensor_copy(flat(total[:, :, :]), up[1][:, 0:E * NT]))
            link(V.tensor_tensor_scan(flat(upto[:, :, :]), ones128[:, 0:E * NT], flat(total[:, :, :]), 0.0, ALU.mult, ALU.add))
            link(V.tensor_tensor(flat(total[:, :, :]), flat(upto[:, :, :]), flat(total[:, :, :]), ALU.subtract))
            link(V.tensor_tensor(flat(total[:, :, :]), up[0][:, 0:E * NT], flat(total[:, :, :]), ALU.add))
            link(V.tensor_tensor(total[:, :, :], total[:, :, :], is_h[:, :, :], ALU.mult))
            link(V.tensor_reduce(place[:, :], total[:, :, :].rearrange("p e t -> p t e"), AX.X, ALU.add))
            V.tensor_copy(place_i[:, :], place[:, :]).then_inc(placed.sem, 1)
            ends = upto[:, :, NT - 1].unsqueeze(1).broadcast_to([128, NT, E])
            c8 = cmp[:, :, 0:E]
            for out, shift in ((lowest, 0.0), (highest, 127.0)):
                link(V.tensor_scalar(h1[:, :], tile_start[:, :], shift, None, ALU.add))
                link(V.tensor_tensor(c8, h1[:, :].unsqueeze(2).broadcast_to([128, NT, E]), ends, ALU.is_ge))
                link(V.tensor_reduce(out[:, :], c8, AX.X, ALU.add))
            link(V.tensor_tensor(h1[:, :], highest[:, :], lowest[:, :], ALU.subtract))
            V.tensor_tensor(reach[:, 0, :], h1[:, :], pair_before[:, :], ALU.mult)
            V.tensor_tensor(reach[:, 1, :], lowest[:, :], pair_is[:, :], ALU.mult)
            link(V.tensor_tensor(reach[:, 2, :], highest[:, :], pair_is[:, :], ALU.mult))
            link(V.tensor_reduce(pair[:, 0:3], reach[:, 0:3, :], AX.X, ALU.add))
            link(V.tensor_tensor(pair[:, 3:4], pair[:, 0:1], pair_base[:, :], ALU.add))
            link(V.tensor_tensor(pair[:, 3:4], pair[:, 3:4], pair[:, 1:2], ALU.subtract))
            link(V.tensor_tensor(pair[:, 4:5], pair_v[:, :], pair[:, 1:2], ALU.is_ge))
            link(V.tensor_scalar(pair[:, 5:6], pair[:, 2:3], 1.0, None, ALU.add))
            link(V.tensor_tensor(pair[:, 5:6], pair[:, 5:6], pair_v[:, :], ALU.is_ge))
            link(V.tensor_tensor(pair[:, 4:5], pair[:, 4:5], pair[:, 5:6], ALU.mult))
            V.tensor_scalar(is_job[:, :], job_no[:, :], pair[:, 3:4], pair[:, 4:5], ALU.is_equal, ALU.mult).then_inc(jobs_known.sem, 1)
            dve.wait_ge(drawn.sem, 1)
            V.tensor_copy(table[:, 0:2, :].rearrange("p c n -> p (c n)"), down[0][0:1, 0:2 * (JOBS + 2)]).then_inc(tabled.sem, 1)
            V.tensor_scalar(table[:, 2, :], down[0][0:1, 2 * (JOBS + 2):3 * (JOBS + 2)], float(NV), None, ALU.add).then_inc(tabled.sem, 1)
            dve.wait_ge(sorted_in.sem, 16)
            V.tensor_copy(origin[:, :], x[:, :, D])
            for out, own_no, next_no, n in ((share, expert_no, expert_before, E), (share_v, v_no, v_before, NV + 1)):
                of_h = x[:, :, D + 1].unsqueeze(2).broadcast_to([128, NT, n])
                V.tensor_tensor(eq1[:, :, 0:n], of_h, own_no[:, :].unsqueeze(1).broadcast_to([128, NT, n]), ALU.is_equal)
                link(V.tensor_tensor(out[:, :, :], of_h, next_no[:, :].unsqueeze(1).broadcast_to([128, NT, n]), ALU.is_equal))
                link(V.tensor_tensor(out[:, :, :], out[:, :, :], eq1[:, :, 0:n], ALU.add))
                V.tensor_scalar(out[:, :, :], out[:, :, :], 0.5, None, ALU.mult).then_inc(shares.sem, 1)
            for t in range(NT):
                dve.wait_ge(bias_done.sem, t + 1)
                V.tensor_tensor(acc[:, t, :], down[t % 2][:, 0:D], x[:, t, 0:D], ALU.add).then_inc(acc0.sem, 1)
            dve.wait_ge(acc0.sem, NT)
            dve.wait_ge(shares.sem, 2)
            dve.wait_ge(tabled.sem, 2)
            dve.wait_ge(xt_sb.sem, NT * KC // 4)
            dve.wait_ge(loaded.sem, 16 * 2 * E)

            def fetch(i, k):
                tile = dve.value_load(table[0:1, 0, bass.ds(i * PER + k, 1)], min_val=0, max_val=NT - 1)
                e = dve.value_load(table[0:1, 1, bass.ds(i * PER + k, 1)], min_val=0, max_val=E - 1)
                if not (isinstance(i, int) and k < 2):
                    dve.wait_ge(up_done.sem, up_done.at(i, 2 * k - 2))
                V.tensor_scalar(xj[:, k % 2, :, :].rearrange("p k c -> p (k c)"), xt[:, bass.ds(tile, 1), :, :].rearrange("p t k c -> p (t k c)"), 1.0, None, ALU.mult)
                if not (isinstance(i, int) and k < 2):
                    dve.wait_ge(relu_done.sem, relu_done.at(i, 2 * k - 4))
                V.tensor_scalar(b1j[:, k % 3, :], b1[:, bass.ds(e * FT, FT)], 1.0, None, ALU.mult).then_inc(job_in.sem, 1)

            def take(i, k):
                if not (isinstance(i, int) and k == 0):
                    dve.wait_ge(hid_turned.sem, hid_turned.at(i, 2 * k))
                for half in range(2):
                    n = 2 * k + half
                    dve.wait_ge(up_done.sem, up_done.at(i, n + 1))
                    V.tensor_copy(hid[:, half * 512:(half + 1) * 512], up[n % 4][:, :]).then_inc(hid_sb.sem, 1)

            def gather(i, k):
                tile = dve.value_load(table[0:1, 0, bass.ds(i * PER + k, 1)], min_val=0, max_val=NT - 1)
                column = dve.value_load(table[0:1, 2, bass.ds(i * PER + k, 1)], min_val=0, max_val=NV)
                dve.wait_ge(down_done.sem, down_done.at(i, k + 1))
                dve.wait_ge(added.sem, added.at(i, k))
                V.scalar_tensor_tensor(acc[:, bass.ds(tile, 1), :].rearrange("p t o -> p (t o)"), down[k % 2][:, 0:D],
                                       share_v[:, bass.ds(tile, 1), bass.ds(column, 1)].rearrange("p t o -> p (t o)"),
                                       acc[:, bass.ds(tile, 1), :].rearrange("p t o -> p (t o)"), ALU.mult, ALU.add).then_inc(added.sem, 1)

            fetch(0, 0)
            fetch(0, 1)
            take(0, 0)
            with dve.Fori(0, JOBS // PER) as i:
                for k in range(PER):
                    fetch(i, k + 2)
                    take(i, k + 1)
                    gather(i, k)
            dve.wait_ge(added.sem, added.at(JOBS // PER, 0))
            layer_norms(dve, nc, vlink, 0, [acc[:, t, :] for t in range(NT)], stats, [acc[:, t, :] for t in range(NT)], [normed] * NT)


def _constants():
    import numpy as np

    inv = (1.0 / 10000.0 ** (np.arange(0, DH, 2, dtype=np.float32) / DH)).astype(np.float32)
    ang = np.arange(T, dtype=np.float32)[:, None] * inv[None, :]
    s = np.sin(ang)
    c = {
        "cos": np.concatenate([np.cos(ang)] * 2, axis=1), "sin": np.concatenate([-s, s], axis=1),
        "ident": np.eye(128), "earlier": np.triu(np.ones((T, T)), 1), "ones": np.ones((T, T)),
        "count_to": np.tile(np.arange(1, TOP + 1), (128, 1)), "eights": np.tile(np.arange(8, 2 * TOP + 1, 8), (128, 1)),
        "expert_no": np.tile(np.arange(E), (128, 1)), "expert_before": np.tile((np.arange(E) - 1) % E, (128, 1)),
        "rev": np.tile(np.arange(E, 0, -1), (T, 1)), "slot_no": np.tile(np.arange(CAP), (T, 1)),
        "causal": np.triu(np.full((T, T), NEG), 1), "row_of": np.arange(XD)[:, None, None] - RANK == np.arange(2 * NST)[None, :, None] + np.zeros((1, 1, 128)),
        "maskrow": (np.arange(128) % PAD == DH)[None, :],
    }
    wide = lambda v: np.tile(v, (128, 1))
    v_no = np.append(np.arange(NV), -5)
    tile, v = np.divmod(np.arange(128), NV)
    v = np.where(tile < NT, v, -5)
    c.update(
        token_no=np.arange(B * T).reshape(NT, 128).T, before128=np.triu(np.ones((128, 128)), 1), ones128=np.ones((128, 128)),
        v_no=wide(v_no), v_before=wide(np.append(np.arange(NV) - 1, -5)), tile_start=wide(128 * np.arange(NT)),
        pair_before=np.arange(NT)[None, :] < tile[:, None], pair_is=np.arange(NT)[None, :] == tile[:, None],
        pair_base=(2 * tile + v)[:, None], pair_v=v[:, None], pair_vals=np.stack([tile, v % E, v - NV], axis=1), job_no=wide(np.arange(JOBS + 2)),
    )
    return {k: np.ascontiguousarray(v, dtype=np.float32) for k, v in c.items()}


def _layouts(a):
    import numpy as np

    def chunks(w):
        return w.reshape(-1, 128, w.shape[1]).transpose(1, 0, 2)

    def pad_heads(w):
        out = np.zeros(w.shape[:-1] + (HEADS, PAD), w.dtype)
        out[..., :DH] = w.reshape(w.shape[:-1] + (HEADS, DH))
        return out

    def pad_rows(w):
        out = np.zeros((HEADS, PAD, w.shape[1]), w.dtype)
        out[:, :DH] = w.reshape(HEADS, DH, -1)
        return out.reshape(HG, 128, -1).transpose(1, 0, 2)

    def columns(v):
        return v.reshape(-1, 128).T

    rows = lambda v: v.reshape(DT, 128, -1).transpose(1, 0, 2)
    bq = pad_heads(a["L0_xattn_bq"])
    bq[:, DH] = 1.0
    out = dict(a)
    out.update(
        xt=a["x"].reshape(B, T, KC, 128).transpose(0, 3, 2, 1), ctxt=a["ctx_1024"].reshape(B, S2, KC, 128).transpose(0, 3, 2, 1),
        mask=np.ascontiguousarray(a["mask_BxS2_bk0"]).reshape(-1).view(np.int32),
        wqkv=chunks(a["L0_attn_qkv_w"].T), wproj=pad_rows(a["L0_attn_proj_w"].T),
        wqx=chunks(pad_heads(a["L0_xattn_Wq"].T).reshape(D, -1)), bqx=columns(bq.reshape(-1)),
        wkx=chunks(pad_heads(a["L0_xattn_Wk"].T).reshape(D, -1)), bkx=columns(pad_heads(a["L0_xattn_bk"]).reshape(-1)),
        wvx=chunks(a["L0_xattn_Wv"].T), wox=pad_rows(a["L0_xattn_Wo"].T), router=chunks(a["L0_ffn_router_w"]),
        w0=a["L0_ffn_w0_kernel"].reshape(E, KC, 128, HID).transpose(0, 2, 1, 3), w1=a["L0_ffn_w1_kernel"].reshape(E, KC, 128, HID).transpose(0, 2, 1, 3),
        wo=a["L0_ffn_wo_kernel"].reshape(E, HT, HP, D).transpose(0, 2, 1, 3),
        win=chunks(a["L1_attn_W_in"].T), convw=rows(a["L1_attn_conv_w"].reshape(DIN, TAPS)), convb=columns(a["L1_attn_conv_b"]),
        wx=chunks(a["L1_attn_W_x"].T), wdt=a["L1_attn_W_dt"].T, bdt=columns(a["L1_attn_b_dt"]), alog=rows(a["L1_attn_A_log"]),
        ctx_rows=a["ctx_1024"].reshape(B, KT, KP, D).transpose(0, 2, 1, 3), wk=chunks(a["L1_xattn_Wk"].T), wv=chunks(a["L1_xattn_Wv"].T),
        wq=chunks(a["L1_xattn_Wq"].T), wih=chunks(a["L1_xattn_gru_wih"].T), whh=chunks(a["L1_xattn_gru_whh"].T),
        snorm=columns(a["L1_xattn_slot_norm_w"]), inorm=columns(a["L1_xattn_input_norm_w"]),
        W1=a["L1_ffn_W1"].reshape(E, KC, 128, DFF).transpose(0, 2, 1, 3), W2=a["L1_ffn_W2"].reshape(E, FT, 128, D).transpose(0, 2, 1, 3),
        b1=a["L1_ffn_b1"].reshape(E, FT, 128).transpose(0, 2, 1),
        dp=columns(a["L1_attn_Dp"]), wout=chunks(a["L1_attn_W_out"].T),
    )
    out.update(_constants())
    return out


def _views(d):
    if "mask" in d:
        d["mask"] = d["mask"].bitcast(U8).rearrange("(b o s) -> b o s", o=1, s=S2)
    if "s_xe" in d:
        d["s_xe_by_expert"] = d["s_xe"].rearrange("g p k (e c) -> e k p g c", e=E)
    if "s_eo" in d:
        d["s_eo_by_expert"] = d["s_eo"].rearrange("(s g) (e c) d -> e g c s d", g=2, e=E)
        d["s_eo_by_group"] = d["s_eo"].rearrange("g (s p) d -> g p s d", p=T)
    if "s_x4" in d:
        d["s_x4_by_four"] = d["s_x4"].rearrange("(i b) t d -> i t b d", b=QB)
    if "s_x5" in d:
        d["s_x5_by_four"] = d["s_x5"].rearrange("(i b) t d -> i t b d", b=QB)
        d["s_x5_by_tile"] = d["s_x5"].rearrange("b t d -> (b t) d").rearrange("(n p) d -> p n d", p=128)
    if "s_sorted" in d:
        d["s_sorted_by_tile"] = d["s_sorted"].rearrange("(n p) d -> p n d", p=128)
    if "out" in d:
        d["out_rows"] = d["out"].rearrange("b t d -> (b t) d")


_A = ["xt", "x", "ctxt", "mask", "wqkv", "L0_attn_qkv_b", "wproj", "L0_attn_proj_b", "wqx", "bqx", "wkx", "bkx", "wvx", "L0_xattn_bv",
      "wox", "L0_xattn_bo", "cos", "sin", "ident", "causal", "maskrow"]
_B = ["w0", "w1", "wo"]
_C = ["win", "convw", "convb", "wx", "wdt", "bdt", "alog", "dp", "wout", "row_of"]
_INS = list(dict.fromkeys(_A + _B + _C + ROUTE_INPUTS + SLOT_INPUTS + HASH_INPUTS))
_SCRATCH = {"s_x2": (G, T, GB, D), "s_xe": (G, 128, KC, SL), "s_ct": (G, T, GB, ST, T), "s_eo": (G, SL, D), "s_x4": (B, T, D), "s_x5": (B, T, D), "s_sorted": (B * T, XW)}


def kernel(**inputs):
    import numpy as np
    import concourse.bacc as bacc
    from concourse.bass_utils import run_bass_kernel_spmd

    nc = bacc.Bacc("TRN2", target_bir_lowering=False, num_devices=1)
    laid = _layouts({k: np.asarray(v) for k, v in inputs.items()})
    arrays = {f"in_{n}": np.ascontiguousarray(laid[n]) for n in _INS}
    d = {n: nc.dram_tensor(f"in_{n}", arrays[f"in_{n}"].shape, mybir.dt.from_np(arrays[f"in_{n}"].dtype), kind="ExternalInput").ap() for n in _INS}
    for n, shape in _SCRATCH.items():
        d[n] = nc.dram_tensor(n, shape, F32, kind="Internal").ap()
    d["out"] = nc.dram_tensor("out", (B, T, D), F32, kind="ExternalOutput").ap()
    _views(d)
    for phase in (attention_phase, routing_phase, expert_phase, mixer_phase, slot_phase, hashed_phase):
        run_phase(nc, phase, d)
    return run_bass_kernel_spmd(nc, [arrays], core_ids=[0]).results[0]["out"]
```
